# Optimizing a Trainium2 kernel written in Bass

```python
import numpy as np
import jax
import jax.numpy as jnp

def _softmax(x, axis=-1):
    return jax.nn.softmax(x, axis=axis)

def _gelu(x):
    return jax.nn.gelu(x, approximate=True)

def _silu(x):
    return jax.nn.silu(x)

def _sigmoid(x):
    return jax.nn.sigmoid(x)

def _layernorm(x, axis=-1, eps=1e-05):
    m = jnp.mean(x, axis=axis, keepdims=True)
    v = jnp.var(x, axis=axis, keepdims=True)
    return (x - m) / jnp.sqrt(v + eps)

def _scatter_add(tgt, idx, src, axis=0):
    return tgt.at[idx].add(src)

def _segment_sum(src, seg, n):
    return jax.ops.segment_sum(src, seg, n)
kernel_name = 'mk_gnn_preln_d4_gnn_r16_358d30'

def setup_inputs(seed: int=0):
    np.random.seed(seed)
    _w = jnp.asarray

    def _rec_inputs():
        import jax
        import jax.numpy as jnp
        _gk = jax.random.key(seed)
        x = -0.0005121 + 1.001 * jax.random.normal(jax.random.fold_in(_gk, 1), (3125, 64), jnp.float32)
        src = jax.random.randint(jax.random.fold_in(_gk, 2), (100000,), 0, 3125, jnp.int32)
        dst = jax.random.randint(jax.random.fold_in(_gk, 3), (100000,), 0, 3125, jnp.int32)
        _o = jnp.argsort(dst, stable=True)
        src = src[_o]
        dst = dst[_o]
        edge_attr_64 = -8.16379e-05 + 0.999858 * jax.random.normal(jax.random.fold_in(_gk, 12), (100000, 64), jnp.float32)
        return (x, src, dst, edge_attr_64)
    x, src, dst, edge_attr_64 = _rec_inputs()

    def _L0_gnn_setup():
        import jax, jax.numpy as jnp
        import numpy as np
        N_NODES = 3125
        N_EDGES = 37500
        D = 64
        H = 4
        L = 4
        NEG_SLOPE = 0.2

        def _gat_layer(h, src_e, dst_e, W, al, ar, b):
            fs = (h @ W).reshape(N_NODES, H, D)
            el = jnp.einsum('nhd,hd->nh', fs, al)
            er = jnp.einsum('nhd,hd->nh', fs, ar)
            e = jax.nn.leaky_relu(el[src_e] + er[dst_e], NEG_SLOPE)
            m = jax.ops.segment_max(e, dst_e, num_segments=N_NODES)
            m = jax.lax.stop_gradient(m)
            ex = jnp.exp(e - m[dst_e])
            denom = jax.ops.segment_sum(ex, dst_e, num_segments=N_NODES)
            alpha = ex / denom[dst_e]
            msg = alpha[:, :, None] * fs[src_e]
            rst = jax.ops.segment_sum(msg, dst_e, num_segments=N_NODES)
            rst = rst + b.reshape(1, H, D)
            return rst.sum(axis=1)
        key = jax.random.key(seed)
        ks = jax.random.split(key, 9)
        feat = jax.random.normal(ks[0], (N_NODES, D), dtype=jnp.float32)
        src = jax.random.randint(ks[1], (N_EDGES,), 0, N_NODES, dtype=jnp.int32)
        dst = jax.random.randint(ks[2], (N_EDGES,), 0, N_NODES, dtype=jnp.int32)
        Ws = jax.random.normal(ks[3], (L, D, H * D), dtype=jnp.float32) / np.sqrt(D)
        attn_l = jax.random.normal(ks[4], (L, H, D), dtype=jnp.float32) / np.sqrt(D)
        attn_r = jax.random.normal(ks[5], (L, H, D), dtype=jnp.float32) / np.sqrt(D)
        gat_bias = jax.random.normal(ks[6], (L, H * D), dtype=jnp.float32) * 0.02
        h_bias = jax.random.normal(ks[7], (D,), dtype=jnp.float32) * 0.02
        return {'feat': feat, 'src': src, 'dst': dst, 'Ws': Ws, 'attn_l': attn_l, 'attn_r': attn_r, 'gat_bias': gat_bias, 'h_bias': h_bias}
    _L0_gnn_all = _L0_gnn_setup()
    _L0_gnn_in = {k: v for k, v in _L0_gnn_all.items() if k in ('Ws', 'attn_l', 'attn_r', 'gat_bias', 'h_bias')}
    del _L0_gnn_all

    def _L1_gnn_setup():
        import jax, jax.numpy as jnp
        import numpy as np
        N, D = (6250, 64)
        E, DE = (100000, 64)
        MSG_H, MSG_OUT = (128, 64)
        NODE_H = 128
        LN_EPS = 1e-05
        key = jax.random.key(seed)
        ks = jax.random.split(key, 10)

        def glorot(k, shape):
            fan_in = shape[0]
            return jax.random.normal(k, shape, jnp.float32) / jnp.sqrt(jnp.float32(fan_in))
        return {'nodes': jax.random.normal(ks[0], (N, D), jnp.float32), 'edges': jax.random.normal(ks[1], (E, DE), jnp.float32), 'senders': jax.random.randint(ks[2], (E,), 0, N, jnp.int32), 'receivers': jax.random.randint(ks[3], (E,), 0, N, jnp.int32), 'msg_W1': glorot(ks[4], (2 * D + DE, MSG_H)), 'msg_b1': jnp.zeros((MSG_H,), jnp.float32), 'msg_W2': glorot(ks[5], (MSG_H, MSG_OUT)), 'msg_b2': jnp.zeros((MSG_OUT,), jnp.float32), 'node_W1': glorot(ks[6], (D + MSG_OUT, NODE_H)), 'node_b1': jnp.zeros((NODE_H,), jnp.float32), 'node_W2': glorot(ks[7], (NODE_H, D)), 'node_b2': jnp.zeros((D,), jnp.float32), 'ln_scale': jnp.ones((D,), jnp.float32), 'ln_offset': jnp.zeros((D,), jnp.float32)}
    _L1_gnn_all = _L1_gnn_setup()
    _L1_gnn_in = {k: v for k, v in _L1_gnn_all.items() if k in ('msg_W1', 'msg_b1', 'msg_W2', 'msg_b2', 'node_W1', 'node_b1', 'node_W2', 'node_b2', 'ln_scale', 'ln_offset')}
    del _L1_gnn_all

    def _L2_gnn_setup():
        import jax, jax.numpy as jnp
        import numpy as np
        N_NODES = 6250
        N_EDGES = 75000
        H = 64
        L = 3
        BN_EPS = 1e-05
        key = jax.random.key(seed)
        ks = jax.random.split(key, 6)
        scale = 1.0 / np.sqrt(H)
        x = jax.random.normal(ks[0], (N_NODES, H), jnp.float32)
        edge_index = jax.random.randint(ks[1], (2, N_EDGES), 0, N_NODES)
        Wl = jax.random.normal(ks[2], (L, H, H), jnp.float32) * scale
        Wr = jax.random.normal(ks[3], (L, H, H), jnp.float32) * scale
        b = jnp.zeros((L, H), jnp.float32)
        gamma = jnp.ones((L, H), jnp.float32)
        beta = jnp.zeros((L, H), jnp.float32)
        Wp = jax.random.normal(ks[4], (H, L * H), jnp.float32) * (1.0 / np.sqrt(L * H))
        bp = jnp.zeros((H,), jnp.float32)
        return {'x': x, 'edge_index': edge_index, 'Wl': Wl, 'Wr': Wr, 'b': b, 'gamma': gamma, 'beta': beta, 'Wp': Wp, 'bp': bp}
    _L2_gnn_all = _L2_gnn_setup()
    _L2_gnn_in = {k: v for k, v in _L2_gnn_all.items() if k in ('Wl', 'Wr', 'b', 'gamma', 'beta', 'Wp', 'bp')}
    del _L2_gnn_all

    def _L3_gnn_setup():
        import jax, jax.numpy as jnp
        import numpy as np
        N_NODES = 6250
        N_EDGES = 100000
        D_IN = 64
        D_OUT = 64
        key = jax.random.key(seed)
        k1, k2, k3, k4 = jax.random.split(key, 4)
        x = jax.random.normal(k1, (N_NODES, D_IN), dtype=jnp.float32)
        W = jax.random.normal(k2, (D_OUT, D_IN), dtype=jnp.float32) * 0.1
        b = jax.random.normal(k3, (D_OUT,), dtype=jnp.float32) * 0.1
        edge_index = jax.random.randint(k4, (2, N_EDGES), 0, N_NODES, dtype=jnp.int64 if jax.config.jax_enable_x64 else jnp.int32)
        return {'x': x, 'W': W, 'b': b, 'edge_index': edge_index}
    _L3_gnn_all = _L3_gnn_setup()
    _L3_gnn_in = {k: v for k, v in _L3_gnn_all.items() if k in ('W', 'b')}
    del _L3_gnn_all
    return {'x': x, 'src': src, 'dst': dst, 'edge_attr_64': edge_attr_64, 'L0_gnn_Ws': _L0_gnn_in['Ws'], 'L0_gnn_attn_l': _L0_gnn_in['attn_l'], 'L0_gnn_attn_r': _L0_gnn_in['attn_r'], 'L0_gnn_gat_bias': _L0_gnn_in['gat_bias'], 'L0_gnn_h_bias': _L0_gnn_in['h_bias'], 'L1_gnn_msg_W1': _L1_gnn_in['msg_W1'], 'L1_gnn_msg_b1': _L1_gnn_in['msg_b1'], 'L1_gnn_msg_W2': _L1_gnn_in['msg_W2'], 'L1_gnn_msg_b2': _L1_gnn_in['msg_b2'], 'L1_gnn_node_W1': _L1_gnn_in['node_W1'], 'L1_gnn_node_b1': _L1_gnn_in['node_b1'], 'L1_gnn_node_W2': _L1_gnn_in['node_W2'], 'L1_gnn_node_b2': _L1_gnn_in['node_b2'], 'L1_gnn_ln_scale': _L1_gnn_in['ln_scale'], 'L1_gnn_ln_offset': _L1_gnn_in['ln_offset'], 'L2_gnn_Wl': _L2_gnn_in['Wl'], 'L2_gnn_Wr': _L2_gnn_in['Wr'], 'L2_gnn_b': _L2_gnn_in['b'], 'L2_gnn_gamma': _L2_gnn_in['gamma'], 'L2_gnn_beta': _L2_gnn_in['beta'], 'L2_gnn_Wp': _L2_gnn_in['Wp'], 'L2_gnn_bp': _L2_gnn_in['bp'], 'L3_gnn_W': _L3_gnn_in['W'], 'L3_gnn_b': _L3_gnn_in['b']}

def reference(x, src, dst, edge_attr_64, L0_gnn_Ws, L0_gnn_attn_l, L0_gnn_attn_r, L0_gnn_gat_bias, L0_gnn_h_bias, L1_gnn_msg_W1, L1_gnn_msg_b1, L1_gnn_msg_W2, L1_gnn_msg_b2, L1_gnn_node_W1, L1_gnn_node_b1, L1_gnn_node_W2, L1_gnn_node_b2, L1_gnn_ln_scale, L1_gnn_ln_offset, L2_gnn_Wl, L2_gnn_Wr, L2_gnn_b, L2_gnn_gamma, L2_gnn_beta, L2_gnn_Wp, L2_gnn_bp, L3_gnn_W, L3_gnn_b):
    import jax
    import jax.numpy as jnp

    def _L0_gnn_ref(feat, src, dst, Ws, attn_l, attn_r, gat_bias, h_bias):
        import jax, jax.numpy as jnp
        import numpy as np
        N_NODES = 3125
        N_EDGES = 37500
        D = 64
        H = 4
        L = 4
        NEG_SLOPE = 0.2

        def _gat_layer(h, src_e, dst_e, W, al, ar, b):
            fs = (h @ W).reshape(N_NODES, H, D)
            el = jnp.einsum('nhd,hd->nh', fs, al)
            er = jnp.einsum('nhd,hd->nh', fs, ar)
            e = jax.nn.leaky_relu(el[src_e] + er[dst_e], NEG_SLOPE)
            m = jax.ops.segment_max(e, dst_e, num_segments=N_NODES)
            m = jax.lax.stop_gradient(m)
            ex = jnp.exp(e - m[dst_e])
            denom = jax.ops.segment_sum(ex, dst_e, num_segments=N_NODES)
            alpha = ex / denom[dst_e]
            msg = alpha[:, :, None] * fs[src_e]
            rst = jax.ops.segment_sum(msg, dst_e, num_segments=N_NODES)
            rst = rst + b.reshape(1, H, D)
            return rst.sum(axis=1)
        loops = jnp.arange(N_NODES, dtype=src.dtype)
        src_e = jnp.concatenate([src, loops])
        dst_e = jnp.concatenate([dst, loops])
        h = feat
        for i in range(L):
            h = _gat_layer(h, src_e, dst_e, Ws[i], attn_l[i], attn_r[i], gat_bias[i])
        return h + h_bias

    def _L1_gnn_ref(nodes, edges, senders, receivers, msg_W1, msg_b1, msg_W2, msg_b2, node_W1, node_b1, node_W2, node_b2, ln_scale, ln_offset):
        import jax, jax.numpy as jnp
        import numpy as np
        N, D = (6250, 64)
        E, DE = (100000, 64)
        MSG_H, MSG_OUT = (128, 64)
        NODE_H = 128
        LN_EPS = 1e-05
        x = jnp.concatenate([nodes[senders], nodes[receivers], edges], axis=-1)
        h = jax.nn.relu(x @ msg_W1 + msg_b1)
        messages = jax.nn.relu(h @ msg_W2 + msg_b2)
        agg = jax.ops.segment_sum(messages, receivers, num_segments=nodes.shape[0])
        y = jnp.concatenate([nodes, agg], axis=-1)
        y = jax.nn.relu(y @ node_W1 + node_b1)
        y = y @ node_W2 + node_b2
        mean = jnp.mean(y, axis=-1, keepdims=True)
        var = jnp.var(y, axis=-1, keepdims=True)
        y = (y - mean) * jax.lax.rsqrt(var + LN_EPS) * ln_scale + ln_offset
        return nodes + y

    def _L2_gnn_ref(x, edge_index, Wl, Wr, b, gamma, beta, Wp, bp):
        import jax, jax.numpy as jnp
        import numpy as np
        N_NODES = 6250
        N_EDGES = 75000
        H = 64
        L = 3
        BN_EPS = 1e-05
        src, dst = (edge_index[0], edge_index[1])
        n = x.shape[0]
        deg = jax.ops.segment_sum(jnp.ones((src.shape[0],), x.dtype), dst, num_segments=n)
        inv_deg = (1.0 / jnp.maximum(deg, 1.0))[:, None]
        h = x
        layer_outputs = []
        for i in range(L):
            agg = jax.ops.segment_sum(h[src], dst, num_segments=n) * inv_deg
            h = agg @ Wl[i].T + b[i] + h @ Wr[i].T
            mu = h.mean(axis=0)
            var = h.var(axis=0)
            h = gamma[i] * (h - mu) * jax.lax.rsqrt(var + BN_EPS) + beta[i]
            h = jax.nn.relu(h)
            layer_outputs.append(h)
        h_cat = jnp.concatenate(layer_outputs, axis=-1)
        return h_cat @ Wp.T + bp

    def _L3_gnn_ref(x, W, b, edge_index):
        import jax, jax.numpy as jnp
        import numpy as np
        N_NODES = 6250
        N_EDGES = 100000
        D_IN = 64
        D_OUT = 64
        N = x.shape[0]
        loop = jnp.arange(N, dtype=edge_index.dtype)
        src = jnp.concatenate([edge_index[0], loop])
        dst = jnp.concatenate([edge_index[1], loop])
        E = src.shape[0]
        h = x @ W.T + b
        ones = jnp.ones((E,), dtype=h.dtype)
        deg = jax.ops.segment_sum(ones, src, num_segments=N)
        deg_inv_sqrt = jnp.where(deg > 0, jax.lax.rsqrt(jnp.maximum(deg, 1.0)), 0.0)
        norm = deg_inv_sqrt[src] * deg_inv_sqrt[dst]
        msg = norm[:, None] * h[src]
        agg_sum = jax.ops.segment_sum(msg, dst, num_segments=N)
        cnt = jax.ops.segment_sum(ones, dst, num_segments=N)
        out = agg_sum / jnp.maximum(cnt, 1.0)[:, None]
        return out
    edge_index = jnp.stack([src, dst])
    h = jnp.maximum(_layernorm(x, axis=-1), 0.0)
    x = x + _L0_gnn_ref(h, src, dst, L0_gnn_Ws, L0_gnn_attn_l, L0_gnn_attn_r, L0_gnn_gat_bias, L0_gnn_h_bias)
    h = jnp.maximum(_layernorm(x, axis=-1), 0.0)
    x = x + _L1_gnn_ref(h, edge_attr_64, src, dst, L1_gnn_msg_W1, L1_gnn_msg_b1, L1_gnn_msg_W2, L1_gnn_msg_b2, L1_gnn_node_W1, L1_gnn_node_b1, L1_gnn_node_W2, L1_gnn_node_b2, L1_gnn_ln_scale, L1_gnn_ln_offset)
    h = jnp.maximum(_layernorm(x, axis=-1), 0.0)
    x = x + _L2_gnn_ref(h, edge_index, L2_gnn_Wl, L2_gnn_Wr, L2_gnn_b, L2_gnn_gamma, L2_gnn_beta, L2_gnn_Wp, L2_gnn_bp)
    h = jnp.maximum(_layernorm(x, axis=-1), 0.0)
    x = x + _L3_gnn_ref(h, L3_gnn_W, L3_gnn_b, edge_index)
    return x

_drawn_inputs = setup_inputs


def setup_inputs(seed=0):
    import zlib

    import numpy as np

    out = dict(_drawn_inputs(seed))
    spreads = {'L1_gnn_msg_b1': (0.0, 0.275),
     'L1_gnn_msg_b2': (0.0, 0.1),
     'L1_gnn_node_b1': (0.0, 2.0),
     'L1_gnn_node_b2': (0.0, 0.8),
     'L1_gnn_ln_scale': (1.0, 0.2),
     'L1_gnn_ln_offset': (0.0, 0.46),
     'L2_gnn_b': (0.0, 2.0),
     'L2_gnn_gamma': (1.0, 0.534),
     'L2_gnn_beta': (0.0, 0.504),
     'L2_gnn_bp': (0.0, 0.449)}
    factors = {'L0_gnn_attn_r': 49.952, 'L0_gnn_h_bias': 8.0, 'L3_gnn_W': 8.0, 'L3_gnn_b': 64.0}
    for name, (base, spread) in spreads.items():
        noise = np.random.default_rng([zlib.crc32(name.encode()), seed]).standard_normal(out[name].shape)
        drawn = base * np.exp(spread * noise) if base else spread * noise
        out[name] = jnp.asarray(drawn.astype(out[name].dtype))
    for name, factor in factors.items():
        out[name] = (out[name] * factor).astype(out[name].dtype)
    return out
```

```python
from contextlib import ExitStack

import numpy as np

import concourse.bass as bass
from concourse import mybir
from concourse.alu_op_type import AluOpType as ALU

f32 = mybir.dt.float32
bf16 = mybir.dt.bfloat16
i32 = mybir.dt.int32
ACT = mybir.ActivationFunctionType
AX = mybir.AxisListType

N, E, D = 3125, 100000, 64
P = 125
T = N // P
GT = 5
NG = T // GT
ROWLEN = P
NROW = E // ROWLEN
HALF = NROW // 2
BLK = 4
NBLK = E // BLK
CH = 8
BPC = CH // BLK
HEADS = 4
L0, L2 = 4, 3
HID = 128
KEYCAP = 4095
KEYMUL = 4096
FAR = -1.0e30
MAXG = E // CH + (E // P) // CH + 3 * T + 2
AW = HEADS * (D + 1)


def build(nc, x_in, src_in, dst_in, attr_in, W0, al0, ar0, gb0, hb0, mW1, mb1, mW2, mb2, nW1, nb1,
          nW2, nb2, lnS, lnO, Wl2, Wr2, b2_, gam2, bet2, Wp2, bp2, W3, b3, out):
    ctx = ExitStack()
    with ctx:
        def sb(name, shape, dt=f32):
            return ctx.enter_context(nc.sbuf_tensor(name, shape, dt))

        def pb(name, shape):
            return ctx.enter_context(nc.psum_tensor(name, shape, f32))

        def sem(name):
            return ctx.enter_context(nc.semaphore(name))

        def dram(name, shape, dt=f32):
            return nc.dram_tensor(name, shape, dt, kind="Internal").ap()

        starts_d = dram("starts_d", [N + 1], i32)
        keys_d = dram("keys_d", [N])
        meta_d = dram("meta_d", [N, 4], i32)
        rec_d = dram("rec_d", [MAXG, P, CH + BPC], i32)
        tab0_d = dram("tab0_d", [N + 1, D + 1 + HEADS])
        tab1_d = dram("tab1_d", [N + 1, HID + 1])
        tab2_d = dram("tab2_d", [N + 1, D])
        hist_d = dram("hist_d", [64 * 64, 1])

        ident = sb("ident", [128, 128])
        ones = sb("ones", [1, 128])
        tail_end = sb("tail_end", [1, 1], i32)
        nodeid = sb("nodeid", [P, T])
        nodeid_i = sb("nodeid_i", [P, T], i32)
        iota8 = sb("iota8", [P, CH])
        iota8_i = sb("iota8_i", [P, CH], i32)
        iota64 = sb("iota64", [P, 64], bf16)
        iota64_i = sb("iota64_i", [P, 64], i32)
        step3 = sb("step3", [P, 3])
        padrow = sb("padrow", [1, HID + 1 + HEADS])

        firsts_i = sb("firsts_i", [1, NROW], i32)
        firsts = sb("firsts", [1, NROW])
        firsts_b = sb("firsts_b", [P, NROW])
        wide = sb("wide", [P, T * HID])
        kcount = sb("kcount", [P, T])
        krow = sb("krow", [P, T])
        krow_i = sb("krow_i", [P, T], i32)
        start_i = sb("start_i", [P, T], i32)
        end_i = sb("end_i", [P, T], i32)
        pf = [sb(f"pf{i}", [P, T]) for i in range(6)]
        pi = [sb(f"pi{i}", [P, T], i32) for i in range(4)]
        keys_b = sb("keys_b", [P, N])
        drows = keys_b[:, :].bitcast(i32).rearrange("p (t m) -> p t m", m=ROWLEN)
        rank_i = sb("rank_i", [P, T], i32)
        meta_o = sb("meta_o", [P, T, 4], i32)
        meta = sb("meta", [P, T, 4], i32)
        perm = sb("perm", [P, T], i32)
        nch_f = sb("nch_f", [P, T])
        tmax = sb("tmax", [P, T])
        cs_a = sb("cs_a", [1, T + 1])
        cs_b = sb("cs_b", [1, T + 1])
        cs_i = sb("cs_i", [1, T + 1], i32)
        edge_cur = sb("edge_cur", [P, T, 3])
        cur = sb("cur", [P, 3])
        blk_ix = sb("blk_ix", [P, 2, BPC], i32)
        raw_src = sb("raw_src", [P, 2, CH], i32)
        vmask = sb("vmask", [P, 2, CH])
        recs = sb("recs", [P, 2, CH + BPC], i32)
        deg = sb("deg", [P, T])

        x = sb("x", [P, T, D])
        h = sb("h", [P, T, D])
        xc = sb("xc", [P, T, D])
        sq = sb("sq", [P, T, D])
        stat = sb("stat", [P, T])
        std = sb("std", [P, T])
        rstd = sb("rstd", [P, T])
        tab = sb("tab", [P, T, HID + 1])
        er = sb("er", [P, T, HEADS])
        tr5 = sb("tr5", [128, GT, P])

        idx = sb("idx", [P, 2, CH + BPC], i32)
        rows = sb("rows", [P, 2, CH, HID + 1])
        zz = sb("zz", [P, CH + 1, HEADS])
        pz = sb("pz", [P, CH + 1, HEADS])
        pe = sb("pe", [P, CH + 1, HEADS])
        mnew = sb("mnew", [P, HEADS])
        acc = sb("acc", [P, HEADS, D + 1])
        prod = sb("prod", [P, CH, HEADS, D + 1])
        part = sb("part", [P, HEADS, D + 1])
        rden = sb("rden", [P, HEADS])
        u = sb("u", [P, HEADS, D])
        uT = sb("uT", [128, 2, P])
        hs = sb("hs", [P, D])
        hT = sb("hT", [D, P])

        cat = sb("cat", [P, T, 2 * D])
        Bn = wide[:, :].rearrange("p (t c) -> p t c", t=T)
        attr = sb("attr", [P, 2, CH, D])
        at_s = sb("at_s", [P, CH, D])
        atT = sb("atT", [128, CH // 2, P])
        pre_s = sb("pre_s", [P, CH, HID])
        real = sb("real", [P, CH])
        hidT = sb("hidT", [128, 2, CH // 2, P])
        msgs = sb("msgs", [P, 2, CH // 2, D])
        msum = sb("msum", [P, D])
        macc = sb("macc", [P, D])
        zT5 = sb("zT5", [128, GT, P])
        y = sb("y", [P, T, D])
        srcs_i = sb("srcs_i", [P, NROW], i32)
        hilo_i = sb("hilo_i", [P, 2, NROW], i32)
        hilo = sb("hilo", [P, 2, NROW], bf16)
        OHC = NROW // T
        oh = sb("oh", [P, 2, OHC, 64], bf16)
        hist = sb("hist", [64, 64])

        hTall = sb("hTall", [D, T, P])
        yT = keys_b[0:D, :].rearrange("p (t n) -> p t n", n=P)
        bnst = sb("bnst", [D, 8])
        wst = sb("wst", [D, 2, D])
        iw = sb("iw", [D, 2 * D])
        agg = sb("agg", [P, T, D])
        odeg = sb("odeg", [P, T])
        dinv = sb("dinv", [P, T])
        invd = sb("invd", [P, T])

        W1ab = sb("W1ab", [D, 2, HID])
        W1c = sb("W1c", [128, HID])
        W2s = sb("W2s", [HID, D])
        b1b = sb("b1b", [P, HID])
        b2b = sb("b2b", [P, D])
        nW1s = sb("nW1s", [128, HID])
        nW2s = sb("nW2s", [HID, D])
        nb1c = sb("nb1c", [HID, 1])
        nb2b = sb("nb2b", [P, D])
        lnSb = sb("lnSb", [P, D])
        lnOb = sb("lnOb", [P, D])
        wnat = sb("wnat", [D, 10, D])
        wT = sb("wT", [D, 10, D])
        bnc = sb("bnc", [D, 3, L2])
        bpb = sb("bpb", [P, D])
        b3b = sb("b3b", [P, D])
        W0s = sb("W0s", [128, L0, 2, D])
        early = cat[0:D, :, :].rearrange("p t c -> p (t c)")
        alr = early[:, 0:2 * L0 * HEADS * D].rearrange("p (k l h d) -> p k l h d", k=2, l=L0, h=HEADS)
        W0k = early[:, 2 * L0 * HEADS * D:3 * L0 * HEADS * D].rearrange("p (l h d) -> p l h d", l=L0, h=HEADS)
        WL = sb("WL", [D, L0 + 1, 2 * HEADS])
        gbb = agg[:, :, :].rearrange("p t d -> p (t d)")[:, 0:L0 * HEADS * D]\
            .rearrange("p (l h d) -> p l h d", l=L0, h=HEADS)
        gbs = sb("gbs", [P, L0, D])
        hbb = sb("hbb", [P, D])

        psA = pb("psA", [128, 1024])
        psB = pb("psB", [128, 1024])
        psC = pb("psC", [128, 1024])
        psD = pb("psD", [128, 1024])
        firsts_ps = psA[0:P, :].rearrange("p (b c) -> p b c", b=2)[:, :, 0:HALF]
        uT_ps = psC[:, 0:256].rearrange("p (k c) -> p k c", k=2)[:, :, 0:P]
        hn_ps = psC[0:P, 512:512 + D]
        hT_ps = psD[0:D, 0:P]
        elr_ps = psD[0:P, 512:512 + 2 * HEADS]
        tr_ps = psA[:, 0:GT * 128].rearrange("p (j c) -> p j c", j=GT)
        mm_ps = psB[0:P, 0:GT * 128].rearrange("p (j c) -> p j c", j=GT)

        mm2_ps = psC[0:P, 0:GT * 128].rearrange("p (j c) -> p j c", j=GT)
        mmT_ps = psB[:, 0:GT * 128].rearrange("p (j c) -> p j c", j=GT)
        wT_ps = psA[0:D, 0:10 * D].rearrange("p (j c) -> p j c", j=10)
        atT_ps = psA[:, 0:P * CH // 2].rearrange("p (k c) -> p k c", k=CH // 2)
        hid_ps = [psC[:, q * 512:q * 512 + P * CH // 2].rearrange("p (k c) -> p k c", k=CH // 2) for q in range(2)]
        msg_ps = [psD[0:P, q * 512:q * 512 + D * CH // 2].rearrange("p (k c) -> p k c", k=CH // 2) for q in range(2)]
        hist_ps = psB[0:64, 0:64]

        s_first = sem("firsts_loaded")
        s_const = sem("constants_made")
        s_firstf = sem("firsts_cast")
        s_firstp = sem("firsts_in_psum")
        s_krow = sem("row_numbers_made")
        s_drows = sem("receiver_rows_landed")
        s_start = sem("starts_made")
        s_startst = sem("starts_stored")
        s_end = sem("ends_loaded")
        s_key = sem("keys_made")
        s_keyst = sem("keys_stored")
        s_keyb = sem("keys_spread")
        s_rank = sem("ranks_made")
        s_metast = sem("meta_scattered")
        s_meta = sem("meta_loaded")
        s_nch = sem("node_chunks_made")
        s_tmax = sem("tile_chunks_made")
        s_cs = sem("chunk_starts_made")
        s_perm = sem("perm_made")
        s_bix = sem("block_index_made")
        s_raw = [sem(f"senders_landed{i}") for i in range(2)]
        s_rawrdy = sem("senders_ready")
        s_recm = sem("record_made")
        s_recst = [sem(f"record_stored{i}") for i in range(2)]
        s_recfree = sem("record_buffer_free")
        s_x = sem("x_gathered")
        s_w0 = sem("attention_weights_loaded")
        s_WL = sem("attention_vectors_folded")
        s_pad = sem("padding_rows_stored")
        s_var = sem("variance_made")
        s_std = sem("deviation_made")
        s_h = sem("normed_made")
        s_itr = sem("init_transposed")
        s_itrs = sem("init_transpose_copied")
        s_imm = sem("init_scores_made")
        s_tabr = sem("table_rows_made")
        s_tabst = sem("table_scattered")
        s_idx = [sem(f"index_loaded{i}") for i in range(2)]
        s_land = [sem(f"rows_landed{i}") for i in range(2)]
        s_rows = sem("rows_ready")
        s_free = sem("rows_free")
        s_z = sem("scores_ready")
        s_p = sem("probs_ready")
        s_u = sem("tile_sums_ready")
        s_uTp = sem("sums_transposed")
        s_uT = sem("sums_transpose_copied")
        s_hn = sem("new_rows_in_psum")
        s_hs = sem("new_rows_copied")
        s_hTp = sem("rows_transposed")
        s_hT = sem("rows_transpose_copied")
        s_elr = sem("attention_scores_made")
        s_tile = sem("tile_finished")
        s_gate = sem("gates_passed")
        s_w1 = sem("message_weights_loaded")
        s_w2 = sem("other_weights_loaded")
        s_wTp = sem("weights_transposed")
        s_wT = sem("weights_transpose_copied")
        s_tr = sem("group_transposed")
        s_trs = sem("group_transpose_copied")
        s_mm = sem("group_product_made")
        s_mms = sem("group_product_copied")
        s_mm2 = sem("group_second_product_made")
        s_mm2s = sem("group_second_product_used")
        s_bn = sem("features_centered")
        s_bns = sem("feature_deviation_made")
        s_scale = sem("feature_scale_made")
        s_hTall = sem("features_normed")
        s_stage = sem("layer_weights_staged")
        s_tab1 = sem("message_table_made")
        s_tab2 = sem("sum_tables_made")
        s_land1 = [sem(f"message_rows_landed{i}") for i in range(2)]
        s_at = sem("edge_features_staged")
        s_atTp = sem("edge_features_transposed")
        s_atT = sem("edge_transpose_copied")
        s_pre = sem("node_parts_staged")
        s_hidp = sem("hidden_made")
        s_hid = sem("hidden_rectified")
        s_msg = sem("messages_made")
        s_msgu = sem("messages_used")
        s_oh = sem("one_hots_made")
        s_hist = sem("counts_made")
        s_histo = sem("counts_summed")
        s_histst = sem("counts_stored")
        s_deg = sem("counts_gathered")
        s_srcc = sem("senders_loaded")
        s_out = sem("output_ready")
        s_outst = sem("output_stored")

        MAXC = MAXG - 1

        def wait_reg(eng, sem_, value):
            eng.wait_ge(sem_, value).then_inc(s_gate, 1)

        def chunk_range(eng, t):
            lo = eng.value_load(cs_i[0:1, bass.ds(t, 1)], min_val=0, max_val=MAXC)
            hi = eng.value_load(cs_i[0:1, bass.ds(t + 1, 1)], min_val=1, max_val=MAXC)
            return lo, hi

        def chunk_count(eng):
            return eng.value_load(cs_i[0:1, T:T + 1], min_val=2, max_val=MAXC)

        block = ctx.enter_context(nc.Block())

        @block.sync
        def _(eng):
            with nc.allow_non_contiguous_dma("the receivers of every 125th edge, and node records"):
                eng.dma_start(firsts_i[:, :], dst_in.rearrange("(k m) -> m k", m=ROWLEN)[0:1, :])\
                   .then_inc(s_first, 16)
                for l in range(L0):
                    eng.dma_start(W0k[:, l, :, :], W0[l].rearrange("k (h d) -> k h d", h=HEADS)).then_inc(s_w0, 16)
                    for hh in range(2):
                        eng.dma_start(W0s[hh * D:(hh + 1) * D, l, :, :],
                                      W0[l].rearrange("k (a b d) -> k b a d", a=2, b=2)[:, hh]).then_inc(s_w0, 16)
                eng.dma_start(alr[:, 0, :, :, :], al0.unsqueeze(0).to_broadcast([D, L0, HEADS, D])).then_inc(s_w0, 16)
                eng.dma_start(alr[:, 1, :, :, :], ar0.unsqueeze(0).to_broadcast([D, L0, HEADS, D])).then_inc(s_w0, 16)
                eng.dma_start(gbb[:, :, :, :], gb0.rearrange("l (h d) -> l h d", h=HEADS).unsqueeze(0)
                              .to_broadcast([P, L0, HEADS, D])).then_inc(s_w0, 16)
                eng.dma_start(hbb[:, :], hb0.unsqueeze(0).to_broadcast([P, D])).then_inc(s_w0, 16)
                eng.dma_start(W1ab[:, 0, :], mW1[0:D, :]).then_inc(s_w1, 16)
                eng.dma_start(W1ab[:, 1, :], mW1[D:2 * D, :]).then_inc(s_w1, 16)
                for k in range(2):
                    eng.dma_start(W1c[k * D:(k + 1) * D, :], mW1[2 * D:3 * D, :]).then_inc(s_w1, 16)
                eng.dma_start(W2s[:, :], mW2).then_inc(s_w1, 16)
                eng.dma_start(b1b[:, :], mb1.unsqueeze(0).to_broadcast([P, HID])).then_inc(s_w1, 16)
                eng.dma_start(b2b[:, :], mb2.unsqueeze(0).to_broadcast([P, D])).then_inc(s_w1, 16)
                eng.dma_start(nW1s[:, :], nW1).then_inc(s_w1, 16)
                eng.dma_start(nW2s[:, :], nW2).then_inc(s_w1, 16)
                eng.dma_start(nb1c[:, :], nb1.unsqueeze(1)).then_inc(s_w1, 16)
                eng.dma_start(nb2b[:, :], nb2.unsqueeze(0).to_broadcast([P, D])).then_inc(s_w1, 16)
                eng.dma_start(lnSb[:, :], lnS.unsqueeze(0).to_broadcast([P, D])).then_inc(s_w1, 16)
                eng.dma_start(lnOb[:, :], lnO.unsqueeze(0).to_broadcast([P, D])).then_inc(s_w1, 16)
                eng.dma_start(wnat[:, 0:3, :], Wl2.rearrange("l o k -> o l k")).then_inc(s_w2, 16)
                eng.dma_start(wnat[:, 3:6, :], Wr2.rearrange("l o k -> o l k")).then_inc(s_w2, 16)
                eng.dma_start(wnat[:, 6:9, :], Wp2.rearrange("o (l k) -> o l k", l=L2)).then_inc(s_w2, 16)
                eng.dma_start(wnat[:, 9, :], W3).then_inc(s_w2, 16)
                for k, v in enumerate((b2_, gam2, bet2)):
                    eng.dma_start(bnc[:, k, :], v.rearrange("l d -> d l")).then_inc(s_w2, 16)
                eng.dma_start(bpb[:, :], bp2.unsqueeze(0).to_broadcast([P, D])).then_inc(s_w2, 16)
                eng.dma_start(b3b[:, :], b3.unsqueeze(0).to_broadcast([P, D])).then_inc(s_w2, 16)
                eng.dma_start(srcs_i[:, :], src_in.rearrange("(p c) -> p c", p=P)).then_inc(s_srcc, 16)
                eng.wait_ge(s_start, 2)
                eng.dma_start(starts_d[0:N].rearrange("(p t) -> p t", t=T), start_i[:, :]).then_inc(s_startst, 16)
                eng.dma_start(starts_d[N:N + 1].unsqueeze(0), tail_end[:, :]).then_inc(s_startst, 16)
                eng.wait_ge(s_startst, 32)
                eng.dma_start(end_i[:, :], starts_d[1:N + 1].rearrange("(p t) -> p t", t=T)).then_inc(s_end, 16)
                eng.wait_ge(s_key, 1)
                eng.dma_start(keys_d.rearrange("(p t) -> p t", t=T), pf[5][:, :]).then_inc(s_keyst, 16)
                eng.wait_ge(s_keyst, 16)
                eng.dma_start(keys_b[:, :], keys_d.unsqueeze(0).to_broadcast([P, N])).then_inc(s_keyb, 16)
                eng.wait_ge(s_metast, 16 * T)
                eng.dma_start(meta[:, :, :], meta_d.rearrange("(t p) c -> p t c", p=P)).then_inc(s_meta, 16)
                eng.wait_ge(s_const, 1)
                eng.dma_start(tab0_d[N:N + 1, 0:D + 1], padrow[:, 0:D + 1]).then_inc(s_pad, 16)
                eng.dma_start(tab0_d[N:N + 1, D + 1:D + 1 + HEADS],
                              padrow[:, HID + 1:HID + 1 + HEADS]).then_inc(s_pad, 16)
                eng.dma_start(tab1_d[N:N + 1, :], padrow[:, 0:HID + 1]).then_inc(s_pad, 16)
                eng.dma_start(tab2_d[N:N + 1, :], padrow[:, 0:D]).then_inc(s_pad, 16)

                eng.wait_ge(s_cs, 1)
                pairs = chunk_count(eng) // 2
                with eng.Fori(0, pairs) as n:
                    for b in range(2):
                        eng.wait_ge(s_raw[b], (n + 1) * 16 * BPC).then_inc(s_rawrdy, 1)
                        eng.wait_ge(s_recm, n * 2 + b + 1)
                        eng.dma_start(rec_d[bass.ds(n * 2 + b, 1)].rearrange("o p c -> (o p) c"), recs[:, b, :])\
                           .then_inc(s_recst[b], 16)
                        eng.wait_ge(s_recst[b], (n + 1) * 16).then_inc(s_recfree, 1)

                def load_index(c, b):
                    eng.dma_start(idx[:, b, :], rec_d[bass.ds(c, 1)].rearrange("o p c -> (o p) c"))\
                       .then_inc(s_idx[b], 16)

                def relay_pass(k, landed, per_chunk):
                    with eng.Fori(0, pairs) as n:
                        following = eng.snap((n + 1) % pairs)
                        for b in range(2):
                            eng.wait_ge(landed[b], (k * pairs + n + 1) * 16 * per_chunk).then_inc(s_rows, 1)
                            load_index(following * 2 + b, b)

                for b in range(2):
                    load_index(b, b)

                with eng.Fori(0, L0) as layer:
                    relay_pass(layer, s_land, CH)
                relay_pass(0, s_land1, CH + BPC)
                eng.wait_ge(s_histo, 1)
                eng.dma_start(hist_d.rearrange("(a b) o -> a (b o)", b=64), hist[:, :]).then_inc(s_histst, 16)
                with eng.Fori(0, L2 + 1) as layer:
                    relay_pass(layer + L0, s_land, CH)
                for b in range(2):
                    wait_reg(eng, s_idx[b], ((L0 + 1 + L2 + 1) * pairs + 1) * 16)
                eng.wait_ge(s_outst, 16 * T)

        @block.gpsimd
        def _(eng):
            eng.memset(ident[:, :], 0.0)
            eng.memset(ones[:, :], 1.0)
            eng.memset(tail_end[:, :], E)
            eng.memset(padrow[:, 0:HID + 1], 0.0)
            eng.memset(padrow[:, HID + 1:HID + 1 + HEADS], FAR)
            eng.memset(step3[:, 0:1], float(BPC))
            eng.memset(step3[:, 1:3], float(-CH))
            eng.iota(nodeid_i[:, :], pattern=[[1, T]], base=0, channel_multiplier=T)
            eng.iota(iota8_i[:, :], pattern=[[1, CH]], base=0, channel_multiplier=0)
            eng.iota(iota64_i[:, :], pattern=[[1, 64]], base=0, channel_multiplier=0)
            eng.drain()
            eng.affine_select(out=ident[:, :], in_=ident[:, :], compare_op=ALU.not_equal, fill=1.0,
                              base=0, pattern=[[-1, 128]], channel_multiplier=1)
            eng.drain().then_inc(s_const, 1)

            eng.wait_ge(s_krow, 1)
            dst_rows = dst_in.rearrange("(k m) -> k m", m=ROWLEN)
            for t in range(T):
                eng.indirect_dma_start(out=drows[:, t, :], out_offset=None, in_=dst_rows,
                                       in_offset=bass.IndirectOffsetOnAxis(ap=krow_i[:, t:t + 1], axis=0))\
                   .then_inc(s_drows, 16)
            eng.wait_ge(s_rank, 1)
            for t in range(T):
                eng.indirect_dma_start(out=meta_d, out_offset=bass.IndirectOffsetOnAxis(ap=rank_i[:, t:t + 1], axis=0),
                                       in_=meta_o[:, t, :], in_offset=None).then_inc(s_metast, 16)
            eng.wait_ge(s_nch, 1)
            eng.partition_all_reduce(tmax[:, :], nch_f[:, :], P, bass.bass_isa.ReduceOp.max).then_inc(s_tmax, 1)
            eng.wait_ge(s_perm, 1)
            for t in range(T):
                eng.indirect_dma_start(out=x[:, t, :], out_offset=None, in_=x_in,
                                       in_offset=bass.IndirectOffsetOnAxis(ap=perm[:, t:t + 1], axis=0))\
                   .then_inc(s_x, 16)

            eng.wait_ge(s_cs, 1)
            pairs = chunk_count(eng) // 2
            src_blocks = src_in.rearrange("(k m) -> k m", m=BLK)
            with eng.Fori(0, pairs) as n:
                for b in range(2):
                    wait_reg(eng, s_bix, n * 2 + b + 1)
                    for j in range(BPC):
                        eng.indirect_dma_start(out=raw_src[:, b, j * BLK:(j + 1) * BLK], out_offset=None, in_=src_blocks,
                                               in_offset=bass.IndirectOffsetOnAxis(ap=blk_ix[:, b, j:j + 1], axis=0))\
                           .then_inc(s_raw[b], 16)

            def scatter_table(table, width, k):
                for t in range(T):
                    eng.indirect_dma_start(out=table, out_offset=bass.IndirectOffsetOnAxis(ap=perm[:, t:t + 1], axis=0),
                                           in_=tab[:, t, 0:width], in_offset=None).then_inc(s_tabst, 16)
                wait_reg(eng, s_tabst, (k + 1) * 16 * T)

            attr_blocks = attr_in.rearrange("(k m) d -> k (m d)", m=BLK)

            def gather_pass(k, table, width, landed, edges=False):
                with eng.Fori(0, pairs) as n:
                    for b in range(2):
                        eng.wait_ge(s_idx[b], (k * pairs + n + 1) * 16)
                        wait_reg(eng, s_free, (k * pairs + n) * 2 + b + 1)
                        for s in range(CH):
                            eng.indirect_dma_start(out=rows[:, b, s, 0:width], out_offset=None, in_=table,
                                                   in_offset=bass.IndirectOffsetOnAxis(ap=idx[:, b, s:s + 1], axis=0))\
                               .then_inc(landed[b], 16)
                        for j in range(BPC if edges else 0):
                            eng.indirect_dma_start(out=attr[:, b, j * BLK:(j + 1) * BLK, :].rearrange("p s d -> p (s d)"),
                                                   out_offset=None, in_=attr_blocks,
                                                   in_offset=bass.IndirectOffsetOnAxis(ap=idx[:, b, CH + j:CH + j + 1], axis=0))\
                               .then_inc(landed[b], 16)

            eng.wait_ge(s_pad, 64)
            with eng.Fori(0, L0) as layer:
                wait_reg(eng, s_tabr, (layer + 1) * T)
                scatter_table(tab0_d, D + 1 + HEADS, layer)
                gather_pass(layer, tab0_d, D + 1 + HEADS, s_land)
            eng.wait_ge(s_tab1, 2)
            scatter_table(tab1_d, HID + 1, L0)
            gather_pass(L0, tab1_d, HID + 1, s_land1, edges=True)
            eng.wait_ge(s_histst, 16)
            for t in range(T):
                eng.indirect_dma_start(out=odeg[:, t:t + 1], out_offset=None, in_=hist_d,
                                       in_offset=bass.IndirectOffsetOnAxis(ap=perm[:, t:t + 1], axis=0)).then_inc(s_deg, 16)
            with eng.Fori(0, L2 + 1) as layer:
                wait_reg(eng, s_tab2, layer + 1)
                scatter_table(tab2_d, D, layer + (L0 + 1))
                gather_pass(layer + (L0 + 1), tab2_d, D, s_land)
            eng.wait_ge(s_out, 1)
            for t in range(T):
                eng.indirect_dma_start(out=out, out_offset=bass.IndirectOffsetOnAxis(ap=perm[:, t:t + 1], axis=0),
                                       in_=x[:, t, :], in_offset=None).then_inc(s_outst, 16)
            eng.wait_ge(s_outst, 16 * T)

        @block.scalar
        def _(eng):
            def deviations(k):
                eng.wait_ge(s_var, k)
                eng.activation(std[:, :], stat[:, :], ACT.Sqrt).then_inc(s_std, 1)

            deviations(1)
            for g in range(NG):
                j = slice(g * GT, (g + 1) * GT)
                eng.wait_ge(s_itr, g + 1)
                eng.activation(tr5[0:D, :, :], tr_ps[0:D, :, 0:P], ACT.Copy).then_inc(s_itrs, 1)
                eng.wait_ge(s_imm, g + 1)
                eng.activation(tab[:, j, D + 1:D + 1 + HEADS], mm_ps[:, :, 0:HEADS], ACT.Copy)
                eng.activation(er[:, j, :], mm_ps[:, :, HEADS:2 * HEADS], ACT.Copy)
                eng.drain().then_inc(s_tabr, GT)

            eng.wait_ge(s_cs, 1)
            chunks = chunk_count(eng)
            with eng.Fori(0, L0) as layer:
                with eng.Fori(0, T) as t:
                    lo, hi = chunk_range(eng, t)
                    with eng.Fori(lo, hi) as c:
                        eng.wait_ge(s_z, layer * chunks + c + 1)
                        eng.activation(pe[:, :, :], pz[:, :, :], ACT.Exp).then_inc(s_p, 1)
                    done = layer * T + t + 1
                    eng.wait_ge(s_uTp, done)
                    eng.activation(uT[:, :, :], uT_ps, ACT.Copy).then_inc(s_uT, 1)
                    eng.wait_ge(s_hn, done)
                    eng.activation(hs[:, :], hn_ps, ACT.Copy).then_inc(s_hs, 1)
                    eng.activation(tab[:, bass.ds(t, 1), 0:D].rearrange("p o d -> p (o d)"), hn_ps, ACT.Copy)
                    eng.wait_ge(s_hTp, done)
                    eng.activation(hT[:, :], hT_ps, ACT.Copy).then_inc(s_hT, 1)
                    eng.wait_ge(s_elr, done)
                    eng.activation(tab[:, bass.ds(t, 1), D + 1:D + 1 + HEADS].rearrange("p o d -> p (o d)"),
                                   elr_ps[:, 0:HEADS], ACT.Copy)
                    eng.activation(er[:, bass.ds(t, 1), :].rearrange("p o d -> p (o d)"),
                                   elr_ps[:, HEADS:2 * HEADS], ACT.Copy)
                    eng.drain().then_inc(s_tabr, 1)

            eng.wait_ge(s_wTp, 1)
            eng.activation(wT[:, :, :], wT_ps, ACT.Copy).then_inc(s_wT, 1)

            deviations(2)
            for g in range(NG):
                j = slice(g * GT, (g + 1) * GT)
                eng.wait_ge(s_tr, g + 1)
                eng.activation(tr5[0:D, :, :], tr_ps[0:D, :, 0:P], ACT.Copy).then_inc(s_trs, 1)
                eng.wait_ge(s_mm, g + 1)
                eng.activation(tab[:, j, 0:HID], mm_ps, ACT.Copy).then_inc(s_mms, 1)
            eng.drain().then_inc(s_tab1, 1)
            with eng.Fori(0, T) as t:
                lo, hi = chunk_range(eng, t)
                with eng.Fori(lo, hi) as c:
                    eng.wait_ge(s_rows, chunks * L0 + c + 1)
                    eng.activation(at_s[:, :, :], attr[:, bass.ds(c % 2, 1), :, :].rearrange("p o s d -> p (o s) d"),
                                   ACT.Copy).then_inc(s_at, 1)
                    eng.wait_ge(s_atTp, c + 1)
                    eng.activation(atT[:, :, :], atT_ps, ACT.Copy).then_inc(s_atT, 1)
                    for q in range(2):
                        eng.wait_ge(s_hidp, c * 2 + q + 1)
                        eng.activation(hidT[:, q, :, :], hid_ps[q], ACT.Relu).then_inc(s_hid, 1)
            eng.wait_ge(s_w1, 16 * 13)
            for g in range(NG):
                eng.wait_ge(s_tr, NG + g + 1)
                eng.activation(tr5[:, :, :], tr_ps[:, :, 0:P], ACT.Copy).then_inc(s_trs, 1)
                eng.wait_ge(s_mm, NG + g + 1)
                eng.activation(zT5[:, :, :], mmT_ps[:, :, 0:P], ACT.Relu, bias=nb1c[:, 0:1]).then_inc(s_mms, 1)
            deviations(3)

            deviations(4)
            for g in range(NG):
                j = slice(g * GT, (g + 1) * GT)
                eng.wait_ge(s_tr, 2 * NG + g + 1)
                eng.activation(hTall[:, j, :], tr_ps[0:D, :, 0:P], ACT.Copy).then_inc(s_trs, 1)
            with eng.Fori(0, L2) as layer:
                base = eng.snap(layer * NG)
                for g in range(NG):
                    j = slice(g * GT, (g + 1) * GT)
                    eng.wait_ge(s_tr, base + (3 * NG + g + 1))
                    eng.activation(tr5[0:D, :, :], tr_ps[0:D, :, 0:P], ACT.Copy).then_inc(s_trs, 1)
                    eng.wait_ge(s_mm, base + (2 * NG + g + 1))
                    eng.activation(yT[:, j, :], mmT_ps[0:D, :, 0:P], ACT.Identity, bias=bnst[:, 4:5]).then_inc(s_mms, 1)
                eng.wait_ge(s_bn, layer + 1)
                eng.activation(bnst[:, 2:3], bnst[:, 1:2], ACT.Sqrt).then_inc(s_bns, 1)
                eng.wait_ge(s_scale, layer + 1)
                eng.activation(hTall[:, :, :], yT[:, :, :], ACT.Relu, bias=bnst[:, 6:7], scale=bnst[:, 5:6])\
                   .then_inc(s_hTall, 1)
                for g in range(NG):
                    j = slice(g * GT, (g + 1) * GT)
                    eng.wait_ge(s_mm2, base + (2 * NG + g + 1))
                    eng.activation(tab[:, j, 0:D], mm2_ps[:, :, 0:D], ACT.Copy).then_inc(s_mm2s, 1)

            deviations(5)
            for g in range(NG):
                eng.wait_ge(s_tr, (3 + L2) * NG + g + 1)
                eng.activation(tr5[0:D, :, :], tr_ps[0:D, :, 0:P], ACT.Copy).then_inc(s_trs, 1)
            deviations(6)

        @block.tensor
        def _(eng):
            eng.wait_ge(s_firstf, 1)
            eng.wait_ge(s_const, 1)
            for b in range(2):
                last = eng.matmul(firsts_ps[:, b, :], ones[0:1, 0:P], firsts[0:1, b * HALF:(b + 1) * HALF],
                                  start=True, stop=True)
            last.then_inc(s_firstp, 1)

            eng.wait_ge(s_WL, 1)
            eng.wait_ge(s_h, 1)
            for g in range(NG):
                if g:
                    eng.wait_ge(s_tabr, g * GT)
                for j in range(GT):
                    last = eng.transpose(tr_ps[0:D, j, 0:P], h[:, g * GT + j, :], ident[0:P, 0:P])
                last.then_inc(s_itr, 1)
                eng.wait_ge(s_itrs, g + 1)
                for j in range(GT):
                    last = eng.matmul(mm_ps[:, j, 0:2 * HEADS], tr5[0:D, j, :], WL[:, 0, :], start=True, stop=True)
                last.then_inc(s_imm, 1)

            with eng.Fori(0, L0) as layer:
                with eng.Fori(0, T) as t:
                    done = layer * T + t + 1
                    wait_reg(eng, s_u, done)
                    for k in range(2):
                        last = eng.transpose(uT_ps[:, k, :], u[:, 2 * k:2 * k + 2, :].rearrange("p h d -> p (h d)"),
                                             ident[0:P, 0:P])
                    last.then_inc(s_uTp, 1)
                    eng.wait_ge(s_uT, done)
                    wl = W0s[:, bass.ds(layer, 1), :, :].rearrange("p o k d -> p (o k) d")
                    eng.matmul(hn_ps, uT[:, 0, :], wl[:, 0, :], start=True, stop=False)
                    eng.matmul(hn_ps, uT[:, 1, :], wl[:, 1, :], start=False, stop=False)
                    eng.matmul(hn_ps, ident[0:P, 0:P], gbs[:, bass.ds(layer, 1), :].rearrange("p o d -> p (o d)"),
                               start=False, stop=True).then_inc(s_hn, 1)
                    wait_reg(eng, s_hs, done)
                    eng.transpose(hT_ps, hs[:, :], ident[0:P, 0:P]).then_inc(s_hTp, 1)
                    eng.wait_ge(s_hT, done)
                    eng.matmul(elr_ps, hT[:, :], WL[:, bass.ds(layer + 1, 1), :].rearrange("p o d -> p (o d)"),
                               start=True, stop=True).then_inc(s_elr, 1)

            eng.wait_ge(s_w2, 16 * 9)
            for k in range(10):
                last = eng.transpose(wT_ps[:, k, :], wnat[:, k, :], ident[0:D, 0:D])
            last.then_inc(s_wTp, 1)

            eng.wait_ge(s_w1, 16 * 13)
            eng.wait_ge(s_h, 2)
            for g in range(NG):
                if g == 0:
                    eng.wait_ge(s_wT, 1)
                for j in range(GT):
                    last = eng.transpose(tr_ps[0:D, j, 0:P], h[:, g * GT + j, :], ident[0:P, 0:P])
                last.then_inc(s_tr, 1)
                eng.wait_ge(s_trs, g + 1)
                if g:
                    eng.wait_ge(s_mms, g)
                for j in range(GT):
                    last = eng.matmul(mm_ps[:, j, :], tr5[0:D, j, :], W1ab[:, 0, :], start=True, stop=True)
                last.then_inc(s_mm, 1)
                if g:
                    eng.wait_ge(s_mm2s, g)
                for j in range(GT):
                    last = eng.matmul(mm2_ps[:, j, :], tr5[0:D, j, :], W1ab[:, 1, :], start=True, stop=True)
                last.then_inc(s_mm2, 1)
            eng.wait_ge(s_tab1, 2)
            with eng.Fori(0, T) as t:
                lo, hi = chunk_range(eng, t)
                wait_reg(eng, s_oh, t + 1)
                for k in range(OHC):
                    last = eng.matmul(hist_ps, oh[:, 0, k, :], oh[:, 1, k, :], start=(k == 0), stop=(k == OHC - 1))
                last.then_inc(s_hist, 1)
                with eng.Fori(lo, hi) as c:
                    wait_reg(eng, s_at, c + 1)
                    for k in range(CH // 2):
                        last = eng.transpose(atT_ps[:, k, :], at_s[:, 2 * k:2 * k + 2, :].rearrange("p s d -> p (s d)"),
                                             ident[0:P, 0:P])
                    last.then_inc(s_atTp, 1)
                    wait_reg(eng, s_atT, c + 1)
                    for q in range(2):
                        eng.matmul(hid_ps[q], W1c[q * D:(q + 1) * D, :], atT[q * D:(q + 1) * D, :, :],
                                   start=True, stop=False)
                        wait_reg(eng, s_pre, c * 2 + q + 1)
                        for k in range(CH // 2):
                            last = eng.matmul(hid_ps[q][:, k, :], pre_s[:, 2 * k + q, :], ident[0:P, 0:P],
                                              start=False, stop=(k == CH // 2 - 1))
                        last.then_inc(s_hidp, 1)
                    for q in range(2):
                        wait_reg(eng, s_hid, c * 2 + q + 1)
                        for k in range(CH // 2):
                            last = eng.matmul(msg_ps[q][:, k, :], hidT[:, q, k, :], W2s[:, :], start=True, stop=True)
                        last.then_inc(s_msg, 1)
            eng.wait_ge(s_tab1, 3)
            for g in range(NG):
                for j in range(GT):
                    last = eng.transpose(tr_ps[:, j, 0:P], cat[:, g * GT + j, :], ident[0:P, 0:P])
                last.then_inc(s_tr, 1)
                eng.wait_ge(s_trs, NG + g + 1)
                for j in range(GT):
                    last = eng.matmul(mmT_ps[:, j, 0:P], nW1s[:, :], tr5[:, j, :], start=True, stop=True)
                last.then_inc(s_mm, 1)
                eng.wait_ge(s_mms, NG + g + 1)
                if g:
                    eng.wait_ge(s_mm2s, NG + g)
                for j in range(GT):
                    last = eng.matmul(mm2_ps[:, j, 0:D], zT5[:, j, :], nW2s[:, :], start=True, stop=True)
                last.then_inc(s_mm2, 1)

            eng.wait_ge(s_h, 3)
            for g in range(NG):
                if g:
                    eng.wait_ge(s_trs, 2 * NG + g)
                for j in range(GT):
                    last = eng.transpose(tr_ps[0:D, j, 0:P], h[:, g * GT + j, :], ident[0:P, 0:P])
                last.then_inc(s_tr, 1)
            with eng.Fori(0, L2) as layer:
                base = eng.snap(layer * NG)
                wait_reg(eng, s_stage, layer + 1)
                for g in range(NG):
                    if g == 0:
                        wait_reg(eng, s_trs, base + 3 * NG)
                    for j in range(GT):
                        last = eng.transpose(tr_ps[0:D, j, 0:P], agg[:, g * GT + j, :], ident[0:P, 0:P])
                    last.then_inc(s_tr, 1)
                    wait_reg(eng, s_trs, base + (3 * NG + g + 1))
                    wait_reg(eng, s_mms, base + (2 * NG + g))
                    for j in range(GT):
                        eng.matmul(mmT_ps[0:D, j, 0:P], wst[:, 0, :], tr5[0:D, j, :], start=True, stop=False)
                        last = eng.matmul(mmT_ps[0:D, j, 0:P], wst[:, 1, :], hTall[:, g * GT + j, :],
                                          start=False, stop=True)
                    last.then_inc(s_mm, 1)
                wait_reg(eng, s_hTall, layer + 1)
                for g in range(NG):
                    wait_reg(eng, s_mm2s, (base + g) * 2 + 2 * NG)
                    for j in range(GT):
                        last = eng.matmul(mm2_ps[:, j, :], hTall[:, g * GT + j, :], iw[:, :], start=True, stop=True)
                    last.then_inc(s_mm2, 1)

            eng.wait_ge(s_h, 4)
            for g in range(NG):
                for j in range(GT):
                    last = eng.transpose(tr_ps[0:D, j, 0:P], h[:, g * GT + j, :], ident[0:P, 0:P])
                last.then_inc(s_tr, 1)
                eng.wait_ge(s_trs, (3 + L2) * NG + g + 1)
                if g:
                    eng.wait_ge(s_mm2s, 2 * NG + 2 * L2 * NG + g)
                for j in range(GT):
                    last = eng.matmul(mm2_ps[:, j, 0:D], tr5[0:D, j, :], wT[:, 9, :], start=True, stop=True)
                last.then_inc(s_mm2, 1)

        @block.vector
        def _(eng):
            V = nc.vector

            eng.wait_ge(s_first, 16)
            V.tensor_copy(firsts[:, :], firsts_i[:, :]).then_inc(s_firstf, 1)
            eng.wait_ge(s_const, 1)
            V.tensor_copy(nodeid[:, :], nodeid_i[:, :])
            V.tensor_copy(iota8[:, :], iota8_i[:, :])
            V.tensor_copy(iota64[:, :], iota64_i[:, :])
            eng.wait_ge(s_firstp, 1)
            V.tensor_copy(firsts_b[:, :].rearrange("p (b c) -> p b c", b=2), firsts_ps)
            V.drain()
            for t in range(T):
                V.tensor_scalar(wide[:, 0:NROW], firsts_b[:, :], nodeid[:, t:t + 1], 0.0, ALU.is_lt, ALU.add,
                                accum_out=kcount[:, t:t + 1])
                V.drain()
            V.tensor_scalar(krow[:, :], kcount[:, :], -1.0, 0.0, ALU.add, ALU.max)
            V.drain()
            V.tensor_copy(krow_i[:, :], krow[:, :]).then_inc(s_krow, 1)
            eng.wait_ge(s_drows, 16 * T)
            for t in range(T):
                V.tensor_scalar(wide[:, 0:ROWLEN], drows[:, t, :], nodeid[:, t:t + 1], 0.0, ALU.is_lt, ALU.add,
                                accum_out=pf[0][:, t:t + 1])
                V.drain()
            V.scalar_tensor_tensor(pf[1][:, :], krow[:, :], float(ROWLEN), pf[0][:, :], ALU.mult, ALU.add)
            V.drain()
            V.tensor_copy(start_i[:, :], pf[1][:, :]).then_inc(s_start, 2)
            V.drain()
            V.tensor_scalar(pi[0][:, :], start_i[:, :], 2, None, ALU.logical_shift_right)
            V.drain()
            V.tensor_copy(pf[2][:, :], pi[0][:, :])
            eng.wait_ge(s_end, 16)
            V.tensor_copy(pf[3][:, :], end_i[:, :])
            V.drain()
            V.scalar_tensor_tensor(pf[4][:, :], pf[2][:, :], float(-BLK), pf[3][:, :], ALU.mult, ALU.add)
            V.drain()
            V.tensor_scalar(pi[1][:, :], pf[4][:, :], float(BLK - 1), None, ALU.add)
            V.drain()
            V.tensor_scalar(pi[2][:, :], pi[1][:, :], 2, None, ALU.logical_shift_right)
            V.drain()
            V.tensor_scalar(pf[0][:, :], pi[2][:, :], float(KEYCAP), float(KEYMUL), ALU.min, ALU.mult)
            V.tensor_scalar(pi[1][:, :], pi[2][:, :], 1.0, None, ALU.add)
            V.drain()
            V.tensor_tensor(pf[5][:, :], pf[0][:, :], nodeid[:, :], ALU.add).then_inc(s_key, 1)
            V.tensor_scalar(pi[3][:, :], pi[1][:, :], 1, None, ALU.logical_shift_right)
            V.drain()
            V.tensor_copy(meta_o[:, :, 0], nodeid_i[:, :])
            V.tensor_copy(meta_o[:, :, 1], start_i[:, :])
            V.tensor_copy(meta_o[:, :, 2], end_i[:, :])
            V.tensor_copy(meta_o[:, :, 3], pi[3][:, :])
            eng.wait_ge(s_keyb, 16)
            for t in range(T):
                V.tensor_scalar(wide[:, 0:N], keys_b[:, :], pf[5][:, t:t + 1], 0.0, ALU.is_gt, ALU.add,
                                accum_out=pf[0][:, t:t + 1])
                V.drain()
            V.tensor_copy(rank_i[:, :], pf[0][:, :])
            V.drain().then_inc(s_rank, 1)

            eng.wait_ge(s_meta, 16)
            V.tensor_copy(perm[:, :], meta[:, :, 0]).then_inc(s_perm, 1)
            V.tensor_copy(nch_f[:, :], meta[:, :, 3]).then_inc(s_nch, 1)
            V.tensor_scalar(pi[0][:, :], meta[:, :, 1], 2, None, ALU.logical_shift_right)
            V.tensor_copy(pf[1][:, :], meta[:, :, 1])
            V.tensor_copy(pf[2][:, :], meta[:, :, 2])
            V.drain()
            V.tensor_copy(edge_cur[:, :, 0], pi[0][:, :])
            V.tensor_tensor(deg[:, :], pf[2][:, :], pf[1][:, :], ALU.subtract)
            V.drain()
            V.scalar_tensor_tensor(edge_cur[:, :, 1], edge_cur[:, :, 0], float(-BLK), pf[1][:, :], ALU.mult, ALU.add)
            V.scalar_tensor_tensor(edge_cur[:, :, 2], edge_cur[:, :, 0], float(-BLK), pf[2][:, :], ALU.mult, ALU.add)
            V.memset(cs_a[:, 0:1], 0.0)
            V.memset(cs_b[:, 0:1], 0.0)
            eng.wait_ge(s_tmax, 1)
            V.tensor_scalar(cs_a[:, 1:T + 1], tmax[0:1, :], 1.0, None, ALU.max)
            a, b = cs_a, cs_b
            d = 1
            while d < T + 1:
                V.drain()
                V.tensor_copy(b[:, 0:d], a[:, 0:d])
                V.tensor_tensor(b[:, d:T + 1], a[:, d:T + 1], a[:, 0:T + 1 - d], ALU.add)
                a, b = b, a
                d *= 2
            V.drain()
            V.tensor_copy(cs_i[:, :], a[:, :])
            V.drain()
            V.tensor_scalar(b[:, T:T + 1], a[:, T:T + 1], 1.0, None, ALU.add)
            V.drain()
            V.tensor_copy(pi[0][0:1, 0:1], b[:, T:T + 1])
            V.drain()
            V.tensor_scalar(cs_i[:, T:T + 1], pi[0][0:1, 0:1], 1, 1, ALU.logical_shift_right, ALU.logical_shift_left)
            V.drain().then_inc(s_cs, 1)

            chunks = chunk_count(eng)
            V.sem_inc(s_recfree, 2)
            with eng.Fori(0, T) as t:
                lo, hi = chunk_range(eng, t)
                V.tensor_copy(cur[:, :], edge_cur[:, bass.ds(t, 1), :].rearrange("p o c -> p (o c)"))
                with eng.Fori(lo, hi) as c:
                    bix = blk_ix[:, bass.ds(c % 2, 1), :].rearrange("p o c -> p (o c)")
                    raw = raw_src[:, bass.ds(c % 2, 1), :].rearrange("p o c -> p (o c)")
                    rec = recs[:, bass.ds(c % 2, 1), :].rearrange("p o c -> p (o c)")
                    V.drain()
                    V.tensor_scalar(bix, iota8[:, 0:BPC], cur[:, 0:1], float(NBLK - 1), ALU.add, ALU.min)\
                     .then_inc(s_bix, 1)
                    V.tensor_scalar(vmask[:, 0, :], iota8[:, :], cur[:, 1:2], None, ALU.is_ge)
                    V.drain()
                    V.scalar_tensor_tensor(vmask[:, 1, :], iota8[:, :], cur[:, 2:3], vmask[:, 0, :], ALU.is_lt, ALU.mult)
                    eng.wait_ge(s_recfree, c + 1)
                    wait_reg(eng, s_rawrdy, c + 1)
                    V.drain()
                    V.scalar_tensor_tensor(prod[:, 0, 0, 0:CH], raw, float(-N), vmask[:, 1, :], ALU.add, ALU.mult)
                    V.tensor_tensor(cur[:, :], cur[:, :], step3[:, :], ALU.add)
                    V.tensor_copy(rec[:, CH:CH + BPC], bix)
                    V.drain()
                    V.tensor_scalar(rec[:, 0:CH], prod[:, 0, 0, 0:CH], float(N), None, ALU.add)
                    V.drain().then_inc(s_recm, 1)

            eng.wait_ge(s_w0, 16 * (3 * L0 + 4))
            V.memset(WL[:, :, :], 0.0)
            V.drain()
            for k in range(2):
                for l in range(L0):
                    V.tensor_tensor(sq[0:D, 0:HEADS, :], W0k[:, l, :, :], alr[:, k, l, :, :], ALU.mult)
                    V.drain()
                    V.tensor_reduce(WL[:, l, k * HEADS:(k + 1) * HEADS], sq[0:D, 0:HEADS, :], AX.X, ALU.add)
                    V.drain()
            V.tensor_reduce(gbs[:, :, :], gbb[:, :, :, :].rearrange("p l h d -> p l d h"), AX.X, ALU.add)
            V.drain().then_inc(s_WL, 1)

            def normed(k, inp, outp, relu):
                V.tensor_reduce(stat[:, :], inp[:, :, :], AX.X, ALU.add)
                V.drain()
                V.tensor_scalar(stat[:, :], stat[:, :], 1.0 / D, None, ALU.mult)
                V.drain()
                V.tensor_tensor(xc[:, :, :], inp[:, :, :], stat[:, :].unsqueeze(2).to_broadcast([P, T, D]), ALU.subtract)
                V.drain()
                V.tensor_tensor(sq[:, :, :], xc[:, :, :], xc[:, :, :], ALU.mult)
                V.drain()
                V.tensor_reduce(stat[:, :], sq[:, :, :], AX.X, ALU.add)
                V.drain()
                V.tensor_scalar(stat[:, :], stat[:, :], 1.0 / D, 1e-5, ALU.mult, ALU.add).then_inc(s_var, 1)
                eng.wait_ge(s_std, k)
                V.reciprocal(rstd[:, :], std[:, :])
                V.drain()
                V.tensor_tensor(sq[:, :, :], xc[:, :, :], rstd[:, :].unsqueeze(2).to_broadcast([P, T, D]), ALU.mult)
                V.drain()
                if relu:
                    V.tensor_scalar(outp[:, :, :], sq[:, :, :], 0.0, None, ALU.max)
                else:
                    V.tensor_copy(outp[:, :, :], sq[:, :, :])
                V.drain()

            eng.wait_ge(s_x, 16 * T)
            normed(1, x, h, True)
            V.tensor_copy(tab[:, :, 0:D], h[:, :, :])
            V.memset(tab[:, :, D:D + 1], 1.0)
            V.drain().then_inc(s_h, 1)
            V.sem_inc(s_free, 2)

            with eng.Fori(0, L0) as layer:
                wait_reg(eng, s_tabr, (layer + 1) * T)
                with eng.Fori(0, T) as t:
                    lo, hi = chunk_range(eng, t)
                    own = tab[:, bass.ds(t, 1), :].rearrange("p o c -> p (o c)")
                    er_t = er[:, bass.ds(t, 1), :].rearrange("p o c -> p (o c)")
                    V.drain()
                    V.tensor_tensor(mnew[:, :], own[:, D + 1:D + 1 + HEADS], er_t, ALU.add)
                    V.tensor_copy(acc[:, :, :], own[:, 0:D + 1].unsqueeze(1).to_broadcast([P, HEADS, D + 1]))
                    V.drain()
                    V.scalar_tensor_tensor(zz[:, CH, :], mnew[:, :], 0.2, mnew[:, :], ALU.mult, ALU.max)
                    with eng.Fori(lo, hi) as c:
                        eng.wait_ge(s_rows, layer * chunks + c + 1)
                        R = rows[:, bass.ds(c % 2, 1), :, :].rearrange("p o s c -> p (o s) c")
                        V.tensor_tensor(zz[:, 0:CH, :], R[:, :, D + 1:D + 1 + HEADS],
                                        er_t.unsqueeze(1).to_broadcast([P, CH, HEADS]), ALU.add)
                        V.drain()
                        V.scalar_tensor_tensor(zz[:, 0:CH, :], zz[:, 0:CH, :], 0.2, zz[:, 0:CH, :], ALU.mult, ALU.max)
                        V.drain()
                        V.tensor_reduce(mnew[:, :], zz[:, :, :].rearrange("p s h -> p h s"), AX.X, ALU.max)
                        V.drain()
                        V.tensor_tensor(pz[:, :, :], zz[:, :, :], mnew[:, :].unsqueeze(1).to_broadcast([P, CH + 1, HEADS]),
                                        ALU.subtract).then_inc(s_z, 1)
                        V.drain()
                        V.tensor_copy(zz[:, CH, :], mnew[:, :])
                        eng.wait_ge(s_p, layer * chunks + c + 1)
                        V.tensor_tensor(acc[:, :, :], acc[:, :, :],
                                        pe[:, CH, :].unsqueeze(2).to_broadcast([P, HEADS, D + 1]), ALU.mult)
                        V.tensor_tensor(prod[:, :, :, :],
                                        R[:, :, 0:D + 1].unsqueeze(2).to_broadcast([P, CH, HEADS, D + 1]),
                                        pe[:, 0:CH, :].unsqueeze(3).to_broadcast([P, CH, HEADS, D + 1]),
                                        ALU.mult).then_inc(s_free, 1)
                        V.drain()
                        V.tensor_reduce(part[:, :, :], prod[:, :, :, :].rearrange("p s h d -> p h d s"), AX.X, ALU.add)
                        V.drain()
                        V.tensor_tensor(acc[:, :, :], acc[:, :, :], part[:, :, :], ALU.add)
                        V.drain()
                    V.reciprocal(rden[:, :], acc[:, :, D])
                    V.drain()
                    V.tensor_tensor(u[:, :, :], acc[:, :, 0:D], rden[:, :].unsqueeze(2).to_broadcast([P, HEADS, D]),
                                    ALU.mult).then_inc(s_u, 1)
            eng.wait_ge(s_tabr, (L0 + 1) * T)
            V.tensor_tensor(x[:, :, :], x[:, :, :], tab[:, :, 0:D], ALU.add)
            V.drain()
            V.tensor_tensor(x[:, :, :], x[:, :, :], hbb[:, :].unsqueeze(1).to_broadcast([P, T, D]), ALU.add)
            V.drain()

            normed(2, x, h, True)
            V.tensor_copy(cat[:, :, 0:D], h[:, :, :])
            V.memset(tab[:, :, HID:HID + 1], 1.0)
            V.drain().then_inc(s_h, 1)
            eng.wait_ge(s_w1, 16 * 13)
            for g in range(NG):
                j = slice(g * GT, (g + 1) * GT)
                eng.wait_ge(s_mm2, g + 1)
                V.tensor_tensor(Bn[:, j, :], mm2_ps, b1b[:, :].unsqueeze(1).to_broadcast([P, GT, HID]), ALU.add)\
                 .then_inc(s_mm2s, 1)
            eng.wait_ge(s_srcc, 16)
            V.tensor_scalar(hilo_i[:, 0, :], srcs_i[:, :], 6, None, ALU.logical_shift_right)
            V.tensor_scalar(hilo_i[:, 1, :], srcs_i[:, :], 63, None, ALU.bitwise_and)
            V.memset(hist[:, :], 0.0)
            V.drain().then_inc(s_tab1, 1)
            V.tensor_copy(hilo[:, :, :], hilo_i[:, :, :])
            V.drain()

            with eng.Fori(0, T) as t:
                lo, hi = chunk_range(eng, t)
                hl = hilo[:, :, bass.ds(t * OHC, OHC)]
                for k in range(2):
                    V.tensor_tensor(oh[:, k, :, :], iota64[:, :].unsqueeze(1).to_broadcast([P, OHC, 64]),
                                    hl[:, k, :].unsqueeze(2).to_broadcast([P, OHC, 64]), ALU.is_equal)
                V.drain().then_inc(s_oh, 1)
                V.memset(macc[:, :], 0.0)
                Bt = Bn[:, bass.ds(t, 1), :].rearrange("p o c -> p (o c)")
                with eng.Fori(lo, hi) as c:
                    wait_reg(eng, s_rows, chunks * L0 + c + 1)
                    R = rows[:, bass.ds(c % 2, 1), :, :].rearrange("p o s c -> p (o s) c")
                    for q in range(2):
                        V.tensor_tensor(pre_s[:, q::2, :], R[:, q::2, 0:HID],
                                        Bt.unsqueeze(1).to_broadcast([P, CH // 2, HID]), ALU.add).then_inc(s_pre, 1)
                    V.tensor_copy(real[:, :], R[:, :, HID])
                    V.drain()
                    eng.wait_ge(s_at, c + 1).then_inc(s_free, 1)
                    for q in range(2):
                        eng.wait_ge(s_msg, c * 2 + q + 1)
                        V.tensor_tensor(msgs[:, q, :, :], msg_ps[q], b2b[:, :].unsqueeze(1).to_broadcast([P, CH // 2, D]),
                                        ALU.add)
                        V.drain()
                        V.scalar_tensor_tensor(msgs[:, q, :, :], msgs[:, q, :, :], 0.0,
                                               real[:, q::2].unsqueeze(2).to_broadcast([P, CH // 2, D]), ALU.max, ALU.mult)
                    V.drain()
                    V.tensor_reduce(msum[:, :], msgs[:, :, :, :].rearrange("p q k d -> p d (q k)"), AX.X, ALU.add)
                    V.drain()
                    V.tensor_tensor(macc[:, :], macc[:, :], msum[:, :], ALU.add)
                    V.drain()
                V.tensor_copy(cat[:, bass.ds(t, 1), D:2 * D].rearrange("p o d -> p (o d)"), macc[:, :])
                eng.wait_ge(s_hist, t + 1)
                V.tensor_tensor(hist[:, :], hist[:, :], hist_ps, ALU.add)
                V.drain()
            V.drain().then_inc(s_histo, 1)
            V.sem_inc(s_tab1, 1)
            for g in range(NG):
                j = slice(g * GT, (g + 1) * GT)
                eng.wait_ge(s_mm2, NG + g + 1)
                V.tensor_tensor(y[:, j, :], mm2_ps[:, :, 0:D], nb2b[:, :].unsqueeze(1).to_broadcast([P, GT, D]), ALU.add)\
                 .then_inc(s_mm2s, 1)
            V.drain()
            normed(3, y, y, False)
            V.tensor_tensor(y[:, :, :], y[:, :, :], lnSb[:, :].unsqueeze(1).to_broadcast([P, T, D]), ALU.mult)
            V.tensor_tensor(x[:, :, :], x[:, :, :], h[:, :, :], ALU.add)
            V.drain()
            V.tensor_tensor(y[:, :, :], y[:, :, :], lnOb[:, :].unsqueeze(1).to_broadcast([P, T, D]), ALU.add)
            V.drain()
            V.tensor_tensor(x[:, :, :], x[:, :, :], y[:, :, :], ALU.add)
            V.drain()

            normed(4, x, h, True)
            V.tensor_copy(tab[:, :, 0:D], h[:, :, :])
            V.tensor_scalar(stat[:, :], deg[:, :], 1.0, None, ALU.max)
            V.drain().then_inc(s_h, 1)
            V.sem_inc(s_tab2, 1)
            V.reciprocal(invd[:, :], stat[:, :])
            V.tensor_copy(iw[:, 0:D], ident[0:D, 0:D])
            V.tensor_tensor(x[:, :, :], x[:, :, :], bpb[:, :].unsqueeze(1).to_broadcast([P, T, D]), ALU.add)
            V.drain()

            def sum_pass(k):
                with eng.Fori(0, T) as t:
                    lo, hi = chunk_range(eng, t)
                    V.memset(macc[:, :], 0.0)
                    with eng.Fori(lo, hi) as c:
                        eng.wait_ge(s_rows, chunks * k + c + 1)
                        R = rows[:, bass.ds(c % 2, 1), :, :].rearrange("p o s c -> p (o s) c")
                        V.tensor_reduce(msum[:, :], R[:, :, 0:D].rearrange("p s d -> p d s"), AX.X, ALU.add)\
                         .then_inc(s_free, 1)
                        V.drain()
                        V.tensor_tensor(macc[:, :], macc[:, :], msum[:, :], ALU.add)
                        V.drain()
                    V.tensor_copy(agg[:, bass.ds(t, 1), :].rearrange("p o d -> p (o d)"), macc[:, :])
                    V.drain()

            with eng.Fori(0, L2) as layer:
                base = eng.snap(layer * NG)
                for k in range(2):
                    V.tensor_copy(wst[:, k, :], wT[:, bass.ds(layer + 3 * k, 1), :].rearrange("p o d -> p (o d)"))
                V.tensor_copy(iw[:, D:2 * D], wT[:, bass.ds(layer + 6, 1), :].rearrange("p o d -> p (o d)"))
                V.tensor_copy(bnst[:, 4:5], bnc[:, 0, bass.ds(layer, 1)])
                V.drain()
                sum_pass(layer + (L0 + 1))
                V.tensor_tensor(agg[:, :, :], agg[:, :, :], invd[:, :].unsqueeze(2).to_broadcast([P, T, D]), ALU.mult)
                V.drain().then_inc(s_stage, 1)
                eng.wait_ge(s_mms, base + 3 * NG)
                V.tensor_reduce(bnst[:, 0:1], yT[:, :, :].rearrange("p t n -> p (t n)"), AX.X, ALU.add)
                V.drain()
                V.tensor_scalar(bnst[:, 0:1], bnst[:, 0:1], 1.0 / N, None, ALU.mult)
                V.drain()
                V.tensor_scalar(yT[:, :, :], yT[:, :, :], bnst[:, 0:1], None, ALU.subtract)
                V.drain()
                V.tensor_tensor_reduce(out=wide[0:D, 0:N], in0=yT[:, :, :].rearrange("p t n -> p (t n)"),
                                       in1=yT[:, :, :].rearrange("p t n -> p (t n)"), scale=1.0, scalar=0.0,
                                       op0=ALU.mult, op1=ALU.add, accum_out=bnst[:, 3:4])
                V.drain()
                V.tensor_scalar(bnst[:, 1:2], bnst[:, 3:4], 1.0 / N, 1e-5, ALU.mult, ALU.add).then_inc(s_bn, 1)
                eng.wait_ge(s_bns, layer + 1)
                V.reciprocal(bnst[:, 7:8], bnst[:, 2:3])
                V.drain()
                V.tensor_tensor(bnst[:, 5:6], bnst[:, 7:8], bnc[:, 1, bass.ds(layer, 1)], ALU.mult)
                V.tensor_copy(bnst[:, 6:7], bnc[:, 2, bass.ds(layer, 1)])
                V.drain().then_inc(s_scale, 1)
                for g in range(NG):
                    j = slice(g * GT, (g + 1) * GT)
                    wait_reg(eng, s_mm2s, (base + g) * 2 + 2 * NG + 1)
                    V.tensor_tensor(x[:, j, :], x[:, j, :], mm2_ps[:, :, D:2 * D], ALU.add).then_inc(s_mm2s, 1)
                wait_reg(eng, s_mm2s, (base + NG) * 2 + 2 * NG)
                V.drain()
                with eng.If(layer < L2 - 1):
                    V.sem_inc(s_tab2, 1)

            normed(5, x, h, True)
            V.drain().then_inc(s_h, 1)
            for g in range(NG):
                j = slice(g * GT, (g + 1) * GT)
                eng.wait_ge(s_mm2, (2 + L2) * NG + g + 1)
                V.tensor_tensor(y[:, j, :], mm2_ps[:, :, 0:D], b3b[:, :].unsqueeze(1).to_broadcast([P, GT, D]), ALU.add)\
                 .then_inc(s_mm2s, 1)
            eng.wait_ge(s_deg, 16 * T)
            V.tensor_scalar(stat[:, :], odeg[:, :], 1.0, None, ALU.add).then_inc(s_var, 1)
            eng.wait_ge(s_std, 6)
            V.reciprocal(dinv[:, :], std[:, :])
            V.drain()
            V.tensor_tensor(tab[:, :, 0:D], y[:, :, :], dinv[:, :].unsqueeze(2).to_broadcast([P, T, D]), ALU.mult)
            V.tensor_scalar(stat[:, :], deg[:, :], 1.0, None, ALU.add)
            V.drain().then_inc(s_tab2, 1)
            V.reciprocal(rstd[:, :], stat[:, :])
            V.drain()
            V.tensor_tensor(rstd[:, :], rstd[:, :], dinv[:, :], ALU.mult)
            V.drain()
            sum_pass(L0 + 1 + L2)
            V.tensor_tensor(agg[:, :, :], agg[:, :, :], tab[:, :, 0:D], ALU.add)
            V.drain()
            V.tensor_tensor(agg[:, :, :], agg[:, :, :], rstd[:, :].unsqueeze(2).to_broadcast([P, T, D]), ALU.mult)
            V.drain()
            V.tensor_tensor(x[:, :, :], x[:, :, :], agg[:, :, :], ALU.add).then_inc(s_out, 1)


_INS = ['x', 'src', 'dst', 'edge_attr_64', 'L0_gnn_Ws', 'L0_gnn_attn_l', 'L0_gnn_attn_r', 'L0_gnn_gat_bias',
        'L0_gnn_h_bias', 'L1_gnn_msg_W1', 'L1_gnn_msg_b1', 'L1_gnn_msg_W2', 'L1_gnn_msg_b2', 'L1_gnn_node_W1',
        'L1_gnn_node_b1', 'L1_gnn_node_W2', 'L1_gnn_node_b2', 'L1_gnn_ln_scale', 'L1_gnn_ln_offset', 'L2_gnn_Wl',
        'L2_gnn_Wr', 'L2_gnn_b', 'L2_gnn_gamma', 'L2_gnn_beta', 'L2_gnn_Wp', 'L2_gnn_bp', 'L3_gnn_W', 'L3_gnn_b']


def kernel(**inputs):
    import concourse.bacc as _bacc
    from concourse.bass_utils import run_bass_kernel_spmd as _run

    nc = _bacc.Bacc("TRN2", target_bir_lowering=False, num_devices=1)
    arrays, args = {}, []
    for name in _INS:
        a = np.ascontiguousarray(inputs[name])
        arrays[f"in_{name}_dram"] = a
        args.append(nc.dram_tensor(f"in_{name}_dram", a.shape, mybir.dt.from_np(a.dtype), kind="ExternalInput").ap())
    args.append(nc.dram_tensor("out_0_dram", [N, D], f32, kind="ExternalOutput").ap())
    build(nc, *args)
    r = _run(nc, [arrays], core_ids=[0])
    return r.results[0]["out_0_dram"]
```

```python
from contextlib import ExitStack

import numpy as np

import concourse.bass as bass
from concourse import mybir
from concourse.alu_op_type import AluOpType as ALU

f32 = mybir.dt.float32
bf16 = mybir.dt.bfloat16
f16 = mybir.dt.float16
i32 = mybir.dt.int32
ACT = mybir.ActivationFunctionType
AX = mybir.AxisListType

N, E, D = 3125, 100000, 64
P = 125
T = N // P
GT = 5
NG = T // GT
ROWLEN = P
NROW = E // ROWLEN
HALF = NROW // 2
BLK = 4
NBLK = E // BLK
CH = 8
BPC = CH // BLK
HEADS = 4
L0, L2 = 4, 3
HID = 128
KEYCAP = 4095
KEYMUL = 4096
FAR = -1.0e30
MAXG = E // CH + (E // P) // CH + 3 * T + 2
AW = HEADS * (D + 1)
ROW0 = D + 1 + HEADS + 1
WIN = 784
WT, WP = 7, 112
ASL = 2
BANK = 512
EXACT = 2048
RING = 5
PASSES = L2 + 1


def build(nc, x_in, src_in, dst_in, attr_in, W0, al0, ar0, gb0, hb0, mW1, mb1, mW2, mb2, nW1, nb1,
          nW2, nb2, lnS, lnO, Wl2, Wr2, b2_, gam2, bet2, Wp2, bp2, W3, b3, out):
    ctx = ExitStack()
    with ctx:
        def sb(name, shape, dt=f32):
            return ctx.enter_context(nc.sbuf_tensor(name, shape, dt))

        def pb(name, shape):
            return ctx.enter_context(nc.psum_tensor(name, shape, f32))

        def sem(name):
            return ctx.enter_context(nc.semaphore(name))

        def dram(name, shape, dt=f32):
            return nc.dram_tensor(name, shape, dt, kind="Internal").ap()

        starts_d = dram("starts_d", [N + 1], i32)
        keys_d = dram("keys_d", [N])
        meta_d = dram("meta_d", [N, 4], i32)
        rec_d = dram("rec_d", [MAXG, P, CH + BPC], i32)
        tab0_d = dram("tab0_d", [N + 1, ROW0])
        tab1_d = dram("tab1_d", [N + 1, HID + 1])
        tab2_d = dram("tab2_d", [N + 1, D])
        hist_d = dram("hist_d", [64 * 64, 1])
        cnt_d = dram("cnt_d", [L0 * WIN, N], f16)
        invd_d = dram("invd_d", [N])

        ident = sb("ident", [128, 128])
        ones = sb("ones", [1, 128])
        tail_end = sb("tail_end", [1, 1], i32)
        nodeid = sb("nodeid", [P, T])
        nodeid_i = sb("nodeid_i", [P, T], i32)
        iota8 = sb("iota8", [P, CH])
        iota8_i = sb("iota8_i", [P, CH], i32)
        iota64 = sb("iota64", [P, 64], f16)
        iota64_i = sb("iota64_i", [P, 64], i32)
        step3 = sb("step3", [P, 3])
        padrow = sb("padrow", [1, HID + 1 + HEADS + 1])
        ident16 = sb("ident16", [128, 128], f16)
        zeros16 = sb("zeros16", [P, BANK], f16)
        dense_i = sb("dense_i", [1, 1], i32)

        arena = sb("arena", [128, 23620])
        at = {"first": 0, "sums": 0}

        def share(part, parts, shape, dt=f32):
            words = int(np.prod(shape)) if dt in (f32, i32) else (int(np.prod(shape)) + 1) // 2
            lo = at[part]
            at[part] = lo + words
            assert at[part] <= 23620, (part, at[part])
            v = arena[0:parts, lo:lo + words]
            v = v if dt == f32 else v.bitcast(dt)[:, 0:int(np.prod(shape))]
            names = ["a", "b", "c"][:len(shape)]
            if len(shape) > 1:
                v = v.rearrange(f"p ({' '.join(names)}) -> p {' '.join(names)}", **dict(zip(names, shape)))
            return v

        firsts_i = share("first", 1, [NROW], i32)
        firsts = share("first", 1, [NROW])
        firsts_b = share("first", P, [NROW])
        wide = share("first", P, [T * HID])
        kcount = sb("kcount", [P, T])
        krow = sb("krow", [P, T])
        krow_i = sb("krow_i", [P, T], i32)
        start_i = sb("start_i", [P, T], i32)
        end_i = sb("end_i", [P, T], i32)
        pf = [sb(f"pf{i}", [P, T]) for i in range(6)]
        pi = [sb(f"pi{i}", [P, T], i32) for i in range(4)]
        keys_b = sb("keys_b", [P, N])
        drows = keys_b[:, :].bitcast(i32).rearrange("p (t m) -> p t m", m=ROWLEN)
        rank_i = sb("rank_i", [P, T], i32)
        meta_o = sb("meta_o", [P, T, 4], i32)
        meta = sb("meta", [P, T, 4], i32)
        perm = sb("perm", [P, T], i32)
        nch_f = sb("nch_f", [P, T])
        tmax = sb("tmax", [P, T])
        cs_a = sb("cs_a", [1, T + 1])
        cs_b = sb("cs_b", [1, T + 1])
        cs_i = sb("cs_i", [1, T + 1], i32)
        edge_cur = sb("edge_cur", [P, T, 3])
        cur = sb("cur", [P, 3])
        blk_ix = sb("blk_ix", [P, 2, BPC], i32)
        raw_src = sb("raw_src", [P, 2, CH], i32)
        vmask = sb("vmask", [P, 2, CH])
        recs = sb("recs", [P, 2, CH + BPC], i32)
        deg = sb("deg", [P, T])
        dmax = sb("dmax", [P, 2])

        x = sb("x", [P, T, D])
        h = sb("h", [P, T, D])
        xc = sb("xc", [P, T, D])
        sq = sb("sq", [P, T, D])
        stat = sb("stat", [P, T])
        std = sb("std", [P, T])
        rstd = sb("rstd", [P, T])
        tab = sb("tab", [P, T, HID + 1])
        er = sb("er", [P, T, HEADS])
        tr5 = sb("tr5", [128, GT, P])

        idx = sb("idx", [P, 2, CH + BPC], i32)
        rows = sb("rows", [P, 2, CH, HID + 1])
        zz = sb("zz", [P, CH + 1, HEADS])
        pz = sb("pz", [P, CH + 1, HEADS])
        pe = sb("pe", [P, CH + 1, HEADS])
        mnew = sb("mnew", [P, HEADS])
        acc = sb("acc", [P, HEADS, D + 1])
        prod = share("first", P, [CH, HEADS, D + 1])
        rsave = sb("rsave", [P, HEADS])
        ids8 = sb("ids8", [P, CH])
        wofs = sb("wofs", [P, 1])
        iota_w_i = share("first", P, [WIN], i32)
        iota_w = share("first", P, [WIN], f16)
        onehot = share("first", P, [CH, WIN], f16)
        cb = share("first", P, [WIN], f16)
        ctT = share("first", WP, [WT, P], f16)
        rden = sb("rden", [P, HEADS])
        u = sb("u", [P, HEADS, D])
        uT = sb("uT", [128, 2, P])

        cat = share("first", P, [T, 2 * D])
        Bn = wide[:, :].rearrange("p (t c) -> p t c", t=T)
        attr = share("first", P, [2, CH, D])
        at_s = share("first", P, [CH, D])
        atT = share("first", 128, [CH // 2, P])
        pre_s = share("first", P, [CH, HID])
        real = sb("real", [P, CH])
        hidT = share("first", 128, [2, CH // 2, P])
        msgs = share("first", P, [2, CH // 2, D])
        msum = sb("msum", [P, D])
        macc = sb("macc", [P, D])
        zT5 = share("first", 128, [GT, P])
        y = sb("y", [P, T, D])
        srcs_i = share("first", P, [NROW], i32)
        hilo_i = share("first", P, [2, NROW], i32)
        hilo = sb("hilo", [P, 2, NROW], f16)
        OHC = NROW // T
        oh = onehot[:, :, :].rearrange("p s w -> p (s w)")[:, 0:2 * OHC * 64]\
            .rearrange("p (k c n) -> p k c n", k=2, c=OHC)
        hist = sb("hist", [64, 64])

        hTall = share("sums", D, [T, P])
        aggT = share("sums", 128, [N])
        invd_b = share("sums", 128, [N])
        hp12 = share("sums", P, [T, 2 * D], bf16)
        hp3 = share("sums", P, [T, 2 * D], bf16)
        cring = share("sums", P, [RING, N], f16)
        yT = keys_b[0:D, :].rearrange("p (t n) -> p t n", n=P)
        bnst = sb("bnst", [D, 8])
        wst = sb("wst", [128, 2, D])
        iw = sb("iw", [D, 2 * D])
        agg = sb("agg", [P, T, D])
        odeg = sb("odeg", [P, T])
        dinv = sb("dinv", [P, T])
        invd = sb("invd", [P, T])

        W1ab = sb("W1ab", [D, 2, HID])
        W1c = sb("W1c", [128, HID])
        W2s = sb("W2s", [HID, D])
        b1b = sb("b1b", [P, HID])
        b2b = sb("b2b", [P, D])
        nW1s = sb("nW1s", [128, HID])
        nW2s = sb("nW2s", [HID, D])
        nb1c = sb("nb1c", [HID, 1])
        nb2b = sb("nb2b", [P, D])
        lnSb = sb("lnSb", [P, D])
        lnOb = sb("lnOb", [P, D])
        wnat = sb("wnat", [D, 10, D])
        wT = sb("wT", [D, 10, D])
        bnc = sb("bnc", [D, 3, L2])
        bpb = sb("bpb", [P, D])
        b3b = sb("b3b", [P, D])
        W0s = sb("W0s", [128, L0, 2, D + 2 * HEADS])
        early = cat[0:D, :, :].rearrange("p t c -> p (t c)")
        alr = early[:, 0:2 * L0 * HEADS * D].rearrange("p (k l h d) -> p k l h d", k=2, l=L0, h=HEADS)
        W0k = early[:, 2 * L0 * HEADS * D:3 * L0 * HEADS * D].rearrange("p (l h d) -> p l h d", l=L0, h=HEADS)
        WL = sb("WL", [D, L0 + 1, 2 * HEADS])
        gbb = agg[:, :, :].rearrange("p t d -> p (t d)")[:, 0:L0 * HEADS * D]\
            .rearrange("p (l h d) -> p l h d", l=L0, h=HEADS)
        gbs = sb("gbs", [P, L0, D + 2 * HEADS])
        foldT = onehot.rearrange("p s w -> p (s w)")[0:D, 0:6 * L0 * 128].bitcast(f32).rearrange("p (k c) -> p k c", c=128)
        hbb = sb("hbb", [P, D])

        ps = pb("ps", [128, 8 * BANK])

        def bank(b, parts=128, n=1):
            return ps[0:parts, b * BANK:(b + n) * BANK]

        firsts_ps = bank(0, P, 2).rearrange("p (b c) -> p b c", b=2)[:, :, 0:HALF]
        acc_ps = bank(0, P)[:, 0:AW].rearrange("p (h d) -> p h d", h=HEADS)
        ctT_ps = bank(1, WP).bitcast(f16)[:, 0:WT * 128].rearrange("p (k c) -> p k c", k=WT)
        cnt_ps = bank(2, P, 2).rearrange("p (b c) -> p b c", b=2)[:, :, 0:WIN // 2]
        uT_ps = bank(4)[:, 0:256].rearrange("p (k c) -> p k c", k=2)[:, :, 0:P]
        hn_ps = bank(5, P)[:, 0:D + 2 * HEADS]
        foldT_ps = bank(4, D, 3).rearrange("p (k c) -> p k c", c=128)
        fold_ps = bank(7)[:, 0:3 * L0 * 2 * HEADS].rearrange("p (l k c) -> p l k c", l=L0, k=3)
        tr_ps = bank(0, 128, 2)[:, 0:GT * 128].rearrange("p (j c) -> p j c", j=GT)
        mmT_ps = bank(2, 128, 2)[:, 0:GT * 128].rearrange("p (j c) -> p j c", j=GT)
        mm_ps = mmT_ps[0:P]
        mm2_ps = bank(4, P, 2)[:, 0:GT * 128].rearrange("p (j c) -> p j c", j=GT)
        wT_ps = bank(0, D, 2)[:, 0:10 * D].rearrange("p (j c) -> p j c", j=10)
        atT_ps = bank(0)[:, 0:P * CH // 2].rearrange("p (k c) -> p k c", k=CH // 2)
        hid_ps = [bank(4 + q)[:, 0:P * CH // 2].rearrange("p (k c) -> p k c", k=CH // 2) for q in range(2)]
        msg_ps = [bank(6 + q, P)[:, 0:D * CH // 2].rearrange("p (k c) -> p k c", k=CH // 2) for q in range(2)]
        hist_ps = bank(2, 64)[:, 0:64]
        allT_ps = ps[:, 0:N]
        tiles_ps = ps[:, 0:T * 128].rearrange("p (t c) -> p t c", t=T)
        tiles64_ps = ps[0:P, 0:T * D].rearrange("p (t c) -> p t c", t=T)

        s_first = sem("firsts_loaded")
        s_const = sem("constants_made")
        s_firstf = sem("firsts_cast")
        s_firstp = sem("firsts_in_psum")
        s_krow = sem("row_numbers_made")
        s_drows = sem("receiver_rows_landed")
        s_start = sem("starts_made")
        s_startst = sem("starts_stored")
        s_end = sem("ends_loaded")
        s_key = sem("keys_made")
        s_keyst = sem("keys_stored")
        s_keyb = sem("keys_spread")
        s_rank = sem("ranks_made")
        s_metast = sem("meta_scattered")
        s_meta = sem("meta_loaded")
        s_nch = sem("node_chunks_made")
        s_tmax = sem("tile_chunks_made")
        s_cs = sem("chunk_starts_made")
        s_perm = sem("perm_made")
        s_bix = sem("block_index_made")
        s_raw = [sem(f"senders_landed{i}") for i in range(2)]
        s_rawrdy = sem("senders_ready")
        s_recm = sem("record_made")
        s_recst = [sem(f"record_stored{i}") for i in range(2)]
        s_recfree = sem("record_buffer_free")
        s_x = sem("x_gathered")
        s_w0 = sem("attention_weights_loaded")
        s_WL = sem("attention_vectors_folded")
        s_pad = sem("padding_rows_stored")
        s_var = sem("variance_made")
        s_std = sem("deviation_made")
        s_h = sem("normed_made")
        s_itr = sem("init_transposed")
        s_itrs = sem("init_transpose_copied")
        s_imm = sem("init_scores_made")
        s_tabr = sem("table_rows_made")
        s_tabst = sem("table_scattered")
        s_idx = [sem(f"index_loaded{i}") for i in range(2)]
        s_land = [sem(f"rows_landed{i}") for i in range(2)]
        s_rows = sem("rows_ready")
        s_free = sem("rows_free")
        s_z = sem("scores_ready")
        s_p = sem("probs_ready")
        s_u = sem("tile_sums_ready")
        s_uTp = sem("sums_transposed")
        s_uT = sem("sums_transpose_copied")
        s_hn = sem("new_rows_in_psum")
        s_foldTp = sem("fold_operands_transposed")
        s_foldT = sem("fold_transposes_copied")
        s_foldp = sem("folds_in_psum")
        s_fold = sem("folds_copied")
        s_tile = sem("tile_finished")
        s_gate = sem("gates_passed")
        s_w1 = sem("message_weights_loaded")
        s_w2 = sem("other_weights_loaded")
        s_wTp = sem("weights_transposed")
        s_wT = sem("weights_transpose_copied")
        s_tr = sem("group_transposed")
        s_trs = sem("group_transpose_copied")
        s_mm = sem("group_product_made")
        s_mms = sem("group_product_copied")
        s_mm2 = sem("group_second_product_made")
        s_mm2s = sem("group_second_product_used")
        s_bn = sem("features_centered")
        s_bns = sem("feature_deviation_made")
        s_scale = sem("feature_scale_made")
        s_hTall = sem("features_normed")
        s_stage = sem("layer_weights_staged")
        s_tab1 = sem("message_table_made")
        s_tab2 = sem("sum_tables_made")
        s_land1 = [sem(f"message_rows_landed{i}") for i in range(2)]
        s_at = sem("edge_features_staged")
        s_atTp = sem("edge_features_transposed")
        s_atT = sem("edge_transpose_copied")
        s_pre = sem("node_parts_staged")
        s_hidp = sem("hidden_made")
        s_hid = sem("hidden_rectified")
        s_msg = sem("messages_made")
        s_msgu = sem("messages_used")
        s_oh = sem("one_hots_made")
        s_hist = sem("counts_made")
        s_histo = sem("counts_summed")
        s_histst = sem("counts_stored")
        s_deg = sem("counts_gathered")
        s_srcc = sem("senders_loaded")
        s_out = sem("output_ready")
        s_own = sem("tile_begun")
        s_ones = sem("one_hots_of_chunk_made")
        s_prod = sem("weighted_rows_made")
        s_proda = sem("last_slots_weighted")
        s_accp = sem("weighted_rows_summed")
        s_cnt = sem("window_counted")
        s_cntu = sem("one_hots_used")
        s_cb = sem("counts_copied")
        s_ctTp = sem("window_counts_transposed")
        s_ctT = sem("window_transpose_copied")
        s_cntst = sem("window_counts_stored")
        s_dense = sem("count_bound_made")
        s_invd = sem("inverse_degrees_made")
        s_invst = sem("inverse_degrees_stored")
        s_invb = sem("inverse_degrees_spread")
        s_parts = sem("feature_parts_made")
        s_ring = [sem(f"counts_landed{i}") for i in range(RING)]
        s_ringf = sem("counts_tile_used")
        s_aggp = sem("sums_in_psum")
        s_aggT = sem("sums_copied")
        s_fstart = sem("features_ready_to_transpose")
        s_trall = sem("features_transposed_all")
        s_hTc = sem("features_transpose_kept")
        s_y = sem("layer_product_made")
        s_yc = sem("layer_product_kept")
        s_back = sem("features_back_by_node")
        s_backc = sem("new_table_rows_copied")
        s_xd = sem("layer_added_to_x")
        s_aggtr = sem("gathered_sums_transposed")
        s_outst = sem("output_stored")

        MAXC = MAXG - 1

        def wait_reg(eng, sem_, value):
            eng.wait_ge(sem_, value).then_inc(s_gate, 1)

        def is_dense(eng):
            return eng.value_load(dense_i[0:1, 0:1], min_val=0, max_val=1)

        def chunk_range(eng, t):
            lo = eng.value_load(cs_i[0:1, bass.ds(t, 1)], min_val=0, max_val=MAXC)
            hi = eng.value_load(cs_i[0:1, bass.ds(t + 1, 1)], min_val=1, max_val=MAXC)
            return lo, hi

        def chunk_count(eng):
            return eng.value_load(cs_i[0:1, T:T + 1], min_val=2, max_val=MAXC)

        block = ctx.enter_context(nc.Block())

        @block.sync
        def _(eng):
            with nc.allow_non_contiguous_dma("the receivers of every 125th edge, and node records"):
                eng.dma_start(firsts_i[:, :], dst_in.rearrange("(k m) -> m k", m=ROWLEN)[0:1, :])\
                   .then_inc(s_first, 16)
                for l in range(L0):
                    eng.dma_start(W0k[:, l, :, :], W0[l].rearrange("k (h d) -> k h d", h=HEADS)).then_inc(s_w0, 16)
                    for hh in range(2):
                        eng.dma_start(W0s[hh * D:(hh + 1) * D, l, :, 0:D],
                                      W0[l].rearrange("k (a b d) -> k b a d", a=2, b=2)[:, hh]).then_inc(s_w0, 16)
                eng.dma_start(alr[:, 0, :, :, :], al0.unsqueeze(0).to_broadcast([D, L0, HEADS, D])).then_inc(s_w0, 16)
                eng.dma_start(alr[:, 1, :, :, :], ar0.unsqueeze(0).to_broadcast([D, L0, HEADS, D])).then_inc(s_w0, 16)
                eng.dma_start(gbb[:, :, :, :], gb0.rearrange("l (h d) -> l h d", h=HEADS).unsqueeze(0)
                              .to_broadcast([P, L0, HEADS, D])).then_inc(s_w0, 16)
                eng.dma_start(hbb[:, :], hb0.unsqueeze(0).to_broadcast([P, D])).then_inc(s_w0, 16)
                eng.dma_start(W1ab[:, 0, :], mW1[0:D, :]).then_inc(s_w1, 16)
                eng.dma_start(W1ab[:, 1, :], mW1[D:2 * D, :]).then_inc(s_w1, 16)
                for k in range(2):
                    eng.dma_start(W1c[k * D:(k + 1) * D, :], mW1[2 * D:3 * D, :]).then_inc(s_w1, 16)
                eng.dma_start(W2s[:, :], mW2).then_inc(s_w1, 16)
                eng.dma_start(b1b[:, :], mb1.unsqueeze(0).to_broadcast([P, HID])).then_inc(s_w1, 16)
                eng.dma_start(b2b[:, :], mb2.unsqueeze(0).to_broadcast([P, D])).then_inc(s_w1, 16)
                eng.dma_start(nW1s[:, :], nW1).then_inc(s_w1, 16)
                eng.dma_start(nW2s[:, :], nW2).then_inc(s_w1, 16)
                eng.dma_start(nb1c[:, :], nb1.unsqueeze(1)).then_inc(s_w1, 16)
                eng.dma_start(nb2b[:, :], nb2.unsqueeze(0).to_broadcast([P, D])).then_inc(s_w1, 16)
                eng.dma_start(lnSb[:, :], lnS.unsqueeze(0).to_broadcast([P, D])).then_inc(s_w1, 16)
                eng.dma_start(lnOb[:, :], lnO.unsqueeze(0).to_broadcast([P, D])).then_inc(s_w1, 16)
                eng.dma_start(wnat[:, 0:3, :], Wl2.rearrange("l o k -> o l k")).then_inc(s_w2, 16)
                eng.dma_start(wnat[:, 3:6, :], Wr2.rearrange("l o k -> o l k")).then_inc(s_w2, 16)
                eng.dma_start(wnat[:, 6:9, :], Wp2.rearrange("o (l k) -> o l k", l=L2)).then_inc(s_w2, 16)
                eng.dma_start(wnat[:, 9, :], W3).then_inc(s_w2, 16)
                for k, v in enumerate((b2_, gam2, bet2)):
                    eng.dma_start(bnc[:, k, :], v.rearrange("l d -> d l")).then_inc(s_w2, 16)
                eng.dma_start(bpb[:, :], bp2.unsqueeze(0).to_broadcast([P, D])).then_inc(s_w2, 16)
                eng.dma_start(b3b[:, :], b3.unsqueeze(0).to_broadcast([P, D])).then_inc(s_w2, 16)
                eng.dma_start(srcs_i[:, :], src_in.rearrange("(p c) -> p c", p=P)).then_inc(s_srcc, 16)
                eng.wait_ge(s_start, 2)
                eng.dma_start(starts_d[0:N].rearrange("(p t) -> p t", t=T), start_i[:, :]).then_inc(s_startst, 16)
                eng.dma_start(starts_d[N:N + 1].unsqueeze(0), tail_end[:, :]).then_inc(s_startst, 16)
                eng.wait_ge(s_startst, 32)
                eng.dma_start(end_i[:, :], starts_d[1:N + 1].rearrange("(p t) -> p t", t=T)).then_inc(s_end, 16)
                eng.wait_ge(s_key, 1)
                eng.dma_start(keys_d.rearrange("(p t) -> p t", t=T), pf[5][:, :]).then_inc(s_keyst, 16)
                eng.wait_ge(s_keyst, 16)
                eng.dma_start(keys_b[:, :], keys_d.unsqueeze(0).to_broadcast([P, N])).then_inc(s_keyb, 16)
                eng.wait_ge(s_metast, 16 * T)
                eng.dma_start(meta[:, :, :], meta_d.rearrange("(t p) c -> p t c", p=P)).then_inc(s_meta, 16)
                eng.wait_ge(s_const, 1)
                eng.dma_start(tab0_d[N:N + 1, 0:D + 1], padrow[:, 0:D + 1]).then_inc(s_pad, 16)
                eng.dma_start(tab0_d[N:N + 1, D + 1:ROW0],
                              padrow[:, HID + 1:HID + 2 + HEADS]).then_inc(s_pad, 16)
                eng.dma_start(tab1_d[N:N + 1, :], padrow[:, 0:HID + 1]).then_inc(s_pad, 16)
                eng.dma_start(tab2_d[N:N + 1, :], padrow[:, 0:D]).then_inc(s_pad, 16)

                eng.wait_ge(s_cs, 1)
                pairs = chunk_count(eng) // 2
                with eng.Fori(0, pairs) as n:
                    for b in range(2):
                        eng.wait_ge(s_raw[b], (n + 1) * 16 * BPC).then_inc(s_rawrdy, 1)
                        eng.wait_ge(s_recm, n * 2 + b + 1)
                        eng.dma_start(rec_d[bass.ds(n * 2 + b, 1)].rearrange("o p c -> (o p) c"), recs[:, b, :])\
                           .then_inc(s_recst[b], 16)
                        eng.wait_ge(s_recst[b], (n + 1) * 16).then_inc(s_recfree, 1)

                def load_index(c, b):
                    eng.dma_start(idx[:, b, :], rec_d[bass.ds(c, 1)].rearrange("o p c -> (o p) c"))\
                       .then_inc(s_idx[b], 16)

                def relay_pass(k, landed, per_chunk):
                    with eng.Fori(0, pairs) as n:
                        following = eng.snap((n + 1) % pairs)
                        for b in range(2):
                            eng.wait_ge(landed[b], (k * pairs + n + 1) * 16 * per_chunk).then_inc(s_rows, 1)
                            load_index(following * 2 + b, b)

                for b in range(2):
                    load_index(b, b)

                with eng.Fori(0, L0) as layer:
                    relay_pass(layer, s_land, CH)
                relay_pass(0, s_land1, CH + BPC)
                eng.wait_ge(s_histo, 1)
                eng.dma_start(hist_d.rearrange("(a b) o -> a (b o)", b=64), hist[:, :]).then_inc(s_histst, 16)
                eng.wait_ge(s_invd, 1)
                eng.dma_start(invd_d.rearrange("(t p) -> p t", p=P), invd[:, :]).then_inc(s_invst, 16)
                eng.wait_ge(s_invst, 16)
                eng.dma_start(invd_b, invd_d.unsqueeze(0).to_broadcast([128, N])).then_inc(s_invb, 16)
                dense = is_dense(eng)
                with eng.If(dense == 0):
                    with eng.Fori(0, PASSES) as layer:
                        relay_pass(layer + L0, s_land, CH)
                    for b in range(2):
                        wait_reg(eng, s_idx[b], ((L0 + 1 + PASSES) * pairs + 1) * 16)
                for b in range(2):
                    wait_reg(eng, s_idx[b], ((L0 + 1) * pairs + 1) * 16)
                eng.wait_ge(s_outst, 16 * T)

        @block.gpsimd
        def _(eng):
            eng.memset(ident[:, :], 0.0)
            eng.memset(ones[:, :], 1.0)
            eng.memset(tail_end[:, :], E)
            eng.memset(padrow[:, 0:HID + 1], 0.0)
            eng.memset(padrow[:, HID + 1:HID + 1 + HEADS], FAR)
            eng.memset(padrow[:, HID + 1 + HEADS:HID + 2 + HEADS], -1.0)
            eng.memset(zeros16[:, :], 0.0)
            eng.iota(iota_w_i[:, :], pattern=[[1, WIN]], base=0, channel_multiplier=0)
            eng.memset(step3[:, 0:1], float(BPC))
            eng.memset(step3[:, 1:3], float(-CH))
            eng.iota(nodeid_i[:, :], pattern=[[1, T]], base=0, channel_multiplier=T)
            eng.iota(iota8_i[:, :], pattern=[[1, CH]], base=0, channel_multiplier=0)
            eng.iota(iota64_i[:, :], pattern=[[1, 64]], base=0, channel_multiplier=0)
            eng.drain()
            eng.affine_select(out=ident[:, :], in_=ident[:, :], compare_op=ALU.not_equal, fill=1.0,
                              base=0, pattern=[[-1, 128]], channel_multiplier=1)
            eng.drain()
            eng.tensor_copy(ident16[:, :], ident[:, :])
            eng.tensor_copy(iota_w[:, :], iota_w_i[:, :])
            eng.drain().then_inc(s_const, 1)

            eng.wait_ge(s_krow, 1)
            dst_rows = dst_in.rearrange("(k m) -> k m", m=ROWLEN)
            for t in range(T):
                eng.indirect_dma_start(out=drows[:, t, :], out_offset=None, in_=dst_rows,
                                       in_offset=bass.IndirectOffsetOnAxis(ap=krow_i[:, t:t + 1], axis=0))\
                   .then_inc(s_drows, 16)
            eng.wait_ge(s_rank, 1)
            for t in range(T):
                eng.indirect_dma_start(out=meta_d, out_offset=bass.IndirectOffsetOnAxis(ap=rank_i[:, t:t + 1], axis=0),
                                       in_=meta_o[:, t, :], in_offset=None).then_inc(s_metast, 16)
            eng.wait_ge(s_nch, 1)
            eng.partition_all_reduce(tmax[:, :], nch_f[:, :], P, bass.bass_isa.ReduceOp.max)
            eng.partition_all_reduce(dmax[:, 1:2], dmax[:, 0:1], P, bass.bass_isa.ReduceOp.max)
            eng.drain().then_inc(s_tmax, 1)
            eng.wait_ge(s_perm, 1)
            for t in range(T):
                eng.indirect_dma_start(out=x[:, t, :], out_offset=None, in_=x_in,
                                       in_offset=bass.IndirectOffsetOnAxis(ap=perm[:, t:t + 1], axis=0))\
                   .then_inc(s_x, 16)

            eng.wait_ge(s_cs, 1)
            pairs = chunk_count(eng) // 2
            src_blocks = src_in.rearrange("(k m) -> k m", m=BLK)
            with eng.Fori(0, pairs) as n:
                for b in range(2):
                    wait_reg(eng, s_bix, n * 2 + b + 1)
                    for j in range(BPC):
                        eng.indirect_dma_start(out=raw_src[:, b, j * BLK:(j + 1) * BLK], out_offset=None, in_=src_blocks,
                                               in_offset=bass.IndirectOffsetOnAxis(ap=blk_ix[:, b, j:j + 1], axis=0))\
                           .then_inc(s_raw[b], 16)

            def scatter_table(table, width, k):
                for t in range(T):
                    eng.indirect_dma_start(out=table, out_offset=bass.IndirectOffsetOnAxis(ap=perm[:, t:t + 1], axis=0),
                                           in_=tab[:, t, 0:width], in_offset=None).then_inc(s_tabst, 16)
                wait_reg(eng, s_tabst, (k + 1) * 16 * T)

            attr_blocks = attr_in.rearrange("(k m) d -> k (m d)", m=BLK)

            def gather_pass(k, table, width, landed, edges=False):
                with eng.Fori(0, pairs) as n:
                    for b in range(2):
                        eng.wait_ge(s_idx[b], (k * pairs + n + 1) * 16)
                        wait_reg(eng, s_free, (k * pairs + n) * 2 + b + 1)
                        for s in range(CH):
                            eng.indirect_dma_start(out=rows[:, b, s, 0:width], out_offset=None, in_=table,
                                                   in_offset=bass.IndirectOffsetOnAxis(ap=idx[:, b, s:s + 1], axis=0))\
                               .then_inc(landed[b], 16)
                        for j in range(BPC if edges else 0):
                            eng.indirect_dma_start(out=attr[:, b, j * BLK:(j + 1) * BLK, :].rearrange("p s d -> p (s d)"),
                                                   out_offset=None, in_=attr_blocks,
                                                   in_offset=bass.IndirectOffsetOnAxis(ap=idx[:, b, CH + j:CH + j + 1], axis=0))\
                               .then_inc(landed[b], 16)

            eng.wait_ge(s_pad, 64)
            with eng.Fori(0, L0) as layer:
                wait_reg(eng, s_tabr, (layer + 1) * T)
                scatter_table(tab0_d, ROW0, layer)
                gather_pass(layer, tab0_d, ROW0, s_land)
            eng.wait_ge(s_tab1, 2)
            scatter_table(tab1_d, HID + 1, L0)
            gather_pass(L0, tab1_d, HID + 1, s_land1, edges=True)
            eng.wait_ge(s_histst, 16)
            for t in range(T):
                eng.indirect_dma_start(out=odeg[:, t:t + 1], out_offset=None, in_=hist_d,
                                       in_offset=bass.IndirectOffsetOnAxis(ap=perm[:, t:t + 1], axis=0)).then_inc(s_deg, 16)
            dense = is_dense(eng)
            with eng.If(dense == 1):
                eng.wait_ge(s_cntst, 16 * (L0 * T + 1))
                eng.wait_ge(s_invd, 1)
                with eng.Fori(0, PASSES) as layer:
                    for t in range(T):
                        b = t % RING
                        wait_reg(eng, s_ringf, layer * T + (t + 1))
                        eng.indirect_dma_start(out=cring[:, b, :], out_offset=None, in_=cnt_d,
                                               in_offset=bass.IndirectOffsetOnAxis(ap=perm[:, t:t + 1], axis=0))\
                           .then_inc(s_ring[b], 16)
            with eng.If(dense == 0):
                with eng.Fori(0, PASSES) as layer:
                    wait_reg(eng, s_tab2, layer + 1)
                    scatter_table(tab2_d, D, layer + (L0 + 1))
                    gather_pass(layer + (L0 + 1), tab2_d, D, s_land)
            eng.wait_ge(s_out, 1)
            for t in range(T):
                eng.indirect_dma_start(out=out, out_offset=bass.IndirectOffsetOnAxis(ap=perm[:, t:t + 1], axis=0),
                                       in_=x[:, t, :], in_offset=None).then_inc(s_outst, 16)
            eng.wait_ge(s_outst, 16 * T)

        @block.scalar
        def _(eng):
            def deviations(k):
                eng.wait_ge(s_var, k)
                eng.activation(std[:, :], stat[:, :], ACT.Sqrt).then_inc(s_std, 1)

            deviations(1)
            for g in range(NG):
                j = slice(g * GT, (g + 1) * GT)
                eng.wait_ge(s_itr, g + 1)
                eng.activation(tr5[0:D, :, :], tr_ps[0:D, :, 0:P], ACT.Copy).then_inc(s_itrs, 1)
                eng.wait_ge(s_imm, g + 1)
                eng.activation(tab[:, j, D + 1:D + 1 + HEADS], mm_ps[:, :, 0:HEADS], ACT.Copy)
                eng.activation(er[:, j, :], mm_ps[:, :, HEADS:2 * HEADS], ACT.Copy)
                eng.drain().then_inc(s_tabr, GT)

            eng.wait_ge(s_foldTp, 1)
            for k in range(2):
                eng.activation(foldT[:, k::3, :], foldT_ps[:, k::3, :], ACT.Copy)
            eng.activation(foldT[:, 2::3, 0:P], foldT_ps[:, 2::3, 0:P], ACT.Copy).then_inc(s_foldT, 1)
            eng.wait_ge(s_foldp, 1)
            for k in range(2):
                eng.activation(W0s[:, :, k, D:], fold_ps[:, :, k, :], ACT.Copy)
            eng.activation(gbs[:, :, D:], fold_ps[0:P, :, 2, :], ACT.Copy)
            eng.drain().then_inc(s_fold, 1)

            def exp_chunk(layer, t, c):
                eng.wait_ge(s_z, layer * chunks + c + 1)
                eng.activation(pe[:, :, :], pz[:, :, :], ACT.Exp)
                eng.drain().then_inc(s_p, 1)
                eng.wait_ge(s_accp, c + (layer * chunks + layer * T + t + 1))
                for s in range(CH - ASL, CH):
                    for hh in range(HEADS):
                        last = eng.activation(prod[:, s, hh, :],
                                              rows[:, bass.ds(c % 2, 1), s, 0:D + 1].rearrange("p o c -> p (o c)"),
                                              ACT.Copy, scale=pe[:, s, hh:hh + 1])
                last.then_inc(s_proda, 1)

            def tile_rest(layer, t):
                done = layer * T + t + 1
                eng.wait_ge(s_hn, done)
                eng.activation(tab[:, bass.ds(t, 1), 0:D].rearrange("p o d -> p (o d)"), hn_ps[:, 0:D], ACT.Copy)
                eng.activation(tab[:, bass.ds(t, 1), D + 1:D + 1 + HEADS].rearrange("p o d -> p (o d)"),
                               hn_ps[:, D:D + HEADS], ACT.Copy)
                eng.activation(er[:, bass.ds(t, 1), :].rearrange("p o d -> p (o d)"),
                               hn_ps[:, D + HEADS:D + 2 * HEADS], ACT.Copy)
                eng.drain().then_inc(s_tabr, 1)
                eng.wait_ge(s_cntst, done * 16)
                eng.wait_ge(s_ctTp, done)
                eng.activation(ctT, ctT_ps[:, :, 0:P], ACT.Copy).then_inc(s_ctT, 1)
                eng.wait_ge(s_ctT, done)
                eng.dma_start(cnt_d[bass.ds(layer * WIN, WIN), bass.ds(t * P, P)].rearrange("(k p) i -> p k i", p=WP),
                              ctT).then_inc(s_cntst, 16)

            eng.wait_ge(s_cs, 1)
            chunks = chunk_count(eng)
            with eng.Fori(0, L0) as layer:
                with eng.Fori(0, T) as t:
                    lo, hi = chunk_range(eng, t)
                    done = layer * T + t + 1
                    exp_chunk(layer, t, lo)
                    with eng.If(t > 0):
                        tile_rest(layer, eng.snap((t + (T - 1)) % T))
                    with eng.Fori(lo + 1, hi) as c:
                        exp_chunk(layer, t, c)
                    eng.wait_ge(s_cnt, done)
                    eng.activation(cb.rearrange("p (b c) -> p b c", b=2), cnt_ps, ACT.Copy).then_inc(s_cb, 1)
                    eng.wait_ge(s_uTp, done)
                    eng.activation(uT[:, :, :], uT_ps, ACT.Copy).then_inc(s_uT, 1)
                tile_rest(layer, T - 1)

            eng.wait_ge(s_wTp, 1)
            eng.activation(wT[:, :, :], wT_ps, ACT.Copy).then_inc(s_wT, 1)

            deviations(2)
            for g in range(NG):
                j = slice(g * GT, (g + 1) * GT)
                eng.wait_ge(s_tr, g + 1)
                eng.activation(tr5[0:D, :, :], tr_ps[0:D, :, 0:P], ACT.Copy).then_inc(s_trs, 1)
                eng.wait_ge(s_mm, g + 1)
                eng.activation(tab[:, j, 0:HID], mm_ps, ACT.Copy).then_inc(s_mms, 1)
            eng.drain().then_inc(s_tab1, 1)
            with eng.Fori(0, T) as t:
                lo, hi = chunk_range(eng, t)
                with eng.Fori(lo, hi) as c:
                    eng.wait_ge(s_rows, chunks * L0 + c + 1)
                    eng.activation(at_s[:, :, :], attr[:, bass.ds(c % 2, 1), :, :].rearrange("p o s d -> p (o s) d"),
                                   ACT.Copy).then_inc(s_at, 1)
                    eng.wait_ge(s_atTp, c + 1)
                    eng.activation(atT[:, :, :], atT_ps, ACT.Copy).then_inc(s_atT, 1)
                    for q in range(2):
                        eng.wait_ge(s_hidp, c * 2 + q + 1)
                        eng.activation(hidT[:, q, :, :], hid_ps[q], ACT.Relu).then_inc(s_hid, 1)
            eng.wait_ge(s_w1, 16 * 13)
            for g in range(NG):
                eng.wait_ge(s_tr, NG + g + 1)
                eng.activation(tr5[:, :, :], tr_ps[:, :, 0:P], ACT.Copy).then_inc(s_trs, 1)
                eng.wait_ge(s_mm, NG + g + 1)
                eng.activation(zT5[:, :, :], mmT_ps[:, :, 0:P], ACT.Relu, bias=nb1c[:, 0:1]).then_inc(s_mms, 1)
            deviations(3)

            deviations(4)
            eng.wait_ge(s_trall, 1)
            eng.activation(hTall, tiles_ps[0:D, :, 0:P], ACT.Copy).then_inc(s_hTc, 1)
            dense = is_dense(eng)

            def gathered_sums(k):
                with eng.If(dense == 0):
                    eng.wait_ge(s_aggtr, k)
                    eng.activation(aggT[0:D, :].rearrange("p (t n) -> p t n", n=P), tiles_ps[0:D, :, 0:P], ACT.Copy)\
                       .then_inc(s_aggT, 1)

            with eng.Fori(0, L2) as layer:
                gathered_sums(layer + 1)
                eng.wait_ge(s_y, layer + 1)
                eng.activation(yT.rearrange("p t n -> p (t n)"), allT_ps[0:D, :], ACT.Identity, bias=bnst[:, 4:5])\
                   .then_inc(s_yc, 1)
                eng.wait_ge(s_bn, layer + 1)
                eng.activation(bnst[:, 2:3], bnst[:, 1:2], ACT.Sqrt).then_inc(s_bns, 1)
                eng.wait_ge(s_scale, layer + 1)
                eng.activation(hTall, yT, ACT.Relu, bias=bnst[:, 6:7], scale=bnst[:, 5:6]).then_inc(s_hTall, 1)
                eng.wait_ge(s_back, layer + 1)
                eng.activation(tab[:, :, 0:D], tiles_ps[0:P, :, 0:D], ACT.Copy).then_inc(s_backc, 1)

            deviations(5)
            eng.wait_ge(s_trall, 2)
            eng.activation(hTall, tiles_ps[0:D, :, 0:P], ACT.Copy).then_inc(s_hTc, 1)
            deviations(6)
            gathered_sums(PASSES)

        @block.tensor
        def _(eng):
            eng.wait_ge(s_firstf, 1)
            eng.wait_ge(s_const, 1)
            for b in range(2):
                last = eng.matmul(firsts_ps[:, b, :], ones[0:1, 0:P], firsts[0:1, b * HALF:(b + 1) * HALF],
                                  start=True, stop=True)
            last.then_inc(s_firstp, 1)

            eng.wait_ge(s_WL, 1)
            eng.wait_ge(s_h, 1)
            for g in range(NG):
                if g:
                    eng.wait_ge(s_tabr, g * GT)
                for j in range(GT):
                    last = eng.transpose(tr_ps[0:D, j, 0:P], h[:, g * GT + j, :], ident[0:P, 0:P])
                last.then_inc(s_itr, 1)
                eng.wait_ge(s_itrs, g + 1)
                for j in range(GT):
                    last = eng.matmul(mm_ps[:, j, 0:2 * HEADS], tr5[0:D, j, :], WL[:, 0, :], start=True, stop=True)
                last.then_inc(s_imm, 1)

            eng.wait_ge(s_cs, 1)
            chunks = chunk_count(eng)
            eng.wait_ge(s_tabr, T)
            eng.wait_ge(s_tabr, T)
            for l in range(L0):
                for k in range(2):
                    eng.transpose(foldT_ps[:, 3 * l + k, :], W0s[:, l, k, 0:D], ident[:, :])
                last = eng.transpose(foldT_ps[:, 3 * l + 2, 0:P], gbs[:, l, 0:D], ident[0:P, 0:P])
            last.then_inc(s_foldTp, 1)
            eng.wait_ge(s_foldT, 1)
            for l in range(L0):
                for k in range(2):
                    eng.matmul(fold_ps[:, l, k, :], foldT[:, 3 * l + k, :], WL[:, l + 1, :], start=True, stop=True)
                last = eng.matmul(fold_ps[0:P, l, 2, :], foldT[:, 3 * l + 2, 0:P], WL[:, l + 1, :], start=True, stop=True)
            last.then_inc(s_foldp, 1)
            eng.wait_ge(s_fold, 1)

            def sum_chunk(c):
                wait_reg(eng, s_prod, c + 1)
                for k in range(CH):
                    if k == CH - ASL:
                        wait_reg(eng, s_proda, c + 1)
                    last = eng.matmul(acc_ps, ident[0:P, 0:P], prod[:, k, :, :], start=(k == 0), stop=(k == CH - 1))
                last.then_inc(s_accp, 1)
                wait_reg(eng, s_ones, c + 1)
                for k in range(CH):
                    for b in range(2):
                        last = eng.matmul(cnt_ps[:, b, :], ident16[0:P, 0:P],
                                          onehot[:, k, b * (WIN // 2):(b + 1) * (WIN // 2)],
                                          start=False, stop=False, skip_group_check=True)
                last.then_inc(s_cntu, 1)

            def tile_rest(layer, t):
                done = layer * T + t + 1
                wait_reg(eng, s_uT, done)
                wl = W0s[:, bass.ds(layer, 1), :, :].rearrange("p o k d -> p (o k) d")
                eng.matmul(hn_ps, uT[:, 0, :], wl[:, 0, :], start=True, stop=False)
                eng.matmul(hn_ps, uT[:, 1, :], wl[:, 1, :], start=False, stop=False)
                eng.matmul(hn_ps, ident[0:P, 0:P], gbs[:, bass.ds(layer, 1), :].rearrange("p o d -> p (o d)"),
                           start=False, stop=True).then_inc(s_hn, 1)
                wait_reg(eng, s_cb, done + 1)
                for k in range(WT):
                    last = eng.transpose(ctT_ps[:, k, 0:P], cb[:, k * WP:(k + 1) * WP], ident16[0:P, 0:P])
                last.then_inc(s_ctTp, 1)

            with eng.Fori(0, L0) as layer:
                with eng.Fori(0, T) as t:
                    done = layer * T + t + 1
                    lo, hi = chunk_range(eng, t)
                    wait_reg(eng, s_own, done)
                    own = tab[:, bass.ds(t, 1), 0:D + 1].to_broadcast([P, HEADS, D + 1])
                    eng.matmul(acc_ps, ident[0:P, 0:P], own, start=True, stop=True).then_inc(s_accp, 1)
                    wait_reg(eng, s_cb, done)
                    for b in range(2):
                        eng.matmul(cnt_ps[:, b, :], ident16[0:P, 0:P], zeros16[:, 0:WIN // 2], start=True, stop=False,
                                   skip_group_check=True)
                    with eng.If(t > 0):
                        tile_rest(layer, eng.snap((t + (T - 1)) % T))
                    with eng.Fori(lo, hi) as c:
                        sum_chunk(layer * chunks + c)
                    for b in range(2):
                        last = eng.matmul(cnt_ps[:, b, :], ident16[0:P, 0:P], zeros16[:, 0:WIN // 2], start=False, stop=True,
                                          skip_group_check=True)
                    last.then_inc(s_cnt, 1)
                    wait_reg(eng, s_u, done)
                    for k in range(2):
                        last = eng.transpose(uT_ps[:, k, :], u[:, 2 * k:2 * k + 2, :].rearrange("p h d -> p (h d)"),
                                             ident[0:P, 0:P])
                    last.then_inc(s_uTp, 1)
                tile_rest(layer, T - 1)

            eng.wait_ge(s_w2, 16 * 9)
            eng.wait_ge(s_ctT, L0 * T)
            for k in range(10):
                last = eng.transpose(wT_ps[:, k, :], wnat[:, k, :], ident[0:D, 0:D])
            last.then_inc(s_wTp, 1)

            eng.wait_ge(s_w1, 16 * 13)
            eng.wait_ge(s_h, 2)
            for g in range(NG):
                if g == 0:
                    eng.wait_ge(s_wT, 1)
                for j in range(GT):
                    last = eng.transpose(tr_ps[0:D, j, 0:P], h[:, g * GT + j, :], ident[0:P, 0:P])
                last.then_inc(s_tr, 1)
                eng.wait_ge(s_trs, g + 1)
                if g:
                    eng.wait_ge(s_mms, g)
                for j in range(GT):
                    last = eng.matmul(mm_ps[:, j, :], tr5[0:D, j, :], W1ab[:, 0, :], start=True, stop=True)
                last.then_inc(s_mm, 1)
                if g:
                    eng.wait_ge(s_mm2s, g)
                for j in range(GT):
                    last = eng.matmul(mm2_ps[:, j, :], tr5[0:D, j, :], W1ab[:, 1, :], start=True, stop=True)
                last.then_inc(s_mm2, 1)
            eng.wait_ge(s_tab1, 2)
            with eng.Fori(0, T) as t:
                lo, hi = chunk_range(eng, t)
                wait_reg(eng, s_oh, t + 1)
                for k in range(OHC):
                    last = eng.matmul(hist_ps, oh[:, 0, k, :], oh[:, 1, k, :], start=(k == 0), stop=(k == OHC - 1))
                last.then_inc(s_hist, 1)
                with eng.Fori(lo, hi) as c:
                    wait_reg(eng, s_at, c + 1)
                    for k in range(CH // 2):
                        last = eng.transpose(atT_ps[:, k, :], at_s[:, 2 * k:2 * k + 2, :].rearrange("p s d -> p (s d)"),
                                             ident[0:P, 0:P])
                    last.then_inc(s_atTp, 1)
                    wait_reg(eng, s_atT, c + 1)
                    for q in range(2):
                        eng.matmul(hid_ps[q], W1c[q * D:(q + 1) * D, :], atT[q * D:(q + 1) * D, :, :],
                                   start=True, stop=False)
                        wait_reg(eng, s_pre, c * 2 + q + 1)
                        for k in range(CH // 2):
                            last = eng.matmul(hid_ps[q][:, k, :], pre_s[:, 2 * k + q, :], ident[0:P, 0:P],
                                              start=False, stop=(k == CH // 2 - 1))
                        last.then_inc(s_hidp, 1)
                    for q in range(2):
                        wait_reg(eng, s_hid, c * 2 + q + 1)
                        for k in range(CH // 2):
                            last = eng.matmul(msg_ps[q][:, k, :], hidT[:, q, k, :], W2s[:, :], start=True, stop=True)
                        last.then_inc(s_msg, 1)
            eng.wait_ge(s_tab1, 3)
            for g in range(NG):
                for j in range(GT):
                    last = eng.transpose(tr_ps[:, j, 0:P], cat[:, g * GT + j, :], ident[0:P, 0:P])
                last.then_inc(s_tr, 1)
                eng.wait_ge(s_trs, NG + g + 1)
                for j in range(GT):
                    last = eng.matmul(mmT_ps[:, j, 0:P], nW1s[:, :], tr5[:, j, :], start=True, stop=True)
                last.then_inc(s_mm, 1)
                eng.wait_ge(s_mms, NG + g + 1)
                if g:
                    eng.wait_ge(s_mm2s, NG + g)
                for j in range(GT):
                    last = eng.matmul(mm2_ps[:, j, 0:D], zT5[:, j, :], nW2s[:, :], start=True, stop=True)
                last.then_inc(s_mm2, 1)

            dense = is_dense(eng)

            def transpose_features(k):
                eng.wait_ge(s_h, 2 + k)
                for t in range(T):
                    last = eng.transpose(tiles_ps[0:D, t, 0:P], h[:, t, :], ident[0:P, 0:P])
                last.then_inc(s_trall, 1)
                eng.wait_ge(s_hTc, k)

            def sums(k):
                with eng.If(dense == 1):
                    wait_reg(eng, s_parts, k + 1)
                    for g in range(0, N, BANK):
                        w = min(BANK, N - g)
                        eng.matmul(allT_ps[:, g:g + w], hp12[:, 0, :], zeros16[:, 0:w], start=True, stop=False,
                                   skip_group_check=True)
                    with eng.Fori(0, T // RING) as r:
                        for b in range(RING):
                            wait_reg(eng, s_ring[b], (k * (T // RING) + r + 1) * 16)
                            for part in (hp12, hp3):
                                lhs = part[:, bass.ds(r * RING + b, 1), :].rearrange("p o c -> p (o c)")
                                for g in range(0, N, BANK):
                                    w = min(BANK, N - g)
                                    last = eng.matmul(allT_ps[:, g:g + w], lhs, cring[:, b, g:g + w], start=False,
                                                      stop=False, skip_group_check=True)
                            last.then_inc(s_ringf, 1)
                    for g in range(0, N, BANK):
                        w = min(BANK, N - g)
                        last = eng.matmul(allT_ps[:, g:g + w], hp12[:, 0, :], zeros16[:, 0:w], start=False, stop=True,
                                          skip_group_check=True)
                    last.then_inc(s_aggp, 1)
                with eng.If(dense == 0):
                    wait_reg(eng, s_parts, k + 1)
                    for t in range(T):
                        last = eng.transpose(tiles_ps[0:D, t, 0:P], agg[:, t, :], ident[0:P, 0:P])
                    last.then_inc(s_aggtr, 1)
                wait_reg(eng, s_aggT, k + 1)

            transpose_features(1)
            with eng.Fori(0, L2) as layer:
                sums(layer)
                for g in range(0, N, BANK):
                    w = min(BANK, N - g)
                    eng.matmul(allT_ps[0:D, g:g + w], wst[:, 0, :], aggT[:, g:g + w], start=True, stop=False)
                    last = eng.matmul(allT_ps[0:D, g:g + w], wst[0:D, 1, :],
                                      hTall.rearrange("p t n -> p (t n)")[:, g:g + w], start=False, stop=True)
                last.then_inc(s_y, 1)
                wait_reg(eng, s_hTall, layer + 1)
                for t in range(T):
                    last = eng.matmul(tiles_ps[0:P, t, :], hTall[:, t, :], iw[:, :], start=True, stop=True)
                last.then_inc(s_back, 1)
                wait_reg(eng, s_xd, layer + 1)

            transpose_features(2)
            for t in range(T):
                last = eng.matmul(tiles64_ps[:, t, :], hTall[:, t, :], wT[:, 9, :], start=True, stop=True)
            last.then_inc(s_y, 1)
            eng.wait_ge(s_xd, L2 + 1)
            sums(L2)
            for t in range(T):
                last = eng.matmul(tiles64_ps[:, t, :], aggT[:, t * P:(t + 1) * P], wst[:, 0, :], start=True, stop=True)
            last.then_inc(s_y, 1)

        @block.vector
        def _(eng):
            V = nc.vector

            eng.wait_ge(s_first, 16)
            V.tensor_copy(firsts[:, :], firsts_i[:, :]).then_inc(s_firstf, 1)
            eng.wait_ge(s_const, 1)
            V.tensor_copy(nodeid[:, :], nodeid_i[:, :])
            V.tensor_copy(iota8[:, :], iota8_i[:, :])
            V.tensor_copy(iota64[:, :], iota64_i[:, :])
            eng.wait_ge(s_firstp, 1)
            V.tensor_copy(firsts_b[:, :].rearrange("p (b c) -> p b c", b=2), firsts_ps)
            V.drain()
            for t in range(T):
                V.tensor_scalar(wide[:, 0:NROW], firsts_b[:, :], nodeid[:, t:t + 1], 0.0, ALU.is_lt, ALU.add,
                                accum_out=kcount[:, t:t + 1])
                V.drain()
            V.tensor_scalar(krow[:, :], kcount[:, :], -1.0, 0.0, ALU.add, ALU.max)
            V.drain()
            V.tensor_copy(krow_i[:, :], krow[:, :]).then_inc(s_krow, 1)
            eng.wait_ge(s_drows, 16 * T)
            for t in range(T):
                V.tensor_scalar(wide[:, 0:ROWLEN], drows[:, t, :], nodeid[:, t:t + 1], 0.0, ALU.is_lt, ALU.add,
                                accum_out=pf[0][:, t:t + 1])
                V.drain()
            V.scalar_tensor_tensor(pf[1][:, :], krow[:, :], float(ROWLEN), pf[0][:, :], ALU.mult, ALU.add)
            V.drain()
            V.tensor_copy(start_i[:, :], pf[1][:, :]).then_inc(s_start, 2)
            V.drain()
            V.tensor_scalar(pi[0][:, :], start_i[:, :], 2, None, ALU.logical_shift_right)
            V.drain()
            V.tensor_copy(pf[2][:, :], pi[0][:, :])
            eng.wait_ge(s_end, 16)
            V.tensor_copy(pf[3][:, :], end_i[:, :])
            V.drain()
            V.scalar_tensor_tensor(pf[4][:, :], pf[2][:, :], float(-BLK), pf[3][:, :], ALU.mult, ALU.add)
            V.drain()
            V.tensor_scalar(pi[1][:, :], pf[4][:, :], float(BLK - 1), None, ALU.add)
            V.drain()
            V.tensor_scalar(pi[2][:, :], pi[1][:, :], 2, None, ALU.logical_shift_right)
            V.drain()
            V.tensor_scalar(pf[0][:, :], pi[2][:, :], float(KEYCAP), float(KEYMUL), ALU.min, ALU.mult)
            V.tensor_scalar(pi[1][:, :], pi[2][:, :], 1.0, None, ALU.add)
            V.drain()
            V.tensor_tensor(pf[5][:, :], pf[0][:, :], nodeid[:, :], ALU.add).then_inc(s_key, 1)
            V.tensor_scalar(pi[3][:, :], pi[1][:, :], 1, None, ALU.logical_shift_right)
            V.drain()
            V.tensor_copy(meta_o[:, :, 0], nodeid_i[:, :])
            V.tensor_copy(meta_o[:, :, 1], start_i[:, :])
            V.tensor_copy(meta_o[:, :, 2], end_i[:, :])
            V.tensor_copy(meta_o[:, :, 3], pi[3][:, :])
            eng.wait_ge(s_keyb, 16)
            for t in range(T):
                V.tensor_scalar(wide[:, 0:N], keys_b[:, :], pf[5][:, t:t + 1], 0.0, ALU.is_gt, ALU.add,
                                accum_out=pf[0][:, t:t + 1])
                V.drain()
            V.tensor_copy(rank_i[:, :], pf[0][:, :])
            V.drain().then_inc(s_rank, 1)

            eng.wait_ge(s_meta, 16)
            V.tensor_copy(perm[:, :], meta[:, :, 0]).then_inc(s_perm, 1)
            V.tensor_copy(tab[:, :, ROW0 - 1], meta[:, :, 0])
            V.tensor_scalar(pi[0][:, :], meta[:, :, 1], 2, None, ALU.logical_shift_right)
            V.tensor_copy(pf[1][:, :], meta[:, :, 1])
            V.tensor_copy(pf[2][:, :], meta[:, :, 2])
            V.drain()
            V.tensor_copy(edge_cur[:, :, 0], pi[0][:, :])
            V.tensor_tensor(deg[:, :], pf[2][:, :], pf[1][:, :], ALU.subtract)
            V.drain()
            V.tensor_copy(nch_f[:, :], meta[:, :, 3])
            V.tensor_reduce(dmax[:, 0:1], deg[:, :], AX.X, ALU.max)
            V.drain().then_inc(s_nch, 1)
            V.scalar_tensor_tensor(edge_cur[:, :, 1], edge_cur[:, :, 0], float(-BLK), pf[1][:, :], ALU.mult, ALU.add)
            V.scalar_tensor_tensor(edge_cur[:, :, 2], edge_cur[:, :, 0], float(-BLK), pf[2][:, :], ALU.mult, ALU.add)
            V.memset(cs_a[:, 0:1], 0.0)
            V.memset(cs_b[:, 0:1], 0.0)
            eng.wait_ge(s_tmax, 1)
            V.tensor_scalar(cs_a[:, 1:T + 1], tmax[0:1, :], 1.0, None, ALU.max)
            V.tensor_scalar(dense_i[:, :], dmax[0:1, 1:2], float(EXACT), None, ALU.is_le)
            a, b = cs_a, cs_b
            d = 1
            while d < T + 1:
                V.drain()
                V.tensor_copy(b[:, 0:d], a[:, 0:d])
                V.tensor_tensor(b[:, d:T + 1], a[:, d:T + 1], a[:, 0:T + 1 - d], ALU.add)
                a, b = b, a
                d *= 2
            V.drain()
            V.tensor_copy(cs_i[:, :], a[:, :])
            V.drain()
            V.tensor_scalar(b[:, T:T + 1], a[:, T:T + 1], 1.0, None, ALU.add)
            V.drain()
            V.tensor_copy(pi[0][0:1, 0:1], b[:, T:T + 1])
            V.drain()
            V.tensor_scalar(cs_i[:, T:T + 1], pi[0][0:1, 0:1], 1, 1, ALU.logical_shift_right, ALU.logical_shift_left)
            V.drain().then_inc(s_cs, 1)

            chunks = chunk_count(eng)
            V.sem_inc(s_recfree, 2)
            with eng.Fori(0, T) as t:
                lo, hi = chunk_range(eng, t)
                V.tensor_copy(cur[:, :], edge_cur[:, bass.ds(t, 1), :].rearrange("p o c -> p (o c)"))
                with eng.Fori(lo, hi) as c:
                    bix = blk_ix[:, bass.ds(c % 2, 1), :].rearrange("p o c -> p (o c)")
                    raw = raw_src[:, bass.ds(c % 2, 1), :].rearrange("p o c -> p (o c)")
                    rec = recs[:, bass.ds(c % 2, 1), :].rearrange("p o c -> p (o c)")
                    V.drain()
                    V.tensor_scalar(bix, iota8[:, 0:BPC], cur[:, 0:1], float(NBLK - 1), ALU.add, ALU.min)\
                     .then_inc(s_bix, 1)
                    V.tensor_scalar(vmask[:, 0, :], iota8[:, :], cur[:, 1:2], None, ALU.is_ge)
                    V.drain()
                    V.scalar_tensor_tensor(vmask[:, 1, :], iota8[:, :], cur[:, 2:3], vmask[:, 0, :], ALU.is_lt, ALU.mult)
                    eng.wait_ge(s_recfree, c + 1)
                    wait_reg(eng, s_rawrdy, c + 1)
                    V.drain()
                    V.scalar_tensor_tensor(prod[:, 0, 0, 0:CH], raw, float(-N), vmask[:, 1, :], ALU.add, ALU.mult)
                    V.tensor_tensor(cur[:, :], cur[:, :], step3[:, :], ALU.add)
                    V.tensor_copy(rec[:, CH:CH + BPC], bix)
                    V.drain()
                    V.tensor_scalar(rec[:, 0:CH], prod[:, 0, 0, 0:CH], float(N), None, ALU.add)
                    V.drain().then_inc(s_recm, 1)

            eng.wait_ge(s_w0, 16 * (3 * L0 + 4))
            V.memset(WL[:, :, :], 0.0)
            V.drain()
            for k in range(2):
                for l in range(L0):
                    V.tensor_tensor(sq[0:D, 0:HEADS, :], W0k[:, l, :, :], alr[:, k, l, :, :], ALU.mult)
                    V.drain()
                    V.tensor_reduce(WL[:, l, k * HEADS:(k + 1) * HEADS], sq[0:D, 0:HEADS, :], AX.X, ALU.add)
                    V.drain()
            V.tensor_reduce(gbs[:, :, 0:D], gbb[:, :, :, :].rearrange("p l h d -> p l d h"), AX.X, ALU.add)
            V.drain().then_inc(s_WL, 1)

            def normed(k, inp, outp, relu):
                V.tensor_reduce(stat[:, :], inp[:, :, :], AX.X, ALU.add)
                V.drain()
                V.tensor_scalar(stat[:, :], stat[:, :], 1.0 / D, None, ALU.mult)
                V.drain()
                V.tensor_tensor(xc[:, :, :], inp[:, :, :], stat[:, :].unsqueeze(2).to_broadcast([P, T, D]), ALU.subtract)
                V.drain()
                V.tensor_tensor(sq[:, :, :], xc[:, :, :], xc[:, :, :], ALU.mult)
                V.drain()
                V.tensor_reduce(stat[:, :], sq[:, :, :], AX.X, ALU.add)
                V.drain()
                V.tensor_scalar(stat[:, :], stat[:, :], 1.0 / D, 1e-5, ALU.mult, ALU.add).then_inc(s_var, 1)
                eng.wait_ge(s_std, k)
                V.reciprocal(rstd[:, :], std[:, :])
                V.drain()
                V.tensor_tensor(sq[:, :, :], xc[:, :, :], rstd[:, :].unsqueeze(2).to_broadcast([P, T, D]), ALU.mult)
                V.drain()
                if relu:
                    V.tensor_scalar(outp[:, :, :], sq[:, :, :], 0.0, None, ALU.max)
                else:
                    V.tensor_copy(outp[:, :, :], sq[:, :, :])
                V.drain()

            eng.wait_ge(s_x, 16 * T)
            normed(1, x, h, True)
            V.tensor_copy(tab[:, :, 0:D], h[:, :, :])
            V.memset(tab[:, :, D:D + 1], 1.0)
            V.memset(wofs[:, :], 0.0)
            V.drain().then_inc(s_h, 1)
            V.sem_inc(s_free, 2)
            V.sem_inc(s_cntu, 1)
            V.sem_inc(s_cb, 1)
            V.sem_inc(s_cntst, 16)

            with eng.Fori(0, L0) as layer:
                wait_reg(eng, s_tabr, (layer + 1) * T)
                with eng.Fori(0, T) as t:
                    lo, hi = chunk_range(eng, t)
                    own = tab[:, bass.ds(t, 1), :].rearrange("p o c -> p (o c)")
                    er_t = er[:, bass.ds(t, 1), :].rearrange("p o c -> p (o c)")
                    V.drain()
                    V.tensor_tensor(mnew[:, :], own[:, D + 1:D + 1 + HEADS], er_t, ALU.add)
                    V.memset(acc[:, :, :], 0.0)
                    V.memset(rsave[:, :], 0.0)
                    V.drain().then_inc(s_own, 1)
                    V.scalar_tensor_tensor(zz[:, CH, :], mnew[:, :], 0.2, mnew[:, :], ALU.mult, ALU.max)
                    V.drain()
                    with eng.Fori(lo, hi) as c:
                        eng.wait_ge(s_rows, layer * chunks + c + 1)
                        R = rows[:, bass.ds(c % 2, 1), :, :].rearrange("p o s c -> p (o s) c")
                        V.tensor_tensor(zz[:, 0:CH, :], R[:, :, D + 1:D + 1 + HEADS],
                                        er_t.unsqueeze(1).to_broadcast([P, CH, HEADS]), ALU.add)
                        V.drain()
                        V.tensor_tensor(acc[:, :, :], acc[:, :, :],
                                        rsave[:, :].unsqueeze(2).to_broadcast([P, HEADS, D + 1]), ALU.mult)
                        V.tensor_scalar(ids8[:, :], R[:, :, ROW0 - 1], wofs[:, 0:1], None, ALU.add)
                        V.scalar_tensor_tensor(zz[:, 0:CH, :], zz[:, 0:CH, :], 0.2, zz[:, 0:CH, :], ALU.mult, ALU.max)
                        V.drain()
                        V.tensor_reduce(mnew[:, :], zz[:, :, :].rearrange("p s h -> p h s"), AX.X, ALU.max)
                        V.drain()
                        V.tensor_tensor(pz[:, :, :], zz[:, :, :], mnew[:, :].unsqueeze(1).to_broadcast([P, CH + 1, HEADS]),
                                        ALU.subtract).then_inc(s_z, 1)
                        eng.wait_ge(s_accp, c + (layer * chunks + layer * T + t + 1))
                        V.tensor_tensor(acc[:, :, :], acc[:, :, :], acc_ps, ALU.add)
                        eng.wait_ge(s_p, layer * chunks + c + 1)
                        V.tensor_copy(rsave[:, :], pe[:, CH, :])
                        V.tensor_copy(zz[:, CH, :], mnew[:, :])
                        V.tensor_tensor(prod[:, 0:CH - ASL],
                                        R[:, 0:CH - ASL, 0:D + 1].unsqueeze(2).to_broadcast([P, CH - ASL, HEADS, D + 1]),
                                        pe[:, 0:CH - ASL, :].unsqueeze(3).to_broadcast([P, CH - ASL, HEADS, D + 1]), ALU.mult)\
                         .then_inc(s_prod, 1)
                        eng.wait_ge(s_cntu, c + (layer * chunks + 1))
                        for k in range(CH):
                            if k == 2:
                                eng.wait_ge(s_proda, layer * chunks + c + 1)
                            last = V.tensor_scalar(onehot[:, k, :], iota_w, ids8[:, k:k + 1], None, ALU.is_equal)
                            if k == 2:
                                last.then_inc(s_free, 1)
                        last.then_inc(s_ones, 1)
                    V.drain()
                    V.tensor_tensor(acc[:, :, :], acc[:, :, :],
                                    rsave[:, :].unsqueeze(2).to_broadcast([P, HEADS, D + 1]), ALU.mult)
                    V.drain()
                    eng.wait_ge(s_accp, hi + (layer * chunks + layer * T + t + 1))
                    V.tensor_tensor(acc[:, :, :], acc[:, :, :], acc_ps, ALU.add)
                    V.drain()
                    V.reciprocal(rden[:, :], acc[:, :, D])
                    V.drain()
                    V.tensor_tensor(u[:, :, :], acc[:, :, 0:D], rden[:, :].unsqueeze(2).to_broadcast([P, HEADS, D]),
                                    ALU.mult).then_inc(s_u, 1)
                V.tensor_scalar(wofs[:, :], wofs[:, :], float(-WIN), None, ALU.add)
                V.drain()
            eng.wait_ge(s_tabr, (L0 + 1) * T)
            V.tensor_tensor(x[:, :, :], x[:, :, :], tab[:, :, 0:D], ALU.add)
            V.drain()
            V.tensor_tensor(x[:, :, :], x[:, :, :], hbb[:, :].unsqueeze(1).to_broadcast([P, T, D]), ALU.add)
            V.drain()

            normed(2, x, h, True)
            V.tensor_copy(cat[:, :, 0:D], h[:, :, :])
            V.memset(tab[:, :, HID:HID + 1], 1.0)
            V.drain().then_inc(s_h, 1)
            eng.wait_ge(s_w1, 16 * 13)
            for g in range(NG):
                j = slice(g * GT, (g + 1) * GT)
                eng.wait_ge(s_mm2, g + 1)
                V.tensor_tensor(Bn[:, j, :], mm2_ps, b1b[:, :].unsqueeze(1).to_broadcast([P, GT, HID]), ALU.add)\
                 .then_inc(s_mm2s, 1)
            eng.wait_ge(s_srcc, 16)
            V.tensor_scalar(hilo_i[:, 0, :], srcs_i[:, :], 6, None, ALU.logical_shift_right)
            V.tensor_scalar(hilo_i[:, 1, :], srcs_i[:, :], 63, None, ALU.bitwise_and)
            V.memset(hist[:, :], 0.0)
            V.drain().then_inc(s_tab1, 1)
            V.tensor_copy(hilo[:, :, :], hilo_i[:, :, :])
            V.drain()

            with eng.Fori(0, T) as t:
                lo, hi = chunk_range(eng, t)
                hl = hilo[:, :, bass.ds(t * OHC, OHC)]
                for k in range(2):
                    V.tensor_tensor(oh[:, k, :, :], iota64[:, :].unsqueeze(1).to_broadcast([P, OHC, 64]),
                                    hl[:, k, :].unsqueeze(2).to_broadcast([P, OHC, 64]), ALU.is_equal)
                V.drain().then_inc(s_oh, 1)
                V.memset(macc[:, :], 0.0)
                Bt = Bn[:, bass.ds(t, 1), :].rearrange("p o c -> p (o c)")
                with eng.Fori(lo, hi) as c:
                    wait_reg(eng, s_rows, chunks * L0 + c + 1)
                    R = rows[:, bass.ds(c % 2, 1), :, :].rearrange("p o s c -> p (o s) c")
                    for q in range(2):
                        V.tensor_tensor(pre_s[:, q::2, :], R[:, q::2, 0:HID],
                                        Bt.unsqueeze(1).to_broadcast([P, CH // 2, HID]), ALU.add).then_inc(s_pre, 1)
                    V.tensor_copy(real[:, :], R[:, :, HID])
                    V.drain()
                    eng.wait_ge(s_at, c + 1).then_inc(s_free, 1)
                    for q in range(2):
                        eng.wait_ge(s_msg, c * 2 + q + 1)
                        V.tensor_tensor(msgs[:, q, :, :], msg_ps[q], b2b[:, :].unsqueeze(1).to_broadcast([P, CH // 2, D]),
                                        ALU.add)
                        V.drain()
                        V.scalar_tensor_tensor(msgs[:, q, :, :], msgs[:, q, :, :], 0.0,
                                               real[:, q::2].unsqueeze(2).to_broadcast([P, CH // 2, D]), ALU.max, ALU.mult)
                    V.drain()
                    V.tensor_reduce(msum[:, :], msgs[:, :, :, :].rearrange("p q k d -> p d (q k)"), AX.X, ALU.add)
                    V.drain()
                    V.tensor_tensor(macc[:, :], macc[:, :], msum[:, :], ALU.add)
                    V.drain()
                V.tensor_copy(cat[:, bass.ds(t, 1), D:2 * D].rearrange("p o d -> p (o d)"), macc[:, :])
                eng.wait_ge(s_hist, t + 1)
                V.tensor_tensor(hist[:, :], hist[:, :], hist_ps, ALU.add)
                V.drain()
            V.drain().then_inc(s_histo, 1)
            V.sem_inc(s_tab1, 1)
            for g in range(NG):
                j = slice(g * GT, (g + 1) * GT)
                eng.wait_ge(s_mm2, NG + g + 1)
                V.tensor_tensor(y[:, j, :], mm2_ps[:, :, 0:D], nb2b[:, :].unsqueeze(1).to_broadcast([P, GT, D]), ALU.add)\
                 .then_inc(s_mm2s, 1)
            V.drain()
            normed(3, y, y, False)
            V.tensor_tensor(y[:, :, :], y[:, :, :], lnSb[:, :].unsqueeze(1).to_broadcast([P, T, D]), ALU.mult)
            V.tensor_tensor(x[:, :, :], x[:, :, :], h[:, :, :], ALU.add)
            V.drain()
            V.tensor_tensor(y[:, :, :], y[:, :, :], lnOb[:, :].unsqueeze(1).to_broadcast([P, T, D]), ALU.add)
            V.drain()
            V.tensor_tensor(x[:, :, :], x[:, :, :], y[:, :, :], ALU.add)
            V.drain()

            eng.wait_ge(s_cntst, 16 * (L0 * T + 1))
            normed(4, x, h, True)
            V.tensor_copy(tab[:, :, 0:D], h[:, :, :])
            V.tensor_scalar(stat[:, :], deg[:, :], 1.0, None, ALU.max)
            V.drain().then_inc(s_h, 1)
            V.sem_inc(s_tab2, 1)
            V.reciprocal(invd[:, :], stat[:, :]).then_inc(s_invd, 1)
            V.tensor_copy(iw[:, 0:D], ident[0:D, 0:D])
            V.memset(hp3, 0.0)
            V.tensor_tensor(x[:, :, :], x[:, :, :], bpb[:, :].unsqueeze(1).to_broadcast([P, T, D]), ALU.add)
            V.drain()

            def sum_pass(k):
                with eng.Fori(0, T) as t:
                    lo, hi = chunk_range(eng, t)
                    V.memset(macc[:, :], 0.0)
                    with eng.Fori(lo, hi) as c:
                        eng.wait_ge(s_rows, chunks * k + c + 1)
                        R = rows[:, bass.ds(c % 2, 1), :, :].rearrange("p o s c -> p (o s) c")
                        V.tensor_reduce(msum[:, :], R[:, :, 0:D].rearrange("p s d -> p d s"), AX.X, ALU.add)\
                         .then_inc(s_free, 1)
                        V.drain()
                        V.tensor_tensor(macc[:, :], macc[:, :], msum[:, :], ALU.add)
                        V.drain()
                    V.tensor_copy(agg[:, bass.ds(t, 1), :].rearrange("p o d -> p (o d)"), macc[:, :])
                    V.drain()

            dense = is_dense(eng)
            V.sem_inc(s_ringf, RING)

            def sums(k, scaled):
                with eng.If(dense == 1):
                    V.tensor_copy(hp12[:, :, 0:D], tab[:, :, 0:D])
                    V.drain()
                    V.tensor_tensor(xc[:, :, :], tab[:, :, 0:D], hp12[:, :, 0:D], ALU.subtract)
                    V.drain()
                    V.tensor_copy(hp12[:, :, D:2 * D], xc[:, :, :])
                    V.drain()
                    V.tensor_tensor(hp3[:, :, D:2 * D], xc[:, :, :], hp12[:, :, D:2 * D], ALU.subtract)
                    V.drain().then_inc(s_parts, 1)
                    eng.wait_ge(s_aggp, k + 1)
                    if scaled:
                        V.tensor_tensor(aggT, allT_ps, invd_b, ALU.mult).then_inc(s_aggT, 1)
                    else:
                        V.tensor_copy(aggT, allT_ps).then_inc(s_aggT, 1)
                with eng.If(dense == 0):
                    V.memset(aggT[D:2 * D, :], 0.0)
                    sum_pass(k + (L0 + 1))
                    if scaled:
                        V.tensor_tensor(agg[:, :, :], agg[:, :, :], invd[:, :].unsqueeze(2).to_broadcast([P, T, D]),
                                        ALU.mult)
                    V.drain().then_inc(s_parts, 1)

            eng.wait_ge(s_invb, 16)
            with eng.Fori(0, L2) as layer:
                for k in range(2):
                    V.tensor_copy(wst[k * D:(k + 1) * D, 0, :], wT[:, bass.ds(layer, 1), :].rearrange("p o d -> p (o d)"))
                V.tensor_copy(wst[0:D, 1, :], wT[:, bass.ds(layer + 3, 1), :].rearrange("p o d -> p (o d)"))
                V.tensor_copy(iw[:, D:2 * D], wT[:, bass.ds(layer + 6, 1), :].rearrange("p o d -> p (o d)"))
                V.tensor_copy(bnst[:, 4:5], bnc[:, 0, bass.ds(layer, 1)])
                V.drain()
                sums(layer, True)
                eng.wait_ge(s_yc, layer + 1)
                V.tensor_reduce(bnst[:, 0:1], yT[:, :, :].rearrange("p t n -> p (t n)"), AX.X, ALU.add)
                V.drain()
                V.tensor_scalar(bnst[:, 0:1], bnst[:, 0:1], 1.0 / N, None, ALU.mult)
                V.drain()
                V.tensor_scalar(yT[:, :, :], yT[:, :, :], bnst[:, 0:1], None, ALU.subtract)
                V.drain()
                V.tensor_tensor_reduce(out=aggT[0:D, :], in0=yT[:, :, :].rearrange("p t n -> p (t n)"),
                                       in1=yT[:, :, :].rearrange("p t n -> p (t n)"), scale=1.0, scalar=0.0,
                                       op0=ALU.mult, op1=ALU.add, accum_out=bnst[:, 3:4])
                V.drain()
                V.tensor_scalar(bnst[:, 1:2], bnst[:, 3:4], 1.0 / N, 1e-5, ALU.mult, ALU.add).then_inc(s_bn, 1)
                eng.wait_ge(s_bns, layer + 1)
                V.reciprocal(bnst[:, 7:8], bnst[:, 2:3])
                V.drain()
                V.tensor_tensor(bnst[:, 5:6], bnst[:, 7:8], bnc[:, 1, bass.ds(layer, 1)], ALU.mult)
                V.tensor_copy(bnst[:, 6:7], bnc[:, 2, bass.ds(layer, 1)])
                V.drain().then_inc(s_scale, 1)
                eng.wait_ge(s_backc, layer + 1)
                V.tensor_tensor(x[:, :, :], x[:, :, :], tiles_ps[0:P, :, D:2 * D], ALU.add).then_inc(s_xd, 1)
                V.drain()
                with eng.If(layer < L2 - 1):
                    V.sem_inc(s_tab2, 1)

            normed(5, x, h, True)
            for k in range(2):
                V.tensor_copy(wst[k * D:(k + 1) * D, 0, :], ident[0:D, 0:D])
            V.drain().then_inc(s_h, 1)
            eng.wait_ge(s_y, L2 + 1)
            V.tensor_tensor(y[:, :, :], tiles64_ps, b3b[:, :].unsqueeze(1).to_broadcast([P, T, D]), ALU.add)\
             .then_inc(s_xd, 1)
            eng.wait_ge(s_deg, 16 * T)
            V.tensor_scalar(stat[:, :], odeg[:, :], 1.0, None, ALU.add).then_inc(s_var, 1)
            eng.wait_ge(s_std, 6)
            V.reciprocal(dinv[:, :], std[:, :])
            V.drain()
            V.tensor_tensor(tab[:, :, 0:D], y[:, :, :], dinv[:, :].unsqueeze(2).to_broadcast([P, T, D]), ALU.mult)
            V.tensor_scalar(stat[:, :], deg[:, :], 1.0, None, ALU.add)
            V.drain().then_inc(s_tab2, 1)
            V.reciprocal(rstd[:, :], stat[:, :])
            V.drain()
            V.tensor_tensor(rstd[:, :], rstd[:, :], dinv[:, :], ALU.mult)
            V.drain()
            sums(L2, False)
            eng.wait_ge(s_y, L2 + 2)
            V.tensor_tensor(y[:, :, :], tab[:, :, 0:D], tiles64_ps, ALU.add)
            V.drain()
            V.tensor_tensor(y[:, :, :], y[:, :, :], rstd[:, :].unsqueeze(2).to_broadcast([P, T, D]), ALU.mult)
            V.drain()
            V.tensor_tensor(x[:, :, :], x[:, :, :], y[:, :, :], ALU.add).then_inc(s_out, 1)


_INS = ['x', 'src', 'dst', 'edge_attr_64', 'L0_gnn_Ws', 'L0_gnn_attn_l', 'L0_gnn_attn_r', 'L0_gnn_gat_bias',
        'L0_gnn_h_bias', 'L1_gnn_msg_W1', 'L1_gnn_msg_b1', 'L1_gnn_msg_W2', 'L1_gnn_msg_b2', 'L1_gnn_node_W1',
        'L1_gnn_node_b1', 'L1_gnn_node_W2', 'L1_gnn_node_b2', 'L1_gnn_ln_scale', 'L1_gnn_ln_offset', 'L2_gnn_Wl',
        'L2_gnn_Wr', 'L2_gnn_b', 'L2_gnn_gamma', 'L2_gnn_beta', 'L2_gnn_Wp', 'L2_gnn_bp', 'L3_gnn_W', 'L3_gnn_b']


def kernel(**inputs):
    import concourse.bacc as _bacc
    from concourse.bass_utils import run_bass_kernel_spmd as _run

    nc = _bacc.Bacc("TRN2", target_bir_lowering=False, num_devices=1)
    arrays, args = {}, []
    for name in _INS:
        a = np.ascontiguousarray(inputs[name])
        arrays[f"in_{name}_dram"] = a
        args.append(nc.dram_tensor(f"in_{name}_dram", a.shape, mybir.dt.from_np(a.dtype), kind="ExternalInput").ap())
    args.append(nc.dram_tensor("out_0_dram", [N, D], f32, kind="ExternalOutput").ap())
    build(nc, *args)
    r = _run(nc, [arrays], core_ids=[0])
    return r.results[0]["out_0_dram"]
```

```python
from contextlib import ExitStack

import numpy as np

import concourse.bass as bass
from concourse import mybir
from concourse.alu_op_type import AluOpType as ALU

f32 = mybir.dt.float32
bf16 = mybir.dt.bfloat16
f16 = mybir.dt.float16
i32 = mybir.dt.int32
ACT = mybir.ActivationFunctionType
AX = mybir.AxisListType

N, E, D = 3125, 100000, 64
P = 125
T = N // P
GT = 5
NG = T // GT
ROWLEN = P
NROW = E // ROWLEN
HALF = NROW // 2
BLK = 4
NBLK = E // BLK
CH = 8
BPC = CH // BLK
WC = 4
WE = WC * CH
HEADS = 4
L0, L2 = 4, 3
HID = 128
KEYCAP = 4095
KEYMUL = 4096
FAR = -1.0e30
MAXG = E // CH + (E // P) // CH + 3 * T + 2
RBITS = 14
RMUL = 1 << RBITS
assert MAXG <= RMUL
AW = HEADS * (D + 1)
ROW0 = D + 1 + HEADS + 1
WIN = 784
WT, WP = 7, 112
ASL = 2
ARENA = 26000
BANK = 512
EXACT = 2048
RING = 5
PASSES = L2 + 1


def build(nc, x_in, src_in, dst_in, attr_in, W0, al0, ar0, gb0, hb0, mW1, mb1, mW2, mb2, nW1, nb1,
          nW2, nb2, lnS, lnO, Wl2, Wr2, b2_, gam2, bet2, Wp2, bp2, W3, b3, out):
    ctx = ExitStack()
    with ctx:
        def sb(name, shape, dt=f32):
            return ctx.enter_context(nc.sbuf_tensor(name, shape, dt))

        def pb(name, shape):
            return ctx.enter_context(nc.psum_tensor(name, shape, f32))

        def sem(name):
            return ctx.enter_context(nc.semaphore(name))

        def dram(name, shape, dt=f32):
            return nc.dram_tensor(name, shape, dt, kind="Internal").ap()

        starts_d = dram("starts_d", [N + 1], i32)
        keys_d = dram("keys_d", [N])
        meta_d = dram("meta_d", [N, 4], i32)
        srcs_d = dram("srcs_d", [E + WE], i32)
        runs_d = dram("runs_d", [NBLK, WE], i32)
        rec_d = dram("rec_d", [MAXG + WC, P, CH + BPC], i32)
        tab0_d = dram("tab0_d", [N + 1, ROW0])
        tab1_d = dram("tab1_d", [N + 1, D + 1])
        tab2_d = dram("tab2_d", [N + 1, D])
        hist_d = dram("hist_d", [64 * 64, 1])
        cnt_d = dram("cnt_d", [L0 * WIN, N], f16)
        invd_d = dram("invd_d", [N])

        ident = sb("ident", [128, 128])
        ones = sb("ones", [1, 128])
        tail_end = sb("tail_end", [1, 1], i32)
        nodeid = sb("nodeid", [P, T])
        nodeid_i = sb("nodeid_i", [P, T], i32)
        iota8 = sb("iota8", [P, CH])
        iota8_i = sb("iota8_i", [P, CH], i32)
        iota64 = sb("iota64", [P, 64], f16)
        iota64_i = sb("iota64_i", [P, 64], i32)
        step3 = sb("step3", [P, 3])
        iota_e = sb("iota_e", [P, WE])
        iota_ei = sb("iota_ei", [P, WE], i32)
        padrow = sb("padrow", [1, HID + 1 + HEADS + 1])
        ident16 = sb("ident16", [128, 128], f16)
        zeros16 = sb("zeros16", [P, BANK], f16)
        dense_i = sb("dense_i", [1, 1], i32)

        arena = sb("arena", [128, ARENA])
        at = {"first": 0, "sums": 0}

        def share(part, parts, shape, dt=f32):
            words = int(np.prod(shape)) if dt in (f32, i32) else (int(np.prod(shape)) + 1) // 2
            lo = at[part]
            at[part] = lo + words
            assert at[part] <= ARENA, (part, at[part])
            v = arena[0:parts, lo:lo + words]
            v = v if dt == f32 else v.bitcast(dt)[:, 0:int(np.prod(shape))]
            names = ["a", "b", "c"][:len(shape)]
            if len(shape) > 1:
                v = v.rearrange(f"p ({' '.join(names)}) -> p {' '.join(names)}", **dict(zip(names, shape)))
            return v

        firsts_i = share("first", 1, [NROW], i32)
        firsts = share("first", 1, [NROW])
        firsts_b = share("first", P, [NROW])
        wide_all = share("first", 128, [T * HID])
        wide = wide_all[0:P]
        kcount = sb("kcount", [P, T])
        krow = sb("krow", [P, T])
        krow_i = sb("krow_i", [P, T], i32)
        start_i = sb("start_i", [P, T], i32)
        end_i = sb("end_i", [P, T], i32)
        pf = [sb(f"pf{i}", [P, T]) for i in range(6)]
        pi = [sb(f"pi{i}", [P, T], i32) for i in range(4)]
        keys_b = sb("keys_b", [P, N])
        drows = keys_b[:, :].bitcast(i32).rearrange("p (t m) -> p t m", m=ROWLEN)
        rank_i = sb("rank_i", [P, T], i32)
        meta_o = sb("meta_o", [P, T, 4], i32)
        meta = sb("meta", [P, T, 4], i32)
        perm = sb("perm", [P, T], i32)
        nch_f = sb("nch_f", [P, T])
        tmax = sb("tmax", [P, T])
        cs_a = sb("cs_a", [1, T + 1])
        cs_b = sb("cs_b", [1, T + 1])
        cs_i = sb("cs_i", [1, T + 1], i32)
        edge_cur = sb("edge_cur", [P, T, 3])
        blk_ix = sb("blk_ix", [P, T], i32)
        blks = sb("blks", [P, T, WC * BPC])
        nrounds = sb("nrounds", [1, 2], i32)
        ranges = sb("ranges", [1, T], i32)
        deg = sb("deg", [P, T])
        dmax = sb("dmax", [P, 2])

        x = sb("x", [P, T, D])
        h = sb("h", [P, T, D])
        xc = sb("xc", [P, T, D])
        sq = sb("sq", [P, T, D])
        stat = sb("stat", [P, T])
        std = sb("std", [P, T])
        rstd = sb("rstd", [P, T])
        tab = sb("tab", [P, T, ROW0])
        er = sb("er", [P, T, HEADS])
        tr5 = sb("tr5", [128, GT, P])

        y = sb("y", [P, T, D])
        y_ = y[:, :, :].rearrange("p t d -> p (t d)")

        idx = sb("idx", [P, 2, CH + BPC], i32)
        rows = sb("rows", [P, 2, CH, ROW0])
        zz = sb("zz", [P, CH + 1, HEADS])
        pz = sb("pz", [P, CH + 1, HEADS])
        pe = sb("pe", [P, CH + 1, HEADS])
        mnew = sb("mnew", [P, HEADS])
        acc = sb("acc", [P, HEADS, D + 1])
        prod = share("first", P, [CH, HEADS, D + 1])
        rsave = sb("rsave", [P, HEADS])
        ids8 = sb("ids8", [P, CH])
        wofs = sb("wofs", [P, 1])
        iota_w_i = share("first", P, [WIN], i32)
        iota_w = share("first", P, [WIN], f16)
        onehot = share("first", P, [CH, WIN], f16)
        cb = share("first", P, [WIN], f16)
        ctT = share("first", WP, [WT, P], f16)
        spare = onehot.rearrange("p s w -> p (s w)")[:, 6 * L0 * 128:].bitcast(i32)
        recs = spare[:, 0:T * WC * (CH + BPC)].rearrange("p (t k c) -> p t k c", t=T, k=WC)
        raw_src = y_.bitcast(i32)[:, 0:T * WE].rearrange("p (t s) -> p t s", t=T)
        vmask = wide[:, 0:2 * T * WE].rearrange("p (k t s) -> p k t s", k=2, t=T)
        rden = sb("rden", [P, HEADS])
        u = sb("u", [P, HEADS, D])
        uT = sb("uT", [128, 2, P])

        cat = share("first", P, [T, 2 * D])
        BnT = wide_all[:, 0:N].rearrange("p (t n) -> p t n", n=P)
        attr = share("first", P, [2, CH, D])
        at_s = share("first", P, [CH, 2 * D])
        atT = share("first", 128, [2, CH // 2, P])
        hidB = share("first", 128, [2, CH // 2, P])
        real = sb("real", [P, CH])
        hidT = share("first", 128, [2, CH // 2, P])
        msgs = share("first", P, [2, CH // 2, D])
        msum = sb("msum", [P, D])
        macc = sb("macc", [P, D])
        zT5 = share("first", 128, [GT, P])
        srcs_i = share("first", P, [NROW], i32)
        hilo_i = share("first", P, [2, NROW], i32)
        hilo = sb("hilo", [P, 2, NROW], f16)
        OHC = NROW // T
        oh = onehot[:, :, :].rearrange("p s w -> p (s w)")[:, 0:2 * OHC * 64]\
            .rearrange("p (k c n) -> p k c n", k=2, c=OHC)
        hist = sb("hist", [64, 64])

        hTall = share("sums", D, [T, P])
        aggT = share("sums", 128, [N])
        invd_b = share("sums", 128, [N])
        hp12 = share("sums", P, [T, 2 * D], bf16)
        hp3 = share("sums", P, [T, 2 * D], bf16)
        cring = share("sums", P, [RING, N], f16)
        yT = keys_b[0:D, :].rearrange("p (t n) -> p t n", n=P)
        bnst = sb("bnst", [D, 8])
        wst = sb("wst", [128, 2, D])
        iw = sb("iw", [D, 2 * D])
        agg = sb("agg", [P, T, D])
        odeg = sb("odeg", [P, T])
        dinv = sb("dinv", [P, T])
        invd = sb("invd", [P, T])

        W1b = sb("W1b", [D, HID])
        W1ca = sb("W1ca", [2 * D, HID])
        W2s = sb("W2s", [HID, D])
        b1c = sb("b1c", [HID, 1])
        b2b = sb("b2b", [P, D])
        nW1s = sb("nW1s", [128, HID])
        nW2s = sb("nW2s", [HID, D])
        nb1c = sb("nb1c", [HID, 1])
        nb2b = sb("nb2b", [P, D])
        lnSb = sb("lnSb", [P, D])
        lnOb = sb("lnOb", [P, D])
        wnat = sb("wnat", [D, 10, D])
        wT = sb("wT", [D, 10, D])
        bnc = sb("bnc", [D, 3, L2])
        bpb = sb("bpb", [P, D])
        b3b = sb("b3b", [P, D])
        W0s = sb("W0s", [128, L0, 2, D + 2 * HEADS])
        early = cat[0:D, :, :].rearrange("p t c -> p (t c)")
        alr = early[:, 0:2 * L0 * HEADS * D].rearrange("p (k l h d) -> p k l h d", k=2, l=L0, h=HEADS)
        W0k = early[:, 2 * L0 * HEADS * D:3 * L0 * HEADS * D].rearrange("p (l h d) -> p l h d", l=L0, h=HEADS)
        WL = sb("WL", [D, L0 + 1, 2 * HEADS])
        gbb = agg[:, :, :].rearrange("p t d -> p (t d)")[:, 0:L0 * HEADS * D]\
            .rearrange("p (l h d) -> p l h d", l=L0, h=HEADS)
        gbs = sb("gbs", [P, L0, D + 2 * HEADS])
        foldT = onehot.rearrange("p s w -> p (s w)")[0:D, 0:6 * L0 * 128].bitcast(f32).rearrange("p (k c) -> p k c", c=128)
        hbb = sb("hbb", [P, D])

        ps = pb("ps", [128, 8 * BANK])

        def bank(b, parts=128, n=1):
            return ps[0:parts, b * BANK:(b + n) * BANK]

        firsts_ps = bank(0, P, 2).rearrange("p (b c) -> p b c", b=2)[:, :, 0:HALF]
        acc_ps = bank(0, P)[:, 0:AW].rearrange("p (h d) -> p h d", h=HEADS)
        ctT_ps = bank(1, WP).bitcast(f16)[:, 0:WT * 128].rearrange("p (k c) -> p k c", k=WT)
        cnt_ps = bank(2, P, 2).rearrange("p (b c) -> p b c", b=2)[:, :, 0:WIN // 2]
        uT_ps = bank(4)[:, 0:256].rearrange("p (k c) -> p k c", k=2)[:, :, 0:P]
        hn_ps = bank(5, P)[:, 0:D + 2 * HEADS]
        foldT_ps = bank(4, D, 3).rearrange("p (k c) -> p k c", c=128)
        fold_ps = bank(7)[:, 0:3 * L0 * 2 * HEADS].rearrange("p (l k c) -> p l k c", l=L0, k=3)
        tr_ps = bank(0, 128, 2)[:, 0:GT * 128].rearrange("p (j c) -> p j c", j=GT)
        mmT_ps = bank(2, 128, 2)[:, 0:GT * 128].rearrange("p (j c) -> p j c", j=GT)
        mm_ps = mmT_ps[0:P]
        mm2_ps = bank(4, P, 2)[:, 0:GT * 128].rearrange("p (j c) -> p j c", j=GT)
        wT_ps = bank(0, D, 2)[:, 0:10 * D].rearrange("p (j c) -> p j c", j=10)
        atT_ps = [bank(q)[:, 0:P * CH // 2].rearrange("p (k c) -> p k c", k=CH // 2) for q in range(2)]
        hid_ps = [bank(4 + q)[:, 0:P * CH // 2].rearrange("p (k c) -> p k c", k=CH // 2) for q in range(2)]
        msg_ps = [bank(6 + q, P)[:, 0:D * CH // 2].rearrange("p (k c) -> p k c", k=CH // 2) for q in range(2)]
        hist_ps = bank(2, 64)[:, 0:64]
        allT_ps = ps[:, 0:N]
        tiles_ps = ps[:, 0:T * 128].rearrange("p (t c) -> p t c", t=T)
        tiles64_ps = ps[0:P, 0:T * D].rearrange("p (t c) -> p t c", t=T)

        s_first = sem("firsts_loaded")
        s_const = sem("constants_made")
        s_firstf = sem("firsts_cast")
        s_firstp = sem("firsts_in_psum")
        s_krow = sem("row_numbers_made")
        s_drows = sem("receiver_rows_landed")
        s_start = sem("starts_made")
        s_startst = sem("starts_stored")
        s_end = sem("ends_loaded")
        s_key = sem("keys_made")
        s_keyst = sem("keys_stored")
        s_keyb = sem("keys_spread")
        s_rank = sem("ranks_made")
        s_metast = sem("meta_scattered")
        s_meta = sem("meta_loaded")
        s_nch = sem("node_chunks_made")
        s_tmax = sem("tile_chunks_made")
        s_cs = sem("chunk_starts_made")
        s_perm = sem("perm_made")
        s_bix = sem("block_index_made")
        s_srcs = sem("senders_copied")
        s_runs = sem("senders_by_block_stored")
        s_raw = sem("senders_landed")
        s_recm = sem("records_made")
        s_recst = sem("records_stored")
        s_x = sem("x_gathered")
        s_w0 = sem("attention_weights_loaded")
        s_WL = sem("attention_vectors_folded")
        s_pad = sem("padding_rows_stored")
        s_var = sem("variance_made")
        s_std = sem("deviation_made")
        s_h = sem("normed_made")
        s_itr = sem("init_transposed")
        s_itrs = sem("init_transpose_copied")
        s_imm = sem("init_scores_made")
        s_tabr = sem("table_rows_made")
        s_tabst = sem("table_scattered")
        s_idx = [sem(f"index_loaded{i}") for i in range(2)]
        s_land = [sem(f"rows_landed{i}") for i in range(2)]
        s_rows = sem("rows_ready")
        s_clear = sem("landed_counts_cleared")
        s_free = sem("rows_free")
        s_z = sem("scores_ready")
        s_p = sem("probs_ready")
        s_u = sem("tile_sums_ready")
        s_uTp = sem("sums_transposed")
        s_uT = sem("sums_transpose_copied")
        s_hn = sem("new_rows_in_psum")
        s_foldTp = sem("fold_operands_transposed")
        s_foldT = sem("fold_transposes_copied")
        s_foldp = sem("folds_in_psum")
        s_fold = sem("folds_copied")
        s_gate = sem("gates_passed")
        s_w1 = sem("message_weights_loaded")
        s_w2 = sem("other_weights_loaded")
        s_wTp = sem("weights_transposed")
        s_wT = sem("weights_transpose_copied")
        s_tr = sem("group_transposed")
        s_trs = sem("group_transpose_copied")
        s_mm = sem("group_product_made")
        s_mms = sem("group_product_copied")
        s_mm2 = sem("group_second_product_made")
        s_mm2s = sem("group_second_product_used")
        s_bn = sem("features_centered")
        s_bns = sem("feature_deviation_made")
        s_scale = sem("feature_scale_made")
        s_hTall = sem("features_normed")
        s_tab1 = sem("message_table_made")
        s_tab2 = sem("sum_tables_made")
        s_land1 = [sem(f"message_rows_landed{i}") for i in range(2)]
        s_at = sem("edge_features_staged")
        s_atTp = sem("edge_features_transposed")
        s_atT = sem("edge_transpose_copied")
        s_pre = sem("node_parts_staged")
        s_hidp = sem("hidden_made")
        s_hid = sem("hidden_rectified")
        s_msg = sem("messages_made")
        s_oh = sem("one_hots_made")
        s_hist = sem("counts_made")
        s_histo = sem("counts_summed")
        s_histst = sem("counts_stored")
        s_deg = sem("counts_gathered")
        s_srcc = sem("senders_loaded")
        s_out = sem("output_ready")
        s_own = sem("tile_begun")
        s_ones = sem("one_hots_of_chunk_made")
        s_prod = sem("weighted_rows_made")
        s_proda = sem("last_slots_weighted")
        s_accp = sem("weighted_rows_summed")
        s_cnt = sem("window_counted")
        s_cntu = sem("one_hots_used")
        s_cb = sem("counts_copied")
        s_ctTp = sem("window_counts_transposed")
        s_ctT = sem("window_transpose_copied")
        s_cntst = sem("window_counts_stored")
        s_invd = sem("inverse_degrees_made")
        s_invst = sem("inverse_degrees_stored")
        s_invb = sem("inverse_degrees_spread")
        s_parts = sem("feature_parts_made")
        s_ring = [sem(f"counts_landed{i}") for i in range(RING)]
        s_ringf = sem("counts_tile_used")
        s_aggp = sem("sums_in_psum")
        s_aggT = sem("sums_copied")
        s_trall = sem("features_transposed_all")
        s_hTc = sem("features_transpose_kept")
        s_y = sem("layer_product_made")
        s_yc = sem("layer_product_kept")
        s_back = sem("features_back_by_node")
        s_backc = sem("new_table_rows_copied")
        s_xd = sem("layer_added_to_x")
        s_aggtr = sem("gathered_sums_transposed")
        s_outst = sem("output_stored")

        MAXC = MAXG - 1

        def wait_reg(eng, sem_, value):
            eng.wait_ge(sem_, value).then_inc(s_gate, 1)

        def is_dense(eng):
            return eng.value_load(dense_i[0:1, 0:1], min_val=0, max_val=1)

        def chunk_range(eng, t):
            both = eng.value_load(ranges[0:1, bass.ds(t, 1)], min_val=0, max_val=MAXC * RMUL + MAXC)
            return eng.snap(both // RMUL), eng.snap(both % RMUL)

        def chunk_count(eng):
            return eng.value_load(cs_i[0:1, T:T + 1], min_val=T + 1, max_val=MAXC)

        def round_count(eng):
            return eng.value_load(nrounds[0:1, 0:1], min_val=1, max_val=MAXC // WC + 1)

        def store_records(eng, rounds, odd):
            with eng.Fori(0, rounds) as r:
                wait_reg(eng, s_recm, r + 1)
                with eng.Fori(0, (T + 1 - odd) // 2) as t2:
                    t = t2 * 2 + odd
                    lo, hi = chunk_range(eng, t)
                    first = eng.snap(lo + r * WC)
                    left = eng.snap(hi - first)
                    at = eng.snap(first % MAXG)
                    rec = recs[:, bass.ds(t, 1), :, :].rearrange("p o k c -> p (o k) c")
                    for n in range(WC + 1):
                        with eng.If(left >= n if n == WC else (left <= 0 if n == 0 else left == n)):
                            if n == 0:
                                eng.sem_inc(s_recst, 16)
                            else:
                                eng.dma_start(rec_d[bass.ds(at, n)].rearrange("k p c -> p k c"), rec[:, 0:n, :])\
                                   .then_inc(s_recst, 16)

        block = ctx.enter_context(nc.Block())

        @block.sync
        def _(eng):
            with nc.allow_non_contiguous_dma("the receivers of every 125th edge, and node records"):
                eng.dma_start(firsts_i[:, :], dst_in.rearrange("(k m) -> m k", m=ROWLEN)[0:1, :])\
                   .then_inc(s_first, 16)
                for l in range(L0):
                    eng.dma_start(W0k[:, l, :, :], W0[l].rearrange("k (h d) -> k h d", h=HEADS)).then_inc(s_w0, 16)
                    for hh in range(2):
                        eng.dma_start(W0s[hh * D:(hh + 1) * D, l, :, 0:D],
                                      W0[l].rearrange("k (a b d) -> k b a d", a=2, b=2)[:, hh]).then_inc(s_w0, 16)
                eng.dma_start(alr[:, 0, :, :, :], al0.unsqueeze(0).to_broadcast([D, L0, HEADS, D])).then_inc(s_w0, 16)
                eng.dma_start(alr[:, 1, :, :, :], ar0.unsqueeze(0).to_broadcast([D, L0, HEADS, D])).then_inc(s_w0, 16)
                eng.dma_start(gbb[:, :, :, :], gb0.rearrange("l (h d) -> l h d", h=HEADS).unsqueeze(0)
                              .to_broadcast([P, L0, HEADS, D])).then_inc(s_w0, 16)
                eng.dma_start(hbb[:, :], hb0.unsqueeze(0).to_broadcast([P, D])).then_inc(s_w0, 16)
                eng.dma_start(W1b[:, :], mW1[D:2 * D, :]).then_inc(s_w1, 16)
                eng.dma_start(W1ca[0:D, :], mW1[2 * D:3 * D, :]).then_inc(s_w1, 16)
                eng.dma_start(W1ca[D:2 * D, :], mW1[0:D, :]).then_inc(s_w1, 16)
                eng.dma_start(W2s[:, :], mW2).then_inc(s_w1, 16)
                eng.dma_start(b1c[:, :], mb1.unsqueeze(1)).then_inc(s_w1, 16)
                eng.dma_start(b2b[:, :], mb2.unsqueeze(0).to_broadcast([P, D])).then_inc(s_w1, 16)
                eng.dma_start(nW1s[:, :], nW1).then_inc(s_w1, 16)
                eng.dma_start(nW2s[:, :], nW2).then_inc(s_w1, 16)
                eng.dma_start(nb1c[:, :], nb1.unsqueeze(1)).then_inc(s_w1, 16)
                eng.dma_start(nb2b[:, :], nb2.unsqueeze(0).to_broadcast([P, D])).then_inc(s_w1, 16)
                eng.dma_start(lnSb[:, :], lnS.unsqueeze(0).to_broadcast([P, D])).then_inc(s_w1, 16)
                eng.dma_start(lnOb[:, :], lnO.unsqueeze(0).to_broadcast([P, D])).then_inc(s_w1, 16)
                eng.dma_start(wnat[:, 0:3, :], Wl2.rearrange("l o k -> o l k")).then_inc(s_w2, 16)
                eng.dma_start(wnat[:, 3:6, :], Wr2.rearrange("l o k -> o l k")).then_inc(s_w2, 16)
                eng.dma_start(wnat[:, 6:9, :], Wp2.rearrange("o (l k) -> o l k", l=L2)).then_inc(s_w2, 16)
                eng.dma_start(wnat[:, 9, :], W3).then_inc(s_w2, 16)
                for k, v in enumerate((b2_, gam2, bet2)):
                    eng.dma_start(bnc[:, k, :], v.rearrange("l d -> d l")).then_inc(s_w2, 16)
                eng.dma_start(bpb[:, :], bp2.unsqueeze(0).to_broadcast([P, D])).then_inc(s_w2, 16)
                eng.dma_start(b3b[:, :], b3.unsqueeze(0).to_broadcast([P, D])).then_inc(s_w2, 16)
                eng.dma_start(srcs_i[:, :], src_in.rearrange("(p c) -> p c", p=P)).then_inc(s_srcc, 16)
                eng.wait_ge(s_start, 2)
                eng.dma_start(starts_d[0:N].rearrange("(p t) -> p t", t=T), start_i[:, :]).then_inc(s_startst, 16)
                eng.dma_start(starts_d[N:N + 1].unsqueeze(0), tail_end[:, :]).then_inc(s_startst, 16)
                eng.wait_ge(s_startst, 32)
                eng.dma_start(end_i[:, :], starts_d[1:N + 1].rearrange("(p t) -> p t", t=T)).then_inc(s_end, 16)
                eng.wait_ge(s_key, 1)
                eng.dma_start(keys_d.rearrange("(p t) -> p t", t=T), pf[5][:, :]).then_inc(s_keyst, 16)
                eng.wait_ge(s_keyst, 16)
                eng.dma_start(keys_b[:, :], keys_d.unsqueeze(0).to_broadcast([P, N])).then_inc(s_keyb, 16)
                eng.wait_ge(s_metast, 16 * T)
                eng.dma_start(meta[:, :, :], meta_d.rearrange("(t p) c -> p t c", p=P)).then_inc(s_meta, 16)
                eng.wait_ge(s_const, 1)
                eng.dma_start(tab0_d[N:N + 1, 0:D + 1], padrow[:, 0:D + 1]).then_inc(s_pad, 16)
                eng.dma_start(tab0_d[N:N + 1, D + 1:ROW0],
                              padrow[:, HID + 1:HID + 2 + HEADS]).then_inc(s_pad, 16)
                eng.dma_start(tab1_d[N:N + 1, :], padrow[:, 0:D + 1]).then_inc(s_pad, 16)
                eng.dma_start(tab2_d[N:N + 1, :], padrow[:, 0:D]).then_inc(s_pad, 16)

                eng.wait_ge(s_cs, 1)
                pairs = chunk_count(eng) // 2
                rounds = round_count(eng)
                store_records(eng, rounds, 0)
                wait_reg(eng, s_recst, rounds * 16 * T)

                def load_index(c, b):
                    eng.dma_start(idx[:, b, :], rec_d[bass.ds(c, 1)].rearrange("o p c -> (o p) c"))\
                       .then_inc(s_idx[b], 16)

                def relay_pass(k, landed, per_chunk):
                    wait_reg(eng, s_clear, k + 1)
                    with eng.Fori(0, pairs) as n:
                        following = eng.snap((n + 1) % pairs)
                        for b in range(2):
                            eng.wait_ge(landed[b], (n + 1) * 16 * per_chunk).then_inc(s_rows, 1)
                            load_index(following * 2 + b, b)

                for b in range(2):
                    load_index(b, b)

                with eng.Fori(0, L0) as layer:
                    relay_pass(layer, s_land, CH)
                relay_pass(L0, s_land1, CH + BPC)
                eng.wait_ge(s_histo, 1)
                eng.dma_start(hist_d.rearrange("(a b) o -> a (b o)", b=64), hist[:, :]).then_inc(s_histst, 16)
                eng.wait_ge(s_invd, 1)
                eng.dma_start(invd_d.rearrange("(t p) -> p t", p=P), invd[:, :]).then_inc(s_invst, 16)
                eng.wait_ge(s_invst, 16)
                eng.dma_start(invd_b, invd_d.unsqueeze(0).to_broadcast([128, N])).then_inc(s_invb, 16)
                dense = is_dense(eng)
                with eng.If(dense == 0):
                    with eng.Fori(0, PASSES) as layer:
                        relay_pass(layer + (L0 + 1), s_land, CH)
                    for b in range(2):
                        wait_reg(eng, s_idx[b], ((L0 + 1 + PASSES) * pairs + 1) * 16)
                for b in range(2):
                    wait_reg(eng, s_idx[b], ((L0 + 1) * pairs + 1) * 16)
                eng.wait_ge(s_outst, 16 * T)

        @block.gpsimd
        def _(eng):
            eng.memset(ident[:, :], 0.0)
            eng.memset(ones[:, :], 1.0)
            eng.memset(tail_end[:, :], E)
            eng.memset(padrow[:, 0:HID + 1], 0.0)
            eng.memset(padrow[:, HID + 1:HID + 1 + HEADS], FAR)
            eng.memset(padrow[:, HID + 1 + HEADS:HID + 2 + HEADS], -1.0)
            eng.memset(zeros16[:, :], 0.0)
            eng.iota(iota_w_i[:, :], pattern=[[1, WIN]], base=0, channel_multiplier=0)
            eng.memset(step3[:, 0:1], float(WC * BPC))
            eng.memset(step3[:, 1:3], float(-WE))
            eng.iota(iota_ei[:, :], pattern=[[1, WE]], base=0, channel_multiplier=0)
            eng.iota(nodeid_i[:, :], pattern=[[1, T]], base=0, channel_multiplier=T)
            eng.iota(iota8_i[:, :], pattern=[[1, CH]], base=0, channel_multiplier=0)
            eng.iota(iota64_i[:, :], pattern=[[1, 64]], base=0, channel_multiplier=0)
            eng.drain()
            eng.affine_select(out=ident[:, :], in_=ident[:, :], compare_op=ALU.not_equal, fill=1.0,
                              base=0, pattern=[[-1, 128]], channel_multiplier=1)
            eng.drain()
            eng.tensor_copy(ident16[:, :], ident[:, :])
            eng.tensor_copy(iota_w[:, :], iota_w_i[:, :])
            eng.drain().then_inc(s_const, 1)

            eng.wait_ge(s_krow, 1)
            dst_rows = dst_in.rearrange("(k m) -> k m", m=ROWLEN)
            for t in range(T):
                eng.indirect_dma_start(out=drows[:, t, :], out_offset=None, in_=dst_rows,
                                       in_offset=bass.IndirectOffsetOnAxis(ap=krow_i[:, t:t + 1], axis=0))\
                   .then_inc(s_drows, 16)
            eng.wait_ge(s_rank, 1)
            for t in range(T):
                eng.indirect_dma_start(out=meta_d, out_offset=bass.IndirectOffsetOnAxis(ap=rank_i[:, t:t + 1], axis=0),
                                       in_=meta_o[:, t, :], in_offset=None).then_inc(s_metast, 16)
            eng.wait_ge(s_nch, 1)
            eng.partition_all_reduce(tmax[:, :], nch_f[:, :], P, bass.bass_isa.ReduceOp.max)
            eng.partition_all_reduce(dmax[:, 1:2], dmax[:, 0:1], P, bass.bass_isa.ReduceOp.max)
            eng.drain().then_inc(s_tmax, 1)
            eng.wait_ge(s_perm, 1)
            for t in range(T):
                eng.indirect_dma_start(out=x[:, t, :], out_offset=None, in_=x_in,
                                       in_offset=bass.IndirectOffsetOnAxis(ap=perm[:, t:t + 1], axis=0))\
                   .then_inc(s_x, 16)

            eng.wait_ge(s_cs, 1)
            pairs = chunk_count(eng) // 2
            eng.wait_ge(s_runs, 16)
            rounds = round_count(eng)
            with eng.Fori(0, rounds) as r:
                wait_reg(eng, s_bix, r + 1)
                for t in range(T):
                    eng.indirect_dma_start(out=raw_src[:, t, :], out_offset=None, in_=runs_d,
                                           in_offset=bass.IndirectOffsetOnAxis(ap=blk_ix[:, t:t + 1], axis=0))\
                       .then_inc(s_raw, 16)

            def scatter_tiles(table, width, tiles):
                for t in tiles:
                    eng.indirect_dma_start(out=table, out_offset=bass.IndirectOffsetOnAxis(ap=perm[:, t:t + 1], axis=0),
                                           in_=tab[:, t, 0:width], in_offset=None).then_inc(s_tabst, 16)

            def scatter_table(table, width, k):
                scatter_tiles(table, width, range(T))
                wait_reg(eng, s_tabst, (k + 1) * 16 * T)

            attr_blocks = attr_in.rearrange("(k m) d -> k (m d)", m=BLK)

            def gather_pass(k, table, width, landed, edges=False):
                with eng.Fori(0, pairs) as n:
                    for b in range(2):
                        eng.wait_ge(s_idx[b], (k * pairs + n + 1) * 16)
                        wait_reg(eng, s_free, (k * pairs + n) * 2 + b + 1)
                        for s in range(CH):
                            eng.indirect_dma_start(out=rows[:, b, s, 0:width], out_offset=None, in_=table,
                                                   in_offset=bass.IndirectOffsetOnAxis(ap=idx[:, b, s:s + 1], axis=0))\
                               .then_inc(landed[b], 16)
                        for j in range(BPC if edges else 0):
                            eng.indirect_dma_start(out=attr[:, b, j * BLK:(j + 1) * BLK, :].rearrange("p s d -> p (s d)"),
                                                   out_offset=None, in_=attr_blocks,
                                                   in_offset=bass.IndirectOffsetOnAxis(ap=idx[:, b, CH + j:CH + j + 1], axis=0))\
                               .then_inc(landed[b], 16)
                wait_reg(eng, s_rows, (k + 1) * (pairs * 2))
                count = 16 * (CH + (BPC if edges else 0))
                for many, times in ((8, pairs // 8), (1, pairs % 8)):
                    with eng.Fori(0, times) as n:
                        eng.inc_swdge_sem(landed, [many * count, many * count], mode="sub")
                eng.drain().then_inc(s_clear, 1)

            eng.wait_ge(s_pad, 64)
            eng.sem_inc(s_clear, 1)
            with eng.Fori(0, L0) as layer:
                wait_reg(eng, s_tabr, layer * T + (T - 1))
                scatter_tiles(tab0_d, ROW0, range(T - 1))
                wait_reg(eng, s_tabr, (layer + 1) * T)
                scatter_tiles(tab0_d, ROW0, [T - 1])
                wait_reg(eng, s_tabst, (layer + 1) * 16 * T)
                gather_pass(layer, tab0_d, ROW0, s_land)
            eng.wait_ge(s_h, 2)
            scatter_table(tab1_d, D + 1, L0)
            gather_pass(L0, tab1_d, D + 1, s_land1, edges=True)
            eng.wait_ge(s_histst, 16)
            for t in range(T):
                eng.indirect_dma_start(out=odeg[:, t:t + 1], out_offset=None, in_=hist_d,
                                       in_offset=bass.IndirectOffsetOnAxis(ap=perm[:, t:t + 1], axis=0)).then_inc(s_deg, 16)
            dense = is_dense(eng)
            with eng.If(dense == 1):
                eng.wait_ge(s_cntst, 16 * (L0 * T + 1))
                eng.wait_ge(s_invd, 1)
                with eng.Fori(0, PASSES) as layer:
                    for t in range(T):
                        b = t % RING
                        wait_reg(eng, s_ringf, layer * T + (t + 1))
                        eng.indirect_dma_start(out=cring[:, b, :], out_offset=None, in_=cnt_d,
                                               in_offset=bass.IndirectOffsetOnAxis(ap=perm[:, t:t + 1], axis=0))\
                           .then_inc(s_ring[b], 16)
            with eng.If(dense == 0):
                with eng.Fori(0, PASSES) as layer:
                    wait_reg(eng, s_tab2, layer + 1)
                    scatter_table(tab2_d, D, layer + (L0 + 1))
                    gather_pass(layer + (L0 + 1), tab2_d, D, s_land)
            eng.wait_ge(s_out, 1)
            for t in range(T):
                eng.indirect_dma_start(out=out, out_offset=bass.IndirectOffsetOnAxis(ap=perm[:, t:t + 1], axis=0),
                                       in_=x[:, t, :], in_offset=None).then_inc(s_outst, 16)
            eng.wait_ge(s_outst, 16 * T)

        @block.scalar
        def _(eng):
            def deviations(k):
                eng.wait_ge(s_var, k)
                eng.activation(std[:, :], stat[:, :], ACT.Sqrt).then_inc(s_std, 1)

            with nc.allow_non_contiguous_dma("overlapping rows"):
                eng.dma_start(srcs_d[0:E], src_in).then_inc(s_srcs, 16)
                eng.dma_start(srcs_d[E:E + WE], src_in[0:WE]).then_inc(s_srcs, 16)
                eng.wait_ge(s_srcs, 32)
                eng.dma_start(runs_d, bass.AP(tensor=srcs_d.tensor, offset=0, ap=[[BLK, NBLK], [1, WE]]))\
                   .then_inc(s_runs, 16)

            deviations(1)
            for g in range(NG):
                j = slice(g * GT, (g + 1) * GT)
                eng.wait_ge(s_itr, g + 1)
                eng.activation(tr5[0:D, :, :], tr_ps[0:D, :, 0:P], ACT.Copy).then_inc(s_itrs, 1)
                eng.wait_ge(s_imm, g + 1)
                eng.activation(tab[:, j, D + 1:D + 1 + HEADS], mm_ps[:, :, 0:HEADS], ACT.Copy)
                eng.activation(er[:, j, :], mm_ps[:, :, HEADS:2 * HEADS], ACT.Copy)
                eng.drain().then_inc(s_tabr, GT)

            store_records(eng, round_count(eng), 1)

            eng.wait_ge(s_foldTp, 1)
            for k in range(2):
                eng.activation(foldT[:, k::3, :], foldT_ps[:, k::3, :], ACT.Copy)
            eng.activation(foldT[:, 2::3, 0:P], foldT_ps[:, 2::3, 0:P], ACT.Copy).then_inc(s_foldT, 1)
            eng.wait_ge(s_foldp, 1)
            for k in range(2):
                eng.activation(W0s[:, :, k, D:], fold_ps[:, :, k, :], ACT.Copy)
            eng.activation(gbs[:, :, D:], fold_ps[0:P, :, 2, :], ACT.Copy)
            eng.drain().then_inc(s_fold, 1)

            def exp_chunk(layer, t, c):
                eng.wait_ge(s_z, layer * chunks + c + 1)
                eng.activation(pe[:, :, :], pz[:, :, :], ACT.Exp)
                eng.drain().then_inc(s_p, 1)
                eng.wait_ge(s_accp, c + (layer * chunks + layer * T + t + 1))
                for s in range(CH - ASL, CH):
                    for hh in range(HEADS):
                        last = eng.activation(prod[:, s, hh, :],
                                              rows[:, bass.ds(c % 2, 1), s, 0:D + 1].rearrange("p o c -> p (o c)"),
                                              ACT.Copy, scale=pe[:, s, hh:hh + 1])
                last.then_inc(s_proda, 1)

            def tile_rest(layer, t):
                done = layer * T + t + 1
                eng.wait_ge(s_hn, done)
                eng.activation(tab[:, bass.ds(t, 1), 0:D].rearrange("p o d -> p (o d)"), hn_ps[:, 0:D], ACT.Copy)
                eng.activation(tab[:, bass.ds(t, 1), D + 1:D + 1 + HEADS].rearrange("p o d -> p (o d)"),
                               hn_ps[:, D:D + HEADS], ACT.Copy)
                eng.activation(er[:, bass.ds(t, 1), :].rearrange("p o d -> p (o d)"),
                               hn_ps[:, D + HEADS:D + 2 * HEADS], ACT.Copy)
                eng.drain().then_inc(s_tabr, 1)
                eng.wait_ge(s_cntst, done * 16)
                eng.wait_ge(s_ctTp, done)
                eng.activation(ctT, ctT_ps[:, :, 0:P], ACT.Copy).then_inc(s_ctT, 1)
                eng.wait_ge(s_ctT, done)
                eng.dma_start(cnt_d[bass.ds(layer * WIN, WIN), bass.ds(t * P, P)].rearrange("(k p) i -> p k i", p=WP),
                              ctT).then_inc(s_cntst, 16)

            eng.wait_ge(s_cs, 1)
            chunks = chunk_count(eng)
            with eng.Fori(0, L0) as layer:
                with eng.Fori(0, T) as t:
                    lo, hi = chunk_range(eng, t)
                    done = layer * T + t + 1
                    exp_chunk(layer, t, lo)
                    with eng.If(t > 0):
                        tile_rest(layer, eng.snap((t + (T - 1)) % T))
                    with eng.Fori(lo + 1, hi) as c:
                        exp_chunk(layer, t, c)
                    eng.wait_ge(s_cnt, done)
                    eng.activation(cb.rearrange("p (b c) -> p b c", b=2), cnt_ps, ACT.Copy).then_inc(s_cb, 1)
                    eng.wait_ge(s_uTp, done)
                    eng.activation(uT[:, :, :], uT_ps, ACT.Copy).then_inc(s_uT, 1)
                tile_rest(layer, T - 1)

            eng.wait_ge(s_wTp, 1)
            eng.activation(wT[:, :, :], wT_ps, ACT.Copy).then_inc(s_wT, 1)

            deviations(2)
            eng.wait_ge(s_w1, 16 * 12)
            for g in range(NG):
                j = slice(g * GT, (g + 1) * GT)
                eng.wait_ge(s_tr, g + 1)
                eng.activation(tr5[0:D, :, :], tr_ps[0:D, :, 0:P], ACT.Copy).then_inc(s_trs, 1)
                eng.wait_ge(s_mm, g + 1)
                eng.activation(BnT[:, j, :], mmT_ps[:, :, 0:P], ACT.Identity, bias=b1c[:, 0:1]).then_inc(s_mms, 1)
            eng.drain().then_inc(s_tab1, 1)

            def stage_features(c):
                eng.wait_ge(s_rows, chunks * L0 + c + 1)
                eng.activation(at_s[:, :, 0:D], attr[:, bass.ds(c % 2, 1), :, :].rearrange("p o s d -> p (o s) d"),
                               ACT.Copy)
                eng.activation(at_s[:, :, D:2 * D], rows[:, bass.ds(c % 2, 1), :, 0:D].rearrange("p o s d -> p (o s) d"),
                               ACT.Copy).then_inc(s_at, 1)
                for q in range(2):
                    eng.wait_ge(s_atTp, c * 2 + q + 1)
                    eng.activation(atT[:, q, :, :], atT_ps[q], ACT.Copy).then_inc(s_atT, 1)

            def rectify_hidden(c):
                for q in range(2):
                    eng.wait_ge(s_pre, c * 2 + q + 1)
                    eng.activation(hidT[:, q, :, :], hidB[:, q, :, :], ACT.Relu).then_inc(s_hid, 1)

            stage_features(0)
            with eng.Fori(0, chunks) as c:
                rectify_hidden(c)
                with eng.If(c + 1 < chunks):
                    stage_features(c + 1)
            eng.wait_ge(s_w1, 16 * 12)
            for g in range(NG):
                eng.wait_ge(s_tr, NG + g + 1)
                eng.activation(tr5[:, :, :], tr_ps[:, :, 0:P], ACT.Copy).then_inc(s_trs, 1)
                eng.wait_ge(s_mm, NG + g + 1)
                eng.activation(zT5[:, :, :], mmT_ps[:, :, 0:P], ACT.Relu, bias=nb1c[:, 0:1]).then_inc(s_mms, 1)
            deviations(3)

            deviations(4)
            eng.wait_ge(s_trall, 1)
            eng.activation(hTall, tiles_ps[0:D, :, 0:P], ACT.Copy).then_inc(s_hTc, 1)
            dense = is_dense(eng)

            def gathered_sums(k):
                with eng.If(dense == 0):
                    eng.wait_ge(s_aggtr, k)
                    eng.activation(aggT[0:D, :].rearrange("p (t n) -> p t n", n=P), tiles_ps[0:D, :, 0:P], ACT.Copy)\
                       .then_inc(s_aggT, 1)

            with eng.Fori(0, L2) as layer:
                gathered_sums(layer + 1)
                eng.wait_ge(s_y, layer + 1)
                eng.activation(yT.rearrange("p t n -> p (t n)"), allT_ps[0:D, :], ACT.Identity, bias=bnst[:, 4:5])\
                   .then_inc(s_yc, 1)
                eng.wait_ge(s_bn, layer + 1)
                eng.activation(bnst[:, 2:3], bnst[:, 1:2], ACT.Sqrt).then_inc(s_bns, 1)
                eng.wait_ge(s_scale, layer + 1)
                eng.activation(hTall, yT, ACT.Relu, bias=bnst[:, 6:7], scale=bnst[:, 5:6]).then_inc(s_hTall, 1)
                eng.wait_ge(s_back, layer + 1)
                eng.activation(tab[:, :, 0:D], tiles_ps[0:P, :, 0:D], ACT.Copy).then_inc(s_backc, 1)

            deviations(5)
            eng.wait_ge(s_trall, 2)
            eng.activation(hTall, tiles_ps[0:D, :, 0:P], ACT.Copy).then_inc(s_hTc, 1)
            deviations(6)
            gathered_sums(PASSES)

        @block.tensor
        def _(eng):
            eng.wait_ge(s_firstf, 1)
            eng.wait_ge(s_const, 1)
            for b in range(2):
                last = eng.matmul(firsts_ps[:, b, :], ones[0:1, 0:P], firsts[0:1, b * HALF:(b + 1) * HALF],
                                  start=True, stop=True)
            last.then_inc(s_firstp, 1)

            eng.wait_ge(s_WL, 1)
            eng.wait_ge(s_h, 1)
            for g in range(NG):
                if g:
                    eng.wait_ge(s_tabr, g * GT)
                for j in range(GT):
                    last = eng.transpose(tr_ps[0:D, j, 0:P], h[:, g * GT + j, :], ident[0:P, 0:P])
                last.then_inc(s_itr, 1)
                eng.wait_ge(s_itrs, g + 1)
                for j in range(GT):
                    last = eng.matmul(mm_ps[:, j, 0:2 * HEADS], tr5[0:D, j, :], WL[:, 0, :], start=True, stop=True)
                last.then_inc(s_imm, 1)

            eng.wait_ge(s_cs, 1)
            chunks = chunk_count(eng)
            eng.wait_ge(s_tabr, T)
            eng.wait_ge(s_tabr, T)
            for l in range(L0):
                for k in range(2):
                    eng.transpose(foldT_ps[:, 3 * l + k, :], W0s[:, l, k, 0:D], ident[:, :])
                last = eng.transpose(foldT_ps[:, 3 * l + 2, 0:P], gbs[:, l, 0:D], ident[0:P, 0:P])
            last.then_inc(s_foldTp, 1)
            eng.wait_ge(s_foldT, 1)
            for l in range(L0):
                for k in range(2):
                    eng.matmul(fold_ps[:, l, k, :], foldT[:, 3 * l + k, :], WL[:, l + 1, :], start=True, stop=True)
                last = eng.matmul(fold_ps[0:P, l, 2, :], foldT[:, 3 * l + 2, 0:P], WL[:, l + 1, :], start=True, stop=True)
            last.then_inc(s_foldp, 1)
            eng.wait_ge(s_fold, 1)

            def sum_chunk(c):
                wait_reg(eng, s_prod, c + 1)
                for k in range(CH):
                    if k == CH - ASL:
                        wait_reg(eng, s_proda, c + 1)
                    last = eng.matmul(acc_ps, ident[0:P, 0:P], prod[:, k, :, :], start=(k == 0), stop=(k == CH - 1))
                last.then_inc(s_accp, 1)
                wait_reg(eng, s_ones, c + 1)
                for k in range(CH):
                    for b in range(2):
                        last = eng.matmul(cnt_ps[:, b, :], ident16[0:P, 0:P],
                                          onehot[:, k, b * (WIN // 2):(b + 1) * (WIN // 2)],
                                          start=False, stop=False, skip_group_check=True)
                last.then_inc(s_cntu, 1)

            def tile_rest(layer, t):
                done = layer * T + t + 1
                wait_reg(eng, s_uT, done)
                wl = W0s[:, bass.ds(layer, 1), :, :].rearrange("p o k d -> p (o k) d")
                eng.matmul(hn_ps, uT[:, 0, :], wl[:, 0, :], start=True, stop=False)
                eng.matmul(hn_ps, uT[:, 1, :], wl[:, 1, :], start=False, stop=False)
                eng.matmul(hn_ps, ident[0:P, 0:P], gbs[:, bass.ds(layer, 1), :].rearrange("p o d -> p (o d)"),
                           start=False, stop=True).then_inc(s_hn, 1)
                wait_reg(eng, s_cb, done + 1)
                for k in range(WT):
                    last = eng.transpose(ctT_ps[:, k, 0:P], cb[:, k * WP:(k + 1) * WP], ident16[0:P, 0:P])
                last.then_inc(s_ctTp, 1)

            with eng.Fori(0, L0) as layer:
                with eng.Fori(0, T) as t:
                    done = layer * T + t + 1
                    lo, hi = chunk_range(eng, t)
                    wait_reg(eng, s_own, done)
                    own = tab[:, bass.ds(t, 1), 0:D + 1].to_broadcast([P, HEADS, D + 1])
                    eng.matmul(acc_ps, ident[0:P, 0:P], own, start=True, stop=True).then_inc(s_accp, 1)
                    wait_reg(eng, s_cb, done)
                    for b in range(2):
                        eng.matmul(cnt_ps[:, b, :], ident16[0:P, 0:P], zeros16[:, 0:WIN // 2], start=True, stop=False,
                                   skip_group_check=True)
                    with eng.If(t > 0):
                        tile_rest(layer, eng.snap((t + (T - 1)) % T))
                    with eng.Fori(lo, hi) as c:
                        sum_chunk(layer * chunks + c)
                    for b in range(2):
                        last = eng.matmul(cnt_ps[:, b, :], ident16[0:P, 0:P], zeros16[:, 0:WIN // 2], start=False, stop=True,
                                          skip_group_check=True)
                    last.then_inc(s_cnt, 1)
                    wait_reg(eng, s_u, done)
                    for k in range(2):
                        last = eng.transpose(uT_ps[:, k, :], u[:, 2 * k:2 * k + 2, :].rearrange("p h d -> p (h d)"),
                                             ident[0:P, 0:P])
                    last.then_inc(s_uTp, 1)
                tile_rest(layer, T - 1)

            eng.wait_ge(s_w2, 16 * 9)
            eng.wait_ge(s_ctT, L0 * T)
            for k in range(10):
                last = eng.transpose(wT_ps[:, k, :], wnat[:, k, :], ident[0:D, 0:D])
            last.then_inc(s_wTp, 1)

            eng.wait_ge(s_w1, 16 * 12)
            eng.wait_ge(s_h, 2)
            for g in range(NG):
                if g == 0:
                    eng.wait_ge(s_wT, 1)
                for j in range(GT):
                    last = eng.transpose(tr_ps[0:D, j, 0:P], h[:, g * GT + j, :], ident[0:P, 0:P])
                last.then_inc(s_tr, 1)
                eng.wait_ge(s_trs, g + 1)
                if g:
                    eng.wait_ge(s_mms, g)
                for j in range(GT):
                    last = eng.matmul(mmT_ps[:, j, 0:P], W1b[:, :], tr5[0:D, j, :], start=True, stop=True)
                last.then_inc(s_mm, 1)
            eng.wait_ge(s_tab1, 2)

            def transpose_features_of_edges(c):
                wait_reg(eng, s_at, c + 1)
                for q in range(2):
                    for k in range(CH // 2):
                        last = eng.transpose(atT_ps[q][:, k, :], at_s[:, q * (CH // 2) + k, :], ident[0:P, 0:P])
                    last.then_inc(s_atTp, 1)

            def messages_of_chunk(c):
                for q in range(2):
                    wait_reg(eng, s_atT, c * 2 + q + 1)
                    eng.matmul(hid_ps[q], W1ca[:, :], atT[:, q, :, :], start=True, stop=True).then_inc(s_hidp, 1)
                for q in range(2):
                    wait_reg(eng, s_hid, c * 2 + q + 1)
                    for k in range(CH // 2):
                        last = eng.matmul(msg_ps[q][:, k, :], hidT[:, q, k, :], W2s[:, :], start=True, stop=True)
                    last.then_inc(s_msg, 1)

            eng.matmul(hist_ps, zeros16[:, 0:64], zeros16[:, 0:64], start=True, stop=False, skip_group_check=True)
            transpose_features_of_edges(0)
            with eng.Fori(0, chunks) as c:
                messages_of_chunk(c)
                with eng.If(c + 1 < chunks):
                    transpose_features_of_edges(c + 1)
                with eng.If(c < T):
                    wait_reg(eng, s_oh, c + 1)
                    for k in range(OHC):
                        last = eng.matmul(hist_ps, oh[:, 0, k, :], oh[:, 1, k, :], start=False, stop=False,
                                          skip_group_check=True)
                    last.then_inc(s_hist, 1)
            eng.wait_ge(s_oh, T)
            eng.matmul(hist_ps, zeros16[:, 0:64], zeros16[:, 0:64], start=False, stop=True, skip_group_check=True)\
               .then_inc(s_hist, 1)
            eng.wait_ge(s_tab1, 3)
            for g in range(NG):
                for j in range(GT):
                    last = eng.transpose(tr_ps[:, j, 0:P], cat[:, g * GT + j, :], ident[0:P, 0:P])
                last.then_inc(s_tr, 1)
                eng.wait_ge(s_trs, NG + g + 1)
                for j in range(GT):
                    last = eng.matmul(mmT_ps[:, j, 0:P], nW1s[:, :], tr5[:, j, :], start=True, stop=True)
                last.then_inc(s_mm, 1)
                eng.wait_ge(s_mms, NG + g + 1)
                if g:
                    eng.wait_ge(s_mm2s, g)
                for j in range(GT):
                    last = eng.matmul(mm2_ps[:, j, 0:D], zT5[:, j, :], nW2s[:, :], start=True, stop=True)
                last.then_inc(s_mm2, 1)

            dense = is_dense(eng)

            def transpose_features(k):
                eng.wait_ge(s_h, 2 + k)
                for t in range(T):
                    last = eng.transpose(tiles_ps[0:D, t, 0:P], h[:, t, :], ident[0:P, 0:P])
                last.then_inc(s_trall, 1)
                eng.wait_ge(s_hTc, k)

            def sums(k):
                with eng.If(dense == 1):
                    wait_reg(eng, s_parts, k + 1)
                    for g in range(0, N, BANK):
                        w = min(BANK, N - g)
                        eng.matmul(allT_ps[:, g:g + w], hp12[:, 0, :], zeros16[:, 0:w], start=True, stop=False,
                                   skip_group_check=True)
                    with eng.Fori(0, T // RING) as r:
                        for b in range(RING):
                            wait_reg(eng, s_ring[b], (k * (T // RING) + r + 1) * 16)
                            for part in (hp12, hp3):
                                lhs = part[:, bass.ds(r * RING + b, 1), :].rearrange("p o c -> p (o c)")
                                for g in range(0, N, BANK):
                                    w = min(BANK, N - g)
                                    last = eng.matmul(allT_ps[:, g:g + w], lhs, cring[:, b, g:g + w], start=False,
                                                      stop=False, skip_group_check=True)
                            last.then_inc(s_ringf, 1)
                    for g in range(0, N, BANK):
                        w = min(BANK, N - g)
                        last = eng.matmul(allT_ps[:, g:g + w], hp12[:, 0, :], zeros16[:, 0:w], start=False, stop=True,
                                          skip_group_check=True)
                    last.then_inc(s_aggp, 1)
                with eng.If(dense == 0):
                    wait_reg(eng, s_parts, k + 1)
                    for t in range(T):
                        last = eng.transpose(tiles_ps[0:D, t, 0:P], agg[:, t, :], ident[0:P, 0:P])
                    last.then_inc(s_aggtr, 1)
                wait_reg(eng, s_aggT, k + 1)

            transpose_features(1)
            with eng.Fori(0, L2) as layer:
                sums(layer)
                for g in range(0, N, BANK):
                    w = min(BANK, N - g)
                    eng.matmul(allT_ps[0:D, g:g + w], wst[:, 0, :], aggT[:, g:g + w], start=True, stop=False)
                    last = eng.matmul(allT_ps[0:D, g:g + w], wst[0:D, 1, :],
                                      hTall.rearrange("p t n -> p (t n)")[:, g:g + w], start=False, stop=True)
                last.then_inc(s_y, 1)
                wait_reg(eng, s_hTall, layer + 1)
                for t in range(T):
                    last = eng.matmul(tiles_ps[0:P, t, :], hTall[:, t, :], iw[:, :], start=True, stop=True)
                last.then_inc(s_back, 1)
                wait_reg(eng, s_xd, layer + 1)

            transpose_features(2)
            for t in range(T):
                last = eng.matmul(tiles64_ps[:, t, :], hTall[:, t, :], wT[:, 9, :], start=True, stop=True)
            last.then_inc(s_y, 1)
            eng.wait_ge(s_xd, L2 + 1)
            sums(L2)
            for t in range(T):
                last = eng.matmul(tiles64_ps[:, t, :], aggT[:, t * P:(t + 1) * P], wst[:, 0, :], start=True, stop=True)
            last.then_inc(s_y, 1)

        @block.vector
        def _(eng):
            V = nc.vector

            eng.wait_ge(s_first, 16)
            V.tensor_copy(firsts[:, :], firsts_i[:, :]).then_inc(s_firstf, 1)
            eng.wait_ge(s_const, 1)
            V.tensor_copy(nodeid[:, :], nodeid_i[:, :])
            V.tensor_copy(iota8[:, :], iota8_i[:, :])
            V.tensor_copy(iota_e[:, :], iota_ei[:, :])
            V.tensor_copy(iota64[:, :], iota64_i[:, :])
            eng.wait_ge(s_firstp, 1)
            V.tensor_copy(firsts_b[:, :].rearrange("p (b c) -> p b c", b=2), firsts_ps)
            V.drain()
            for t in range(T):
                V.tensor_scalar(wide[:, 0:NROW], firsts_b[:, :], nodeid[:, t:t + 1], 0.0, ALU.is_lt, ALU.add,
                                accum_out=kcount[:, t:t + 1])
                V.drain()
            V.tensor_scalar(krow[:, :], kcount[:, :], -1.0, 0.0, ALU.add, ALU.max)
            V.drain()
            V.tensor_copy(krow_i[:, :], krow[:, :]).then_inc(s_krow, 1)
            eng.wait_ge(s_drows, 16 * T)
            for t in range(T):
                V.tensor_scalar(wide[:, 0:ROWLEN], drows[:, t, :], nodeid[:, t:t + 1], 0.0, ALU.is_lt, ALU.add,
                                accum_out=pf[0][:, t:t + 1])
                V.drain()
            V.scalar_tensor_tensor(pf[1][:, :], krow[:, :], float(ROWLEN), pf[0][:, :], ALU.mult, ALU.add)
            V.drain()
            V.tensor_copy(start_i[:, :], pf[1][:, :]).then_inc(s_start, 2)
            V.drain()
            V.tensor_scalar(pi[0][:, :], start_i[:, :], 2, None, ALU.logical_shift_right)
            V.drain()
            V.tensor_copy(pf[2][:, :], pi[0][:, :])
            eng.wait_ge(s_end, 16)
            V.tensor_copy(pf[3][:, :], end_i[:, :])
            V.drain()
            V.scalar_tensor_tensor(pf[4][:, :], pf[2][:, :], float(-BLK), pf[3][:, :], ALU.mult, ALU.add)
            V.drain()
            V.tensor_scalar(pi[1][:, :], pf[4][:, :], float(BLK - 1), None, ALU.add)
            V.drain()
            V.tensor_scalar(pi[2][:, :], pi[1][:, :], 2, None, ALU.logical_shift_right)
            V.drain()
            V.tensor_scalar(pf[0][:, :], pi[2][:, :], float(KEYCAP), float(KEYMUL), ALU.min, ALU.mult)
            V.tensor_scalar(pi[1][:, :], pi[2][:, :], 1.0, None, ALU.add)
            V.drain()
            V.tensor_tensor(pf[5][:, :], pf[0][:, :], nodeid[:, :], ALU.add).then_inc(s_key, 1)
            V.tensor_scalar(pi[3][:, :], pi[1][:, :], 1, None, ALU.logical_shift_right)
            V.drain()
            V.tensor_copy(meta_o[:, :, 0], nodeid_i[:, :])
            V.tensor_copy(meta_o[:, :, 1], start_i[:, :])
            V.tensor_copy(meta_o[:, :, 2], end_i[:, :])
            V.tensor_copy(meta_o[:, :, 3], pi[3][:, :])
            eng.wait_ge(s_keyb, 16)
            for t in range(T):
                V.tensor_scalar(wide[:, 0:N], keys_b[:, :], pf[5][:, t:t + 1], 0.0, ALU.is_gt, ALU.add,
                                accum_out=pf[0][:, t:t + 1])
                V.drain()
            V.tensor_copy(rank_i[:, :], pf[0][:, :])
            V.drain().then_inc(s_rank, 1)

            eng.wait_ge(s_meta, 16)
            V.tensor_copy(perm[:, :], meta[:, :, 0]).then_inc(s_perm, 1)
            V.tensor_copy(tab[:, :, ROW0 - 1], meta[:, :, 0])
            V.tensor_scalar(pi[0][:, :], meta[:, :, 1], 2, None, ALU.logical_shift_right)
            V.tensor_copy(pf[1][:, :], meta[:, :, 1])
            V.tensor_copy(pf[2][:, :], meta[:, :, 2])
            V.drain()
            V.tensor_copy(edge_cur[:, :, 0], pi[0][:, :])
            V.tensor_tensor(deg[:, :], pf[2][:, :], pf[1][:, :], ALU.subtract)
            V.drain()
            V.tensor_copy(nch_f[:, :], meta[:, :, 3])
            V.tensor_reduce(dmax[:, 0:1], deg[:, :], AX.X, ALU.max)
            V.drain().then_inc(s_nch, 1)
            V.scalar_tensor_tensor(edge_cur[:, :, 1], edge_cur[:, :, 0], float(-BLK), pf[1][:, :], ALU.mult, ALU.add)
            V.scalar_tensor_tensor(edge_cur[:, :, 2], edge_cur[:, :, 0], float(-BLK), pf[2][:, :], ALU.mult, ALU.add)
            V.memset(cs_a[:, 0:1], 0.0)
            V.memset(cs_b[:, 0:1], 0.0)
            eng.wait_ge(s_tmax, 1)
            V.tensor_scalar(cs_a[:, 1:T + 1], tmax[0:1, :], 1.0, None, ALU.max)
            V.tensor_scalar(dense_i[:, :], dmax[0:1, 1:2], float(EXACT), None, ALU.is_le)
            a, b = cs_a, cs_b
            d = 1
            while d < T + 1:
                V.drain()
                V.tensor_copy(b[:, 0:d], a[:, 0:d])
                V.tensor_tensor(b[:, d:T + 1], a[:, d:T + 1], a[:, 0:T + 1 - d], ALU.add)
                a, b = b, a
                d *= 2
            V.drain()
            V.tensor_copy(cs_i[:, :], a[:, :])
            V.drain()
            V.tensor_scalar(b[:, T:T + 1], a[:, T:T + 1], 1.0, None, ALU.add)
            V.drain()
            V.tensor_copy(pi[0][0:1, 0:1], b[:, T:T + 1])
            V.drain()
            V.tensor_scalar(cs_i[:, T:T + 1], pi[0][0:1, 0:1], 1, 1, ALU.logical_shift_right, ALU.logical_shift_left)
            V.drain()

            V.tensor_scalar(blk_ix[:, :], edge_cur[:, :, 0], float(NBLK - 1), None, ALU.min)
            V.tensor_tensor(nrounds[:, 1:2], cs_i[:, T:T + 1], cs_i[:, T - 1:T], ALU.subtract)
            V.tensor_scalar(ranges[:, :], cs_i[:, 0:T], RBITS, None, ALU.logical_shift_left)
            V.drain()
            V.tensor_tensor(ranges[:, :], ranges[:, :], cs_i[:, 1:T + 1], ALU.bitwise_or)
            V.tensor_tensor(nrounds[:, 0:1], nrounds[:, 1:2], cs_i[:, 1:2], ALU.max)
            V.drain()
            V.tensor_scalar(nrounds[:, 1:2], nrounds[:, 0:1], float(WC - 1), None, ALU.add)
            V.drain()
            V.tensor_scalar(nrounds[:, 0:1], nrounds[:, 1:2], 2, None, ALU.logical_shift_right)
            V.drain().then_inc(s_bix, 1)
            V.sem_inc(s_cs, 1)

            chunks = chunk_count(eng)

            eng.wait_ge(s_w0, 16 * (3 * L0 + 4))
            V.memset(WL[:, :, :], 0.0)
            V.drain()
            for k in range(2):
                for l in range(L0):
                    V.tensor_tensor(sq[0:D, 0:HEADS, :], W0k[:, l, :, :], alr[:, k, l, :, :], ALU.mult)
                    V.drain()
                    V.tensor_reduce(WL[:, l, k * HEADS:(k + 1) * HEADS], sq[0:D, 0:HEADS, :], AX.X, ALU.add)
                    V.drain()
            V.tensor_reduce(gbs[:, :, 0:D], gbb[:, :, :, :].rearrange("p l h d -> p l d h"), AX.X, ALU.add)
            V.drain().then_inc(s_WL, 1)

            def normed(k, inp, outp, relu):
                V.tensor_reduce(stat[:, :], inp[:, :, :], AX.X, ALU.add)
                V.drain()
                V.tensor_scalar(stat[:, :], stat[:, :], 1.0 / D, None, ALU.mult)
                V.drain()
                V.tensor_tensor(xc[:, :, :], inp[:, :, :], stat[:, :].unsqueeze(2).to_broadcast([P, T, D]), ALU.subtract)
                V.drain()
                V.tensor_tensor(sq[:, :, :], xc[:, :, :], xc[:, :, :], ALU.mult)
                V.drain()
                V.tensor_reduce(stat[:, :], sq[:, :, :], AX.X, ALU.add)
                V.drain()
                V.tensor_scalar(stat[:, :], stat[:, :], 1.0 / D, 1e-5, ALU.mult, ALU.add).then_inc(s_var, 1)
                eng.wait_ge(s_std, k)
                V.reciprocal(rstd[:, :], std[:, :])
                V.drain()
                V.tensor_tensor(sq[:, :, :], xc[:, :, :], rstd[:, :].unsqueeze(2).to_broadcast([P, T, D]), ALU.mult)
                V.drain()
                if relu:
                    V.tensor_scalar(outp[:, :, :], sq[:, :, :], 0.0, None, ALU.max)
                else:
                    V.tensor_copy(outp[:, :, :], sq[:, :, :])
                V.drain()

            eng.wait_ge(s_x, 16 * T)
            normed(1, x, h, True)
            V.tensor_copy(tab[:, :, 0:D], h[:, :, :])
            V.memset(tab[:, :, D:D + 1], 1.0)
            V.memset(wofs[:, :], 0.0)
            V.drain().then_inc(s_h, 1)

            with eng.Fori(0, round_count(eng)) as r:
                V.tensor_tensor(blks[:, :, :], edge_cur[:, :, 0:1].to_broadcast([P, T, WC * BPC]),
                                iota8[:, :].unsqueeze(1).to_broadcast([P, T, WC * BPC]), ALU.add)
                V.tensor_tensor(vmask[:, 0], iota_e[:, :].unsqueeze(1).to_broadcast([P, T, WE]),
                                edge_cur[:, :, 1:2].to_broadcast([P, T, WE]), ALU.is_ge)
                V.tensor_tensor(vmask[:, 1], iota_e[:, :].unsqueeze(1).to_broadcast([P, T, WE]),
                                edge_cur[:, :, 2:3].to_broadcast([P, T, WE]), ALU.is_lt)
                V.drain()
                V.tensor_tensor(vmask[:, 0], vmask[:, 0], vmask[:, 1], ALU.mult)
                V.drain()
                wait_reg(eng, s_raw, (r + 1) * 16 * T)
                V.scalar_tensor_tensor(vmask[:, 1], raw_src, float(-N), vmask[:, 0], ALU.add, ALU.mult)
                V.drain()
                with eng.If(r > 0):
                    wait_reg(eng, s_recst, r * 16 * T)
                V.tensor_scalar(recs[:, :, :, 0:CH], vmask[:, 1].rearrange("p t (k s) -> p t k s", k=WC), float(N), None, ALU.add)
                V.tensor_scalar(recs[:, :, :, CH:CH + BPC], blks[:, :, :].rearrange("p t (k s) -> p t k s", k=WC),
                                float(NBLK - 1), None, ALU.min)
                V.tensor_tensor(edge_cur[:, :, :], edge_cur[:, :, :], step3[:, :].unsqueeze(1).to_broadcast([P, T, 3]), ALU.add)
                V.drain().then_inc(s_recm, 1)
                V.tensor_scalar(blk_ix[:, :], edge_cur[:, :, 0], float(NBLK - 1), None, ALU.min)
                V.drain().then_inc(s_bix, 1)

            V.sem_inc(s_free, 2)
            V.sem_inc(s_cntu, 1)
            V.sem_inc(s_cb, 1)
            V.sem_inc(s_cntst, 16)

            with eng.Fori(0, L0) as layer:
                wait_reg(eng, s_tabr, (layer + 1) * T)
                with eng.Fori(0, T) as t:
                    lo, hi = chunk_range(eng, t)
                    own = tab[:, bass.ds(t, 1), :].rearrange("p o c -> p (o c)")
                    er_t = er[:, bass.ds(t, 1), :].rearrange("p o c -> p (o c)")
                    V.drain()
                    V.tensor_tensor(mnew[:, :], own[:, D + 1:D + 1 + HEADS], er_t, ALU.add)
                    V.memset(acc[:, :, :], 0.0)
                    V.memset(rsave[:, :], 0.0)
                    V.drain().then_inc(s_own, 1)
                    V.scalar_tensor_tensor(zz[:, CH, :], mnew[:, :], 0.2, mnew[:, :], ALU.mult, ALU.max)
                    V.drain()
                    with eng.Fori(lo, hi) as c:
                        eng.wait_ge(s_rows, layer * chunks + c + 1)
                        R = rows[:, bass.ds(c % 2, 1), :, :].rearrange("p o s c -> p (o s) c")
                        V.tensor_tensor(zz[:, 0:CH, :], R[:, :, D + 1:D + 1 + HEADS],
                                        er_t.unsqueeze(1).to_broadcast([P, CH, HEADS]), ALU.add)
                        V.drain()
                        V.tensor_tensor(acc[:, :, :], acc[:, :, :],
                                        rsave[:, :].unsqueeze(2).to_broadcast([P, HEADS, D + 1]), ALU.mult)
                        V.tensor_scalar(ids8[:, :], R[:, :, ROW0 - 1], wofs[:, 0:1], None, ALU.add)
                        V.scalar_tensor_tensor(zz[:, 0:CH, :], zz[:, 0:CH, :], 0.2, zz[:, 0:CH, :], ALU.mult, ALU.max)
                        V.drain()
                        V.tensor_reduce(mnew[:, :], zz[:, :, :].rearrange("p s h -> p h s"), AX.X, ALU.max)
                        V.drain()
                        V.tensor_tensor(pz[:, :, :], zz[:, :, :], mnew[:, :].unsqueeze(1).to_broadcast([P, CH + 1, HEADS]),
                                        ALU.subtract).then_inc(s_z, 1)
                        eng.wait_ge(s_accp, c + (layer * chunks + layer * T + t + 1))
                        V.tensor_tensor(acc[:, :, :], acc[:, :, :], acc_ps, ALU.add)
                        eng.wait_ge(s_p, layer * chunks + c + 1)
                        V.tensor_copy(rsave[:, :], pe[:, CH, :])
                        V.tensor_copy(zz[:, CH, :], mnew[:, :])
                        V.tensor_tensor(prod[:, 0:CH - ASL],
                                        R[:, 0:CH - ASL, 0:D + 1].unsqueeze(2).to_broadcast([P, CH - ASL, HEADS, D + 1]),
                                        pe[:, 0:CH - ASL, :].unsqueeze(3).to_broadcast([P, CH - ASL, HEADS, D + 1]), ALU.mult)\
                         .then_inc(s_prod, 1)
                        eng.wait_ge(s_cntu, c + (layer * chunks + 1))
                        for k in range(CH):
                            if k == 2:
                                eng.wait_ge(s_proda, layer * chunks + c + 1)
                            last = V.tensor_scalar(onehot[:, k, :], iota_w, ids8[:, k:k + 1], None, ALU.is_equal)
                            if k == 2:
                                last.then_inc(s_free, 1)
                        last.then_inc(s_ones, 1)
                    V.drain()
                    V.tensor_tensor(acc[:, :, :], acc[:, :, :],
                                    rsave[:, :].unsqueeze(2).to_broadcast([P, HEADS, D + 1]), ALU.mult)
                    V.drain()
                    eng.wait_ge(s_accp, hi + (layer * chunks + layer * T + t + 1))
                    V.tensor_tensor(acc[:, :, :], acc[:, :, :], acc_ps, ALU.add)
                    V.drain()
                    V.reciprocal(rden[:, :], acc[:, :, D])
                    V.drain()
                    V.tensor_tensor(u[:, :, :], acc[:, :, 0:D], rden[:, :].unsqueeze(2).to_broadcast([P, HEADS, D]),
                                    ALU.mult).then_inc(s_u, 1)
                V.tensor_scalar(wofs[:, :], wofs[:, :], float(-WIN), None, ALU.add)
                V.drain()
            eng.wait_ge(s_tabr, (L0 + 1) * T)
            V.tensor_tensor(x[:, :, :], x[:, :, :], tab[:, :, 0:D], ALU.add)
            V.drain()
            V.tensor_tensor(x[:, :, :], x[:, :, :], hbb[:, :].unsqueeze(1).to_broadcast([P, T, D]), ALU.add)
            V.drain()

            normed(2, x, h, True)
            V.tensor_copy(cat[:, :, 0:D], h[:, :, :])
            V.tensor_copy(tab[:, :, 0:D], h[:, :, :])
            V.memset(tab[:, :, D:D + 1], 1.0)
            V.drain().then_inc(s_h, 1)
            eng.wait_ge(s_w1, 16 * 12)
            eng.wait_ge(s_srcc, 16)
            V.tensor_scalar(hilo_i[:, 0, :], srcs_i[:, :], 6, None, ALU.logical_shift_right)
            V.tensor_scalar(hilo_i[:, 1, :], srcs_i[:, :], 63, None, ALU.bitwise_and)
            eng.wait_ge(s_mms, NG)
            V.drain().then_inc(s_tab1, 1)
            V.sem_inc(s_hist, 1)
            V.tensor_copy(hilo[:, :, :], hilo_i[:, :, :])
            V.drain()

            with eng.Fori(0, T) as t:
                lo, hi = chunk_range(eng, t)
                V.memset(macc[:, :], 0.0)
                BT = BnT[:, bass.ds(t, 1), :].to_broadcast([128, CH // 2, P])
                with eng.Fori(lo, hi) as c:
                    wait_reg(eng, s_rows, chunks * L0 + c + 1)
                    V.tensor_copy(real[:, :], rows[:, bass.ds(c % 2, 1), :, D].rearrange("p o s -> p (o s)"))
                    V.drain()
                    eng.wait_ge(s_at, c + 1).then_inc(s_free, 1)
                    for q in range(2):
                        eng.wait_ge(s_hidp, c * 2 + q + 1)
                        V.tensor_tensor(hidB[:, q, :, :], hid_ps[q], BT, ALU.add).then_inc(s_pre, 1)
                    for q in range(2):
                        eng.wait_ge(s_msg, c * 2 + q + 1)
                        V.tensor_tensor(msgs[:, q, :, :], msg_ps[q], b2b[:, :].unsqueeze(1).to_broadcast([P, CH // 2, D]),
                                        ALU.add)
                        V.drain()
                        V.scalar_tensor_tensor(msgs[:, q, :, :], msgs[:, q, :, :], 0.0,
                                               real[:, q * (CH // 2):(q + 1) * (CH // 2)].unsqueeze(2).to_broadcast([P, CH // 2, D]), ALU.max, ALU.mult)
                    V.drain()
                    V.tensor_reduce(msum[:, :], msgs[:, :, :, :].rearrange("p q k d -> p d (q k)"), AX.X, ALU.add)
                    V.drain()
                    V.tensor_tensor(macc[:, :], macc[:, :], msum[:, :], ALU.add)
                    V.drain()
                    with eng.If(c < T):
                        part_of_list = eng.snap(c % T)
                        eng.wait_ge(s_hist, part_of_list + 1)
                        hl = hilo[:, :, bass.ds(part_of_list * OHC, OHC)]
                        for k in range(2):
                            V.tensor_tensor(oh[:, k, :, :], iota64[:, :].unsqueeze(1).to_broadcast([P, OHC, 64]),
                                            hl[:, k, :].unsqueeze(2).to_broadcast([P, OHC, 64]), ALU.is_equal)
                        V.drain().then_inc(s_oh, 1)
                V.tensor_copy(cat[:, bass.ds(t, 1), D:2 * D].rearrange("p o d -> p (o d)"), macc[:, :])
                V.drain()
            eng.wait_ge(s_hist, T + 2)
            V.tensor_copy(hist[:, :], hist_ps)
            V.drain().then_inc(s_histo, 1)
            V.sem_inc(s_tab1, 1)
            for g in range(NG):
                j = slice(g * GT, (g + 1) * GT)
                eng.wait_ge(s_mm2, g + 1)
                V.tensor_tensor(y[:, j, :], mm2_ps[:, :, 0:D], nb2b[:, :].unsqueeze(1).to_broadcast([P, GT, D]), ALU.add)\
                 .then_inc(s_mm2s, 1)
            V.drain()
            normed(3, y, y, False)
            V.tensor_tensor(y[:, :, :], y[:, :, :], lnSb[:, :].unsqueeze(1).to_broadcast([P, T, D]), ALU.mult)
            V.tensor_tensor(x[:, :, :], x[:, :, :], h[:, :, :], ALU.add)
            V.drain()
            V.tensor_tensor(y[:, :, :], y[:, :, :], lnOb[:, :].unsqueeze(1).to_broadcast([P, T, D]), ALU.add)
            V.drain()
            V.tensor_tensor(x[:, :, :], x[:, :, :], y[:, :, :], ALU.add)
            V.drain()

            eng.wait_ge(s_cntst, 16 * (L0 * T + 1))
            normed(4, x, h, True)
            V.tensor_copy(tab[:, :, 0:D], h[:, :, :])
            V.tensor_scalar(stat[:, :], deg[:, :], 1.0, None, ALU.max)
            V.drain().then_inc(s_h, 1)
            V.sem_inc(s_tab2, 1)
            V.reciprocal(invd[:, :], stat[:, :]).then_inc(s_invd, 1)
            V.tensor_copy(iw[:, 0:D], ident[0:D, 0:D])
            V.memset(hp3, 0.0)
            V.tensor_tensor(x[:, :, :], x[:, :, :], bpb[:, :].unsqueeze(1).to_broadcast([P, T, D]), ALU.add)
            V.drain()

            def sum_pass(k):
                with eng.Fori(0, T) as t:
                    lo, hi = chunk_range(eng, t)
                    V.memset(macc[:, :], 0.0)
                    with eng.Fori(lo, hi) as c:
                        eng.wait_ge(s_rows, chunks * k + c + 1)
                        R = rows[:, bass.ds(c % 2, 1), :, :].rearrange("p o s c -> p (o s) c")
                        V.tensor_reduce(msum[:, :], R[:, :, 0:D].rearrange("p s d -> p d s"), AX.X, ALU.add)\
                         .then_inc(s_free, 1)
                        V.drain()
                        V.tensor_tensor(macc[:, :], macc[:, :], msum[:, :], ALU.add)
                        V.drain()
                    V.tensor_copy(agg[:, bass.ds(t, 1), :].rearrange("p o d -> p (o d)"), macc[:, :])
                    V.drain()

            dense = is_dense(eng)
            V.sem_inc(s_ringf, RING)

            def sums(k, scaled):
                with eng.If(dense == 1):
                    V.tensor_copy(hp12[:, :, 0:D], tab[:, :, 0:D])
                    V.drain()
                    V.tensor_tensor(xc[:, :, :], tab[:, :, 0:D], hp12[:, :, 0:D], ALU.subtract)
                    V.drain()
                    V.tensor_copy(hp12[:, :, D:2 * D], xc[:, :, :])
                    V.drain()
                    V.tensor_tensor(hp3[:, :, D:2 * D], xc[:, :, :], hp12[:, :, D:2 * D], ALU.subtract)
                    V.drain().then_inc(s_parts, 1)
                    eng.wait_ge(s_aggp, k + 1)
                    if scaled:
                        V.tensor_tensor(aggT, allT_ps, invd_b, ALU.mult).then_inc(s_aggT, 1)
                    else:
                        V.tensor_copy(aggT, allT_ps).then_inc(s_aggT, 1)
                with eng.If(dense == 0):
                    V.memset(aggT[D:2 * D, :], 0.0)
                    sum_pass(k + (L0 + 1))
                    if scaled:
                        V.tensor_tensor(agg[:, :, :], agg[:, :, :], invd[:, :].unsqueeze(2).to_broadcast([P, T, D]),
                                        ALU.mult)
                    V.drain().then_inc(s_parts, 1)

            eng.wait_ge(s_invb, 16)
            with eng.Fori(0, L2) as layer:
                for k in range(2):
                    V.tensor_copy(wst[k * D:(k + 1) * D, 0, :], wT[:, bass.ds(layer, 1), :].rearrange("p o d -> p (o d)"))
                V.tensor_copy(wst[0:D, 1, :], wT[:, bass.ds(layer + 3, 1), :].rearrange("p o d -> p (o d)"))
                V.tensor_copy(iw[:, D:2 * D], wT[:, bass.ds(layer + 6, 1), :].rearrange("p o d -> p (o d)"))
                V.tensor_copy(bnst[:, 4:5], bnc[:, 0, bass.ds(layer, 1)])
                V.drain()
                sums(layer, True)
                eng.wait_ge(s_yc, layer + 1)
                V.tensor_reduce(bnst[:, 0:1], yT[:, :, :].rearrange("p t n -> p (t n)"), AX.X, ALU.add)
                V.drain()
                V.tensor_scalar(bnst[:, 0:1], bnst[:, 0:1], 1.0 / N, None, ALU.mult)
                V.drain()
                V.tensor_scalar(yT[:, :, :], yT[:, :, :], bnst[:, 0:1], None, ALU.subtract)
                V.drain()
                V.tensor_tensor_reduce(out=aggT[0:D, :], in0=yT[:, :, :].rearrange("p t n -> p (t n)"),
                                       in1=yT[:, :, :].rearrange("p t n -> p (t n)"), scale=1.0, scalar=0.0,
                                       op0=ALU.mult, op1=ALU.add, accum_out=bnst[:, 3:4])
                V.drain()
                V.tensor_scalar(bnst[:, 1:2], bnst[:, 3:4], 1.0 / N, 1e-5, ALU.mult, ALU.add).then_inc(s_bn, 1)
                eng.wait_ge(s_bns, layer + 1)
                V.reciprocal(bnst[:, 7:8], bnst[:, 2:3])
                V.drain()
                V.tensor_tensor(bnst[:, 5:6], bnst[:, 7:8], bnc[:, 1, bass.ds(layer, 1)], ALU.mult)
                V.tensor_copy(bnst[:, 6:7], bnc[:, 2, bass.ds(layer, 1)])
                V.drain().then_inc(s_scale, 1)
                eng.wait_ge(s_backc, layer + 1)
                V.tensor_tensor(x[:, :, :], x[:, :, :], tiles_ps[0:P, :, D:2 * D], ALU.add).then_inc(s_xd, 1)
                V.drain()
                with eng.If(layer < L2 - 1):
                    V.sem_inc(s_tab2, 1)

            normed(5, x, h, True)
            for k in range(2):
                V.tensor_copy(wst[k * D:(k + 1) * D, 0, :], ident[0:D, 0:D])
            V.drain().then_inc(s_h, 1)
            eng.wait_ge(s_y, L2 + 1)
            V.tensor_tensor(y[:, :, :], tiles64_ps, b3b[:, :].unsqueeze(1).to_broadcast([P, T, D]), ALU.add)\
             .then_inc(s_xd, 1)
            eng.wait_ge(s_deg, 16 * T)
            V.tensor_scalar(stat[:, :], odeg[:, :], 1.0, None, ALU.add).then_inc(s_var, 1)
            eng.wait_ge(s_std, 6)
            V.reciprocal(dinv[:, :], std[:, :])
            V.drain()
            V.tensor_tensor(tab[:, :, 0:D], y[:, :, :], dinv[:, :].unsqueeze(2).to_broadcast([P, T, D]), ALU.mult)
            V.tensor_scalar(stat[:, :], deg[:, :], 1.0, None, ALU.add)
            V.drain().then_inc(s_tab2, 1)
            V.reciprocal(rstd[:, :], stat[:, :])
            V.drain()
            V.tensor_tensor(rstd[:, :], rstd[:, :], dinv[:, :], ALU.mult)
            V.drain()
            sums(L2, False)
            eng.wait_ge(s_y, L2 + 2)
            V.tensor_tensor(y[:, :, :], tab[:, :, 0:D], tiles64_ps, ALU.add)
            V.drain()
            V.tensor_tensor(y[:, :, :], y[:, :, :], rstd[:, :].unsqueeze(2).to_broadcast([P, T, D]), ALU.mult)
            V.drain()
            V.tensor_tensor(x[:, :, :], x[:, :, :], y[:, :, :], ALU.add).then_inc(s_out, 1)


_INS = ['x', 'src', 'dst', 'edge_attr_64', 'L0_gnn_Ws', 'L0_gnn_attn_l', 'L0_gnn_attn_r', 'L0_gnn_gat_bias',
        'L0_gnn_h_bias', 'L1_gnn_msg_W1', 'L1_gnn_msg_b1', 'L1_gnn_msg_W2', 'L1_gnn_msg_b2', 'L1_gnn_node_W1',
        'L1_gnn_node_b1', 'L1_gnn_node_W2', 'L1_gnn_node_b2', 'L1_gnn_ln_scale', 'L1_gnn_ln_offset', 'L2_gnn_Wl',
        'L2_gnn_Wr', 'L2_gnn_b', 'L2_gnn_gamma', 'L2_gnn_beta', 'L2_gnn_Wp', 'L2_gnn_bp', 'L3_gnn_W', 'L3_gnn_b']


def kernel(**inputs):
    import concourse.bacc as _bacc
    from concourse.bass_utils import run_bass_kernel_spmd as _run

    nc = _bacc.Bacc("TRN2", target_bir_lowering=False, num_devices=1)
    arrays, args = {}, []
    for name in _INS:
        a = np.ascontiguousarray(inputs[name])
        arrays[f"in_{name}_dram"] = a
        args.append(nc.dram_tensor(f"in_{name}_dram", a.shape, mybir.dt.from_np(a.dtype), kind="ExternalInput").ap())
    args.append(nc.dram_tensor("out_0_dram", [N, D], f32, kind="ExternalOutput").ap())
    build(nc, *args)
    r = _run(nc, [arrays], core_ids=[0])
    return r.results[0]["out_0_dram"]
```
